# Optimizing a Trainium2 kernel written in Bass

```python
import numpy as np
import jax
import jax.numpy as jnp

def _softmax(x, axis=-1):
    return jax.nn.softmax(x, axis=axis)

def _gelu(x):
    return jax.nn.gelu(x, approximate=True)

def _silu(x):
    return jax.nn.silu(x)

def _sigmoid(x):
    return jax.nn.sigmoid(x)

def _layernorm(x, axis=-1, eps=1e-05):
    m = jnp.mean(x, axis=axis, keepdims=True)
    v = jnp.var(x, axis=axis, keepdims=True)
    return (x - m) / jnp.sqrt(v + eps)

def _scatter_add(tgt, idx, src, axis=0):
    return tgt.at[idx].add(src)

def _segment_sum(src, seg, n):
    return jax.ops.segment_sum(src, seg, n)
kernel_name = 'mk_decoder_postln_d1_seqx_r4_e4b050'

def setup_inputs(seed: int=0):
    np.random.seed(seed)
    _w = jnp.asarray

    def _rec_inputs():
        import jax
        import jax.numpy as jnp
        _rk = jax.random.key(seed)
        x = -0.0002928 + 1 * jax.random.normal(jax.random.fold_in(_rk, 1), (16, 128, 256), jnp.float32)
        _lenS = 128 - jax.random.randint(jax.random.fold_in(_rk, 7), (16,), 0, max(1, 128 // 4) + 1, jnp.int32)
        _lenS2 = 128 - jax.random.randint(jax.random.fold_in(_rk, 8), (16,), 0, max(1, 128 // 4) + 1, jnp.int32)
        _ctx_1024P = jax.random.normal(jax.random.fold_in(_rk, 11), (16, 16, 256), jnp.float32)
        _ctx_1024c = jax.random.dirichlet(jax.random.fold_in(_rk, 511), 0.3 * jnp.ones((16,), jnp.float32), (16, 128))
        _ctx_1024t = jnp.einsum('bsk,bkd->bsd', _ctx_1024c, _ctx_1024P)
        _ctx_1024t = _ctx_1024t * jax.lax.rsqrt(jnp.mean(jnp.square(_ctx_1024t)) + 1e-12) * 0.953939
        ctx_1024 = -1.39393e-06 + 0.999914 * (_ctx_1024t + 0.3 * jax.random.normal(jax.random.fold_in(_rk, 611), (16, 128, 256), jnp.float32))
        return (x, ctx_1024)
    x, ctx_1024 = _rec_inputs()

    def _L0_attn_setup():
        import jax, jax.numpy as jnp
        import numpy as np
        from functools import partial
        B, S, D = (8, 512, 256)
        HEADS, DIM_HEAD = (16, 64)
        MAX_ALLOWABLE = 256 * 256 * 8

        def _max_pow2_divides(n):
            i = 1
            while n % 2 == 0:
                i *= 2
                n //= 2
            return i

        def _n_splits(bh, sq, sk):
            dimprod = bh * sq * sk
            true_divisor = dimprod / MAX_ALLOWABLE
            if true_divisor < 1:
                return 1
            if true_divisor >= bh:
                return bh
            nearest_pow2 = 2 ** np.round(np.log2(true_divisor))
            return int(min(_max_pow2_divides(bh), nearest_pow2))

        def _sdp_attention(q, k, v, scale):
            scores = jnp.einsum('bid,bjd->bij', q, k) * scale
            probs = jax.nn.softmax(scores, axis=2)
            return jnp.einsum('bij,bjd->bid', probs, v)

        def _scan_attention(q, k, v, scale, n_splits):
            bh = q.shape[0]
            nq, nk, nv = [h.reshape(n_splits, bh // n_splits, h.shape[-2], h.shape[-1]) for h in (q, k, v)]

            def body(carry, args):
                cq, ck, cv = args
                return (None, _sdp_attention(cq, ck, cv, scale))
            outs = jax.lax.scan(body, None, (nq, nk, nv))[1]
            return outs.reshape(-1, outs.shape[-2], outs.shape[-1])

        def _heads_to_batch(t, heads):
            b, s, d = t.shape
            return t.reshape(b, s, heads, d // heads).transpose(0, 2, 1, 3).reshape(b * heads, s, d // heads)

        def _batch_to_heads(t, heads):
            bh, s, d = t.shape
            return t.reshape(bh // heads, heads, s, d).transpose(0, 2, 1, 3).reshape(bh // heads, s, d * heads)
        key = jax.random.key(seed)
        k1, k2, k3, k4 = jax.random.split(key, 4)
        inner = HEADS * DIM_HEAD
        return {'hidden_states': jax.random.normal(k1, (B, S, D), jnp.float32), 'Wq': jax.random.normal(k2, (D, inner), jnp.float32) * D ** (-0.5), 'Wkv': jax.random.normal(k3, (D, 2 * inner), jnp.float32) * D ** (-0.5), 'Wo': jax.random.normal(k4, (inner, D), jnp.float32) * inner ** (-0.5), 'bo': jnp.zeros((D,), jnp.float32)}
    _L0_attn_all = _L0_attn_setup()
    _L0_attn_in = {k: v for k, v in _L0_attn_all.items() if k in ('Wq', 'Wkv', 'Wo', 'bo')}
    del _L0_attn_all

    def _L0_xattn_setup():
        import jax, jax.numpy as jnp
        import numpy as np
        B, S, E, NH = (2, 512, 256, 4)
        HD = E // NH

        def _mlstm_head(q, k, v, ig, fg, eps=1e-06):
            s, dh = q.shape
            log_f = jax.nn.log_sigmoid(fg)
            cs = jnp.concatenate([jnp.zeros((1, 1), log_f.dtype), jnp.cumsum(log_f, axis=0)], axis=0)
            neg = jnp.asarray(-0.7 * jnp.finfo(cs.dtype).max, cs.dtype)
            log_d = jnp.where(jnp.tri(s, dtype=bool), (cs - cs.T)[1:, 1:] + ig.T, neg)
            m = jnp.max(log_d, axis=-1, keepdims=True)
            d = jnp.exp(log_d - m)
            c = q @ (k.T / jnp.sqrt(dh)) * d
            n = jnp.maximum(jnp.sum(c, axis=-1, keepdims=True), jnp.exp(-m))
            return c / (n + eps) @ v
        key = jax.random.key(seed)
        ks = jax.random.split(key, 8)
        return {'q': jax.random.normal(ks[0], (B, S, E), jnp.float32), 'k': jax.random.normal(ks[1], (B, S, E), jnp.float32), 'v': jax.random.normal(ks[2], (B, S, E), jnp.float32), 'igate_kernel': jax.random.normal(ks[3], (3 * E, NH), jnp.float32) * 0.02, 'igate_bias': jax.random.normal(ks[4], (NH,), jnp.float32) * 0.1, 'fgate_kernel': jax.random.normal(ks[5], (3 * E, NH), jnp.float32) * 0.02, 'fgate_bias': jnp.linspace(3.0, 6.0, NH, dtype=jnp.float32), 'rms_scale': jax.random.normal(ks[6], (HD,), jnp.float32) * 0.02}
    _L0_xattn_all = _L0_xattn_setup()
    _L0_xattn_in = {k: v for k, v in _L0_xattn_all.items() if k in ('igate_kernel', 'igate_bias', 'fgate_kernel', 'fgate_bias', 'rms_scale')}
    del _L0_xattn_all

    def _L0_ffn_setup():
        import jax, jax.numpy as jnp
        import numpy as np
        B, S, H, F, E, K = (4, 1024, 256, 1024, 8, 2)
        LN_EPS = 1e-05
        key = jax.random.key(seed)
        kx, kr, k1, k2 = jax.random.split(key, 4)
        x = jax.random.normal(kx, (B, S, H), dtype=jnp.float32)
        gamma = jnp.ones((H,), jnp.float32)
        beta = jnp.zeros((H,), jnp.float32)
        Wr = jax.random.normal(kr, (H, E), jnp.float32) * 0.02
        br = jnp.zeros((E,), jnp.float32)
        W1 = jax.random.normal(k1, (E, H, F), jnp.float32) * (1.0 / np.sqrt(H))
        b1 = jnp.zeros((E, F), jnp.float32)
        W2 = jax.random.normal(k2, (E, F, H), jnp.float32) * (1.0 / np.sqrt(F))
        b2 = jnp.zeros((E, H), jnp.float32)
        return {'x': x, 'gamma': gamma, 'beta': beta, 'Wr': Wr, 'br': br, 'W1': W1, 'b1': b1, 'W2': W2, 'b2': b2}
    _L0_ffn_all = _L0_ffn_setup()
    _L0_ffn_in = {k: v for k, v in _L0_ffn_all.items() if k in ('gamma', 'beta', 'Wr', 'br', 'W1', 'b1', 'W2', 'b2')}
    del _L0_ffn_all
    return {'x': x, 'ctx_1024': ctx_1024, 'L0_attn_Wq': _L0_attn_in['Wq'], 'L0_attn_Wkv': _L0_attn_in['Wkv'], 'L0_attn_Wo': _L0_attn_in['Wo'], 'L0_attn_bo': _L0_attn_in['bo'], 'L0_xattn_igate_kernel': _L0_xattn_in['igate_kernel'], 'L0_xattn_igate_bias': _L0_xattn_in['igate_bias'], 'L0_xattn_fgate_kernel': _L0_xattn_in['fgate_kernel'], 'L0_xattn_fgate_bias': _L0_xattn_in['fgate_bias'], 'L0_xattn_rms_scale': _L0_xattn_in['rms_scale'], 'L0_ffn_gamma': _L0_ffn_in['gamma'], 'L0_ffn_beta': _L0_ffn_in['beta'], 'L0_ffn_Wr': _L0_ffn_in['Wr'], 'L0_ffn_br': _L0_ffn_in['br'], 'L0_ffn_W1': _L0_ffn_in['W1'], 'L0_ffn_b1': _L0_ffn_in['b1'], 'L0_ffn_W2': _L0_ffn_in['W2'], 'L0_ffn_b2': _L0_ffn_in['b2']}

def reference(x, ctx_1024, L0_attn_Wq, L0_attn_Wkv, L0_attn_Wo, L0_attn_bo, L0_xattn_igate_kernel, L0_xattn_igate_bias, L0_xattn_fgate_kernel, L0_xattn_fgate_bias, L0_xattn_rms_scale, L0_ffn_gamma, L0_ffn_beta, L0_ffn_Wr, L0_ffn_br, L0_ffn_W1, L0_ffn_b1, L0_ffn_W2, L0_ffn_b2):
    import jax
    import jax.numpy as jnp

    def _L0_attn_ref(hidden_states, Wq, Wkv, Wo, bo):
        import jax, jax.numpy as jnp
        import numpy as np
        from functools import partial
        B, S, D = (8, 512, 256)
        HEADS, DIM_HEAD = (16, 64)
        MAX_ALLOWABLE = 256 * 256 * 8

        def _max_pow2_divides(n):
            i = 1
            while n % 2 == 0:
                i *= 2
                n //= 2
            return i

        def _n_splits(bh, sq, sk):
            dimprod = bh * sq * sk
            true_divisor = dimprod / MAX_ALLOWABLE
            if true_divisor < 1:
                return 1
            if true_divisor >= bh:
                return bh
            nearest_pow2 = 2 ** np.round(np.log2(true_divisor))
            return int(min(_max_pow2_divides(bh), nearest_pow2))

        def _sdp_attention(q, k, v, scale):
            scores = jnp.einsum('bid,bjd->bij', q, k) * scale
            probs = jax.nn.softmax(scores, axis=2)
            return jnp.einsum('bij,bjd->bid', probs, v)

        def _scan_attention(q, k, v, scale, n_splits):
            bh = q.shape[0]
            nq, nk, nv = [h.reshape(n_splits, bh // n_splits, h.shape[-2], h.shape[-1]) for h in (q, k, v)]

            def body(carry, args):
                cq, ck, cv = args
                return (None, _sdp_attention(cq, ck, cv, scale))
            outs = jax.lax.scan(body, None, (nq, nk, nv))[1]
            return outs.reshape(-1, outs.shape[-2], outs.shape[-1])

        def _heads_to_batch(t, heads):
            b, s, d = t.shape
            return t.reshape(b, s, heads, d // heads).transpose(0, 2, 1, 3).reshape(b * heads, s, d // heads)

        def _batch_to_heads(t, heads):
            bh, s, d = t.shape
            return t.reshape(bh // heads, heads, s, d).transpose(0, 2, 1, 3).reshape(bh // heads, s, d * heads)
        scale = DIM_HEAD ** (-0.5)
        q = hidden_states @ Wq
        kv = hidden_states @ Wkv
        k, v = jnp.split(kv, 2, axis=-1)
        q = _heads_to_batch(q, HEADS)
        k = _heads_to_batch(k, HEADS)
        v = _heads_to_batch(v, HEADS)
        n_splits = _n_splits(q.shape[0], q.shape[1], k.shape[1])
        out = _scan_attention(q, k, v, scale, n_splits)
        out = _batch_to_heads(out, HEADS)
        return out @ Wo + bo

    def _L0_xattn_ref(q, k, v, igate_kernel, igate_bias, fgate_kernel, fgate_bias, rms_scale):
        import jax, jax.numpy as jnp
        import numpy as np
        B, S, E, NH = (2, 512, 256, 4)
        HD = E // NH

        def _mlstm_head(q, k, v, ig, fg, eps=1e-06):
            s, dh = q.shape
            log_f = jax.nn.log_sigmoid(fg)
            cs = jnp.concatenate([jnp.zeros((1, 1), log_f.dtype), jnp.cumsum(log_f, axis=0)], axis=0)
            neg = jnp.asarray(-0.7 * jnp.finfo(cs.dtype).max, cs.dtype)
            log_d = jnp.where(jnp.tri(s, dtype=bool), (cs - cs.T)[1:, 1:] + ig.T, neg)
            m = jnp.max(log_d, axis=-1, keepdims=True)
            d = jnp.exp(log_d - m)
            c = q @ (k.T / jnp.sqrt(dh)) * d
            n = jnp.maximum(jnp.sum(c, axis=-1, keepdims=True), jnp.exp(-m))
            return c / (n + eps) @ v
        b, s, e = q.shape
        nh = igate_kernel.shape[1]
        hd = e // nh
        gate_in = jnp.concatenate((q, k, v), axis=-1)
        ig = (gate_in @ igate_kernel + igate_bias).swapaxes(-1, -2)[..., None]
        fg = (gate_in @ fgate_kernel + fgate_bias).swapaxes(-1, -2)[..., None]
        qh = q.reshape(b, s, nh, hd).swapaxes(1, 2)
        kh = k.reshape(b, s, nh, hd).swapaxes(1, 2)
        vh = v.reshape(b, s, nh, hd).swapaxes(1, 2)
        h = jax.vmap(jax.vmap(_mlstm_head))(qh, kh, vh, ig, fg)
        var = jnp.mean(jnp.square(h.astype(jnp.float32)), axis=-1, keepdims=True)
        h = (h * jax.lax.rsqrt(var + 1e-06)).astype(h.dtype) * (1.0 + rms_scale)
        return h.swapaxes(1, 2).reshape(b, s, e)

    def _L0_ffn_ref(x, gamma, beta, Wr, br, W1, b1, W2, b2):
        import jax, jax.numpy as jnp
        import numpy as np
        B, S, H, F, E, K = (4, 1024, 256, 1024, 8, 2)
        LN_EPS = 1e-05
        residual = x
        mu = jnp.mean(x, axis=-1, keepdims=True)
        var = jnp.var(x, axis=-1, keepdims=True)
        xn = (x - mu) * jax.lax.rsqrt(var + LN_EPS) * gamma + beta
        probs = jax.nn.softmax(xn @ Wr + br, axis=-1)
        scores, idx = jax.lax.top_k(probs, K)

        def expert_fn(w):
            W1_e, b1_e, W2_e, b2_e = w
            return jax.nn.relu(xn @ W1_e + b1_e) @ W2_e + b2_e
        full = jax.lax.map(expert_fn, (W1, b1, W2, b2))
        full = jnp.moveaxis(full, 0, 2)
        c = jnp.einsum('ef,efh->eh', jax.nn.relu(b1), W2) + b2
        c_total = c.sum(axis=0)
        sel_full = jnp.take_along_axis(full, idx[..., None], axis=2)
        c_sel = c[idx]
        output = jnp.sum(scores[..., None] * (sel_full - c_sel + c_total), axis=2)
        return residual + output
    x = _layernorm(x + _L0_attn_ref(x, L0_attn_Wq, L0_attn_Wkv, L0_attn_Wo, L0_attn_bo), axis=-1)
    x = _layernorm(x + _L0_xattn_ref(x, ctx_1024, ctx_1024, L0_xattn_igate_kernel, L0_xattn_igate_bias, L0_xattn_fgate_kernel, L0_xattn_fgate_bias, L0_xattn_rms_scale), axis=-1)
    x = _layernorm(x + _L0_ffn_ref(x, L0_ffn_gamma, L0_ffn_beta, L0_ffn_Wr, L0_ffn_br, L0_ffn_W1, L0_ffn_b1, L0_ffn_W2, L0_ffn_b2), axis=-1)
    return x

_drawn_inputs = setup_inputs


def setup_inputs(seed=0):
    import zlib

    import numpy as np

    out = dict(_drawn_inputs(seed))
    spreads = {'L0_attn_bo': (0.0, 0.1),
     'L0_ffn_gamma': (1.0, 0.2),
     'L0_ffn_beta': (0.0, 0.29),
     'L0_ffn_br': (0.0, 0.1),
     'L0_ffn_b1': (0.0, 0.1),
     'L0_ffn_b2': (0.0, 0.1)}
    factors = {'L0_xattn_igate_bias': 64.0, 'L0_xattn_rms_scale': 3.671}
    for name, (base, spread) in spreads.items():
        noise = np.random.default_rng([zlib.crc32(name.encode()), seed]).standard_normal(out[name].shape)
        drawn = base * np.exp(spread * noise) if base else spread * noise
        out[name] = jnp.asarray(drawn.astype(out[name].dtype))
    for name, factor in factors.items():
        out[name] = (out[name] * factor).astype(out[name].dtype)
    return out
```

```python
from contextlib import ExitStack

import concourse.bass as bass
from concourse import mybir

F32 = mybir.dt.float32
I32 = mybir.dt.int32
U32 = mybir.dt.uint32
ALU = mybir.AluOpType
ACT = mybir.ActivationFunctionType
AX = mybir.AxisListType

P = 128
LN_EPS = 1e-5
MLSTM_EPS = 1e-6
RMS_EPS = 1e-6


class Chain:

    def __init__(self, eng, sem):
        self.eng, self.sem, self.base, self.k = eng, sem, 0, 0

    def start(self, base):
        self.base, self.k = base, 0

    def link(self, ins):
        self.k += 1
        ins.then_inc(self.sem, 1)
        self.eng.wait_ge(self.sem, self.base + self.k)


def decoder_layer(nc, x, ctx, wq, wkv, wo, bo, ig_w, ig_b, fg_w, fg_b, rms, gamma, beta,
                  wr, br, w1, b1, w2, b2, out):
    B, S, D = x.shape
    INNER = wq.shape[1]
    HD = 64
    NH = INNER // HD
    KC = D // P
    PAIRS = B // 2
    HG = NH // 4
    STEPS = 2 * HG
    IC = INNER // P
    SCALE = float(HD) ** -0.5
    XH = ig_w.shape[1]
    E, _, F = w1.shape
    FC = F // P
    QUADS = B // 4
    N_TILES = (2 * B * S + E + E * (P - 1)) // P
    N_SLOTS = N_TILES * P
    MAX_E_TILES = B * S // P + 1
    assert S == P and D == 2 * P and NH == 16 and XH == 4 and XH * HD == D and N_TILES % 2 == 0

    es = ExitStack()
    with es:
        def sb(name, shape, dt=F32):
            return es.enter_context(nc.sbuf_tensor(name, shape, dt))

        def sem(name):
            return es.enter_context(nc.semaphore(name))

        ident = sb("ident", [P, P])
        xres = sb("xres", [P, B, D])
        neghalf = sb("neghalf", [P, 16])
        arena = sb("arena", [P, E * FC * D])
        arena2 = sb("arena2", [P, E * F])
        arena3 = sb("arena3", [P, B * XH * (HD + 1)])
        work = sb("work", [P, 3072])
        w1_sb = sb("w1_sb", [P, E, KC, F])

        off = [0]

        def carve(area, n):
            v = area[:, off[0]:off[0] + n]
            off[0] += n
            return v

        wq_sb = carve(arena, KC * INNER).rearrange("p (c n) -> p c n", c=KC)
        wkv_sb = carve(arena, KC * 2 * INNER).rearrange("p (c n) -> p c n", c=KC)
        wo_sb = carve(arena, IC * D).rearrange("p (c n) -> p c n", c=IC)
        qT = carve(arena, IC * 2 * S).rearrange("p (c t) -> p c t", c=IC)
        kT = carve(arena, IC * 2 * S).rearrange("p (c t) -> p c t", c=IC)
        v_sb = carve(arena, 2 * NH * (HD + 1)).rearrange("p (b h e) -> p b h e", b=2, h=NH)
        pT = carve(arena, 512)
        off[0] = 0
        xs = carve(arena2, 2 * D).rearrange("p (b d) -> p b d", b=2)
        xT = carve(arena2, KC * 2 * S).rearrange("p (c t) -> p c t", c=KC)
        o_sb = carve(arena2, 2 * INNER).rearrange("p (b n) -> p b n", b=2)
        oT = carve(arena2, 2 * IC * S).rearrange("p (b c t) -> p b c t", b=2, c=IC)
        probs = carve(arena2, 2 * 512).rearrange("p (u n) -> p u n", u=2)
        yln = carve(arena2, 2 * D).rearrange("p (b d) -> p b d", b=2)
        bo_rep = carve(arena2, D)

        ctx_aug = arena3[:, :].rearrange("p (b h e) -> p b h e", b=B, h=XH)
        st_all = arena2[:, :].rearrange("p (b h t) -> p b h t", b=B, h=XH)
        u_all = st_all.rearrange("p b h t -> p b (h t)")[:, :, 0:XH * (HD + 1)]
        off[0] = 0
        x1s = carve(work, 2 * D).rearrange("p (b d) -> p b d", b=2)
        cs_ = carve(work, 2 * D).rearrange("p (b d) -> p b d", b=2)
        x1T = carve(work, KC * 2 * S).rearrange("p (c t) -> p c t", c=KC)
        ctxT = carve(work, KC * 2 * S).rearrange("p (c t) -> p c t", c=KC)
        gates = carve(work, 2 * S)[0:2 * XH, :]
        off[0] = 2048
        BH = B * XH
        gi, gf, logf, tln, cum, gdiff, gmax, ones_bh = [carve(work, S)[0:BH, :] for _ in range(8)]
        off[0] = 0
        mrep = [carve(work, XH * S).rearrange("p (h t) -> p h t", h=XH) for _ in range(2)]
        decay = [carve(work, XH * S).rearrange("p (h t) -> p h t", h=XH) for _ in range(2)]
        ctmp = [carve(work, XH * S).rearrange("p (h t) -> p h t", h=XH) for _ in range(2)]
        off[0] = 0
        hq = carve(work, 4 * D)
        sq = carve(work, 4 * D)
        gamma_rep = carve(work, D)
        beta_rep = carve(work, D)
        xnT = hq.rearrange("p (c t) -> p c t", c=KC)
        xns = sq.rearrange("p (b d) -> p b d", b=4)
        xn_all = arena3[:, 0:B * D].rearrange("p (b d) -> p b d", b=B)

        off[0] = 0
        ROUT = B * E
        rt = [carve(work, ROUT).rearrange("p (b e) -> p b e", e=E) for _ in range(8)]
        wide = carve(work, E * N_TILES)
        em8, io128, iotile, tile_f = (carve(work, n) for n in (E, MAX_E_TILES, N_TILES, N_TILES))
        rsmall = carve(work, 4 * B).rearrange("p (k b) -> p k b", b=B)
        esmall = carve(work, 4 * E).rearrange("p (k e) -> p k e", e=E)
        slot_f = carve(work, 2 * B).rearrange("p (k b) -> p k b", b=B)
        off[0] = 2560
        tri = carve(work, P)
        ones = carve(work, P)

        w2_sb = arena[:, :].rearrange("p (e c n) -> p e c n", e=E, c=FC)
        b1_rep = arena2[:, :].rearrange("p (e f) -> p e f", e=E)
        off[0] = 0
        xg = [carve(work, D) for _ in range(2)]
        xgT = [carve(work, KC * P).rearrange("p (c t) -> p c t", c=KC) for _ in range(2)]
        ysb = [carve(work, D) for _ in range(2)]
        off[0] = 0
        hid = [carve(arena3, F) for _ in range(2)]
        hidT = [carve(arena3, F).rearrange("p (c t) -> p c t", c=FC) for _ in range(2)]
        off[0] = 0
        y_all = carve(arena, 2 * B * D).rearrange("p (k b d) -> p k b d", k=2, b=B)
        yz, b2_sb, dterm = [carve(arena, D)[0:E, :] for _ in range(3)]
        zout = carve(arena, 4 * D).rearrange("p (b d) -> p b d", b=4)

        gw = sb("gw", [P, 3 * KC, 2 * XH])
        gws = sb("gws", [P, KC, 2 * XH])
        gb = sb("gb", [2 * XH, 1])
        wr_sb = sb("wr_sb", [P, KC, E])
        br_rep = sb("br_rep", [P, E])
        rms_rep = sb("rms_rep", [P, HD])
        tok = sb("tok", [P, 2 * BH])
        g_tok, em_tok = tok[:, 0:BH], tok[:, BH:]
        den = sb("den", [P, 16])
        rden = sb("rden", [P, 16])
        ssq = sb("ssq", [P, 16])
        rsq = sb("rsq", [P, 16])
        stats4 = sb("stats4", [P, 4, 6])
        mv4 = sb("mv4", [P, 4, 2])
        ve4 = sb("ve4", [P, 4])
        rstd4 = sb("rstd4", [P, 4])
        lg_all = sb("lg_all", [P, B, E])
        score = sb("score", [P, 2, B])
        slot = sb("slot", [P, 2, B], U32)
        tile_e = sb("tile_e", [P, N_TILES], I32)
        zslot_f = sb("zslot_f", [E, 1])
        zslot = sb("zslot", [E, 1], U32)
        wgt = tok[:, :].rearrange("p (b e) -> p b e", e=E)
        off[0] = 0
        wgtT = carve(work, B * S)[0:E, :]

        gates_dram = nc.dram_tensor("gates_dram", [2 * XH, B * S], F32, kind="Internal").ap()
        gmax_dram = nc.dram_tensor("gmax_dram", [BH, S], F32, kind="Internal").ap()
        xg_dram = nc.dram_tensor("xg_dram", [N_SLOTS, D], F32, kind="Internal").ap()
        y_dram = nc.dram_tensor("y_dram", [N_SLOTS, D], F32, kind="Internal").ap()

        mx = sb("mx", [P, 2, 4])
        rsum = sb("rsum", [P, 2, 4])
        stats = sb("stats", [P, 2, 6])
        mv = sb("mv", [P, 2, 2])
        ve = sb("ve", [P, 2])
        rstd = sb("rstd", [P, 2])

        bank = [es.enter_context(nc.psum_tensor(f"bank{i}", [P, 512], F32)) for i in range(8)]
        ps_proj = bank[0:2]
        ps_score = bank[2:4]
        ps_pT = bank[4]
        ps_pv = bank[5:7]
        ps_wo = bank[7]

        ident_ready = sem("ident_ready")
        x0_loaded = sem("x0_loaded")
        x_loaded = sem("x_loaded")
        xs_loaded = sem("xs_loaded")
        wq_loaded = sem("wq_loaded")
        wk_loaded = sem("wk_loaded")
        wv_loaded = sem("wv_loaded")
        wo_loaded = sem("wo_loaded")
        bo_loaded = sem("bo_loaded")
        ones_ready = sem("ones_ready")
        proj_done = sem("proj_done")
        proj_copied = sem("proj_copied")
        scores_done = sem("scores_done")
        shifted = sem("shifted")
        exp_done = sem("exp_done")
        pT_done = sem("pT_done")
        pT_copied = sem("pT_copied")
        pv_done = sem("pv_done")
        o_normed = sem("o_normed")
        wo_done = sem("wo_done")
        wo_read = sem("wo_read")
        var_ready = sem("var_ready")
        rstd_ready = sem("rstd_ready")
        x1_ready = sem("x1_ready")
        dve_step = sem("dve_step")
        stats_seen = sem("stats_seen")
        stored = sem("stored")
        zeros_ready = sem("zeros_ready")
        zeros_stored = sem("zeros_stored")
        aug_ready = sem("aug_ready")
        ctx_loaded = sem("ctx_loaded")
        small_loaded = sem("small_loaded")
        gws_ready = sem("gws_ready")
        st1_loaded = sem("st1_loaded")
        xT_done = sem("xT_done")
        xT_copied = sem("xT_copied")
        ctxT_done = sem("ctxT_done")
        ctxT_copied = sem("ctxT_copied")
        gates_done = sem("gates_done")
        gates_ready = sem("gates_ready")
        gates_stored = sem("gates_stored")
        st_done = sem("st_done")
        st_copied = sem("st_copied")
        gates_loaded = sem("gates_loaded")
        absf_done = sem("absf_done")
        expf_done = sem("expf_done")
        lnf_done = sem("lnf_done")
        gmax_ready = sem("gmax_ready")
        gmax_stored = sem("gmax_stored")
        gtok_done = sem("gtok_done")
        m_ready = sem("m_ready")
        em_ready = sem("em_ready")
        decay_done = sem("decay_done")
        decay_used = sem("decay_used")
        masked = sem("masked")
        ct_done = sem("ct_done")
        u_done = sem("u_done")
        u_copied = sem("u_copied")
        tok_ready = sem("tok_ready")
        act_seen = sem("act_seen")
        dve_seen = sem("dve_seen")
        pool_seen = sem("pool_seen")
        gamma_loaded = sem("gamma_loaded")
        h_ready = sem("h_ready")
        sq_done = sem("sq_done")
        sumsq_ready = sem("sumsq_ready")
        rsq_ready = sem("rsq_ready")
        var4_ready = sem("var4_ready")
        rstd4_ready = sem("rstd4_ready")
        xn_ready = sem("xn_ready")
        xn_kept = sem("xn_kept")
        xnT_done = sem("xnT_done")
        xnT_copied = sem("xnT_copied")
        logits_done = sem("logits_done")
        logits_read = sem("logits_read")
        route_exp_in = sem("route_exp_in")
        route_exp_out = sem("route_exp_out")
        counts_in = sem("counts_in")
        counts_out = sem("counts_out")
        route_ready = sem("route_ready")
        scattered = sem("scattered")
        w1_loaded = sem("w1_loaded")
        w2_loaded = sem("w2_loaded")
        b1_loaded = sem("b1_loaded")
        xgT_done = sem("xgT_done")
        xgT_copied = sem("xgT_copied")
        hid_done = sem("hid_done")
        hid_biased = sem("hid_biased")
        hidT_done = sem("hidT_done")
        hidT_copied = sem("hidT_copied")
        y_done = sem("y_done")
        y_copied = sem("y_copied")
        z_gathered = sem("z_gathered")
        b2_loaded = sem("b2_loaded")
        c_ready = sem("c_ready")
        csum_done = sem("csum_done")
        dterm_ready = sem("dterm_ready")
        wgtT_done = sem("wgtT_done")
        wgtT_copied = sem("wgtT_copied")
        part_done = sem("part_done")
        part_read = sem("part_read")
        out_ready = sem("out_ready")
        consts_ready = sem("consts_ready")
        tri_ready = sem("tri_ready")
        mrep_loaded = [sem(f"mrep_loaded{k}") for k in range(2)]
        xg_loaded = [sem(f"xg_loaded{k}") for k in range(2)]
        y_stored = [sem(f"y_stored{k}") for k in range(2)]
        gathered = [sem(f"gathered{k}") for k in range(QUADS)]

        def fillers(s, more):
            own = {0: [("q", 2), ("k", 2)], 1: [("q", 3), ("k", 3)], 2: [("v", 0, 1)], 3: [("v", 1, 1)],
                   4: [("o", 0, 0)], 5: [("o", 1, 0)], 7: [("o", 0, 1)]}.get(s, [])
            nxt = {3: [("x", 0), ("x", 1)], 4: [("q", 0)], 5: [("k", 0)], 6: [("q", 1)],
                   7: [("k", 1), ("v", 0, 0)]}.get(s, [])
            return own + (nxt if more else [])

        def tail_units(more):
            return ([("v", 1, 0)] if more else []) + [("o", 1, 1)]

        def step(s):
            return s // 4, s // 2 % 2, s % 2

        FIRST = [("x", 0), ("x", 1)] + [(w, g) for g in range(2) for w in "qk"] + [("v", b, 0) for b in range(2)]
        def uses_upto(more):
            return 6

        N_FIRST = len(FIRST)
        SCHEDULE = [u for s in range(STEPS) for u in fillers(s, True)] + tail_units(True)
        N_USES = len(SCHEDULE)
        assert N_USES % 2 == 0 and N_FIRST % 2 == 0

        block = es.enter_context(nc.Block())

        @block.sync
        def _(sp):
            sp.dma_start(xs[:, :, :], x[0:2].rearrange("b s d -> s b d")).then_inc(xs_loaded, 16)
            sp.dma_start(wq_sb, wq.rearrange("(c p) n -> p c n", p=P)).then_inc(wq_loaded, 16)
            wkv_v = wkv.rearrange("(c p) n -> p c n", p=P)
            sp.dma_start(wkv_sb[:, :, 0:INNER], wkv_v[:, :, 0:INNER]).then_inc(wk_loaded, 16)
            sp.dma_start(wkv_sb[:, :, INNER:], wkv_v[:, :, INNER:]).then_inc(wv_loaded, 16)
            sp.dma_start(wo_sb, wo.rearrange("(c p) n -> p c n", p=P)).then_inc(wo_loaded, 16)
            sp.dma_start(bo_rep[:, :], bo[None, :].broadcast_to([P, D])).then_inc(bo_loaded, 16)
            sp.dma_start(xres[:, :, :], x.rearrange("b s d -> s b d")).then_inc(x_loaded, 16)
            for w, b, r in ((ig_w, ig_b, 0), (fg_w, fg_b, XH)):
                sp.dma_start(gw[:, :, r:r + XH], w.rearrange("(c p) n -> p c n", p=P)).then_inc(small_loaded, 16)
                sp.dma_start(gb[r:r + XH, :], b[:, None]).then_inc(small_loaded, 16)
            sp.dma_start(wr_sb[:, :, :], wr.rearrange("(c p) n -> p c n", p=P)).then_inc(small_loaded, 16)
            sp.dma_start(br_rep[:, :], br[None, :].broadcast_to([P, E])).then_inc(small_loaded, 16)
            sp.dma_start(rms_rep[:, :], rms[None, :].broadcast_to([P, HD])).then_inc(small_loaded, 16)
            sp.wait_ge(zeros_ready, 1)
            ROW = N_SLOTS * D // P
            for c in range(4):
                sp.dma_start(xg_dram.rearrange("(p r) d -> p (r d)", p=P)[:, c * ROW // 4:(c + 1) * ROW // 4],
                             arena3[:, 0:ROW // 4]).then_inc(zeros_stored, 16)
            sp.wait_ge(zeros_stored, 64)
            for b in range(B):
                sp.dma_start(ctx_aug[:, b, :, 0:HD], ctx[b].rearrange("s (h e) -> s h e", h=XH)).then_inc(ctx_loaded, 16)
            sp.dma_start(w1_sb[:, :, :, :], w1.rearrange("e (c p) f -> p e c f", p=P)).then_inc(w1_loaded, 16)
            sp.wait_ge(proj_done, 2)
            sp.dma_start(xs[:, :, :], x[2:4].rearrange("b s d -> s b d")).then_inc(xs_loaded, 16)
            X_POS = SCHEDULE.index(("x", 1)) + 1
            with sp.Fori(0, PAIRS - 2) as i:
                sp.wait_ge(proj_done, N_FIRST + i * N_USES + X_POS)
                sp.dma_start(xs[:, :, :], x[bass.ds(2 * i + 4, 2)].rearrange("b s d -> s b d"))\
                    .then_inc(xs_loaded, 16)

            sp.wait_ge(x1_ready, PAIRS)
            sp.dma_start(x1s, xres[:, 0:2, :]).then_inc(st1_loaded, 16)
            sp.dma_start(cs_, ctx[0:2].rearrange("b s d -> s b d")).then_inc(st1_loaded, 16)
            sp.sem_inc(gates_stored, 16)
            with sp.Fori(0, PAIRS - 1) as i:
                sp.wait_ge(ctxT_done, i + 1)
                sp.dma_start(x1s, xres[:, bass.ds(2 * i + 2, 2), :]).then_inc(st1_loaded, 16)
                sp.dma_start(cs_, ctx[bass.ds(2 * i + 2, 2)].rearrange("b s d -> s b d")).then_inc(st1_loaded, 16)
                sp.wait_ge(gates_ready, i + 1)
                sp.dma_start(gates_dram[:, bass.ds(2 * S * i, 2 * S)], gates).then_inc(gates_stored, 16)
            sp.wait_ge(gates_ready, PAIRS)
            sp.dma_start(gates_dram[:, 2 * S * (PAIRS - 1):], gates).then_inc(gates_stored, 16)
            sp.wait_ge(gates_stored, 16 * (PAIRS + 1))
            sp.dma_start(gi, gates_dram[0:XH].rearrange("h (b t) -> (h b) t", b=B)).then_inc(gates_loaded, 16)
            sp.dma_start(gf, gates_dram[XH:].rearrange("h (b t) -> (h b) t", b=B)).then_inc(gates_loaded, 16)
            sp.wait_ge(gmax_ready, 1)
            sp.dma_start(gmax_dram, gmax).then_inc(gmax_stored, 16)
            sp.wait_ge(gmax_stored, 16)
            gm_v = gmax_dram.rearrange("(h b) t -> b h t", b=B)

            def load_mrep(b, par):
                sp.dma_start(mrep[par], gm_v[b][None, :, :].broadcast_to([P, XH, S]) if isinstance(b, int) else
                             gm_v[bass.ds(b, 1)].broadcast_to([P, XH, S])).then_inc(mrep_loaded[par], 16)

            sp.wait_ge(tok_ready, 1)
            for par in range(2):
                load_mrep(par, par)
            with sp.Fori(0, PAIRS - 1) as i:
                for par in range(2):
                    sp.wait_ge(decay_done, 2 * i + par + 1)
                    load_mrep(2 * i + par + 2, par)
            sp.wait_ge(u_copied, B)
            sp.dma_start(gamma_rep, gamma[None, :].broadcast_to([P, D])).then_inc(gamma_loaded, 16)
            sp.dma_start(beta_rep, beta[None, :].broadcast_to([P, D])).then_inc(gamma_loaded, 16)

            sp.wait_ge(xn_ready, QUADS)
            sp.dma_start(b1_rep, b1[None, :, :].broadcast_to([P, E, F])).then_inc(b1_loaded, 16)
            sp.wait_ge(scattered, 16 * 2 * B)
            for par in range(2):
                sp.dma_start(xg[par], xg_dram[par * P:(par + 1) * P, :]).then_inc(xg_loaded[par], 16)

            def slots(j, par, more):
                if more:
                    sp.wait_ge(xgT_done, j + 1)
                    sp.dma_start(xg[par], xg_dram[bass.ds((j + 2) * P, P), :]).then_inc(xg_loaded[par], 16)
                sp.wait_ge(y_copied, j + 1)
                sp.dma_start(y_dram[bass.ds(j * P, P), :], ysb[par]).then_inc(y_stored[par], 16)

            with sp.Fori(0, N_TILES // 2 - 1) as t:
                for par in range(2):
                    slots(2 * t + par, par, True)
            for par in range(2):
                slots(N_TILES - 2 + par, par, False)

            for q in range(QUADS):
                sp.wait_ge(out_ready, q + 1)
                sp.dma_start(out[4 * q:4 * q + 4].rearrange("b s d -> s b d"), xres[:, 4 * q:4 * q + 4, :])\
                    .then_inc(stored, 16)
            sp.wait_ge(stored, 16 * QUADS)

        @block.gpsimd
        def _(pool):
            pool.memset(ident[:, :], 0.0).then_inc(ident_ready, 1)
            pool.memset(neghalf[:, :], -0.5).then_inc(ident_ready, 1)
            pool.wait_ge(ident_ready, 2)
            pool.affine_select(out=ident[:, :], in_=ident[:, :], compare_op=ALU.not_equal, fill=1.0,
                               base=0, pattern=[[-1, P]], channel_multiplier=1).then_inc(ident_ready, 1)
            pool.memset(v_sb[:, :, :, HD:HD + 1], 1.0).then_inc(ones_ready, 1)
            pool.memset(arena3[:, 0:N_SLOTS * D // P // 4], 0.0).then_inc(zeros_ready, 1)
            with pool.Fori(0, PAIRS) as i:
                pool.wait_ge(var_ready, i + 1)
                pool.tensor_tensor(rstd[:, :], ve[:, :], neghalf[:, 0:2], ALU.pow).then_inc(rstd_ready, 1)

            pool.wait_ge(zeros_stored, 64)
            pool.memset(ctx_aug[:, :, :, HD:HD + 1], 1.0).then_inc(aug_ready, 1)
            pool.memset(ones_bh, 1.0).then_inc(aug_ready, 1)
            with pool.Fori(0, PAIRS) as i:
                for par in range(2):
                    pool.wait_ge(decay_done, 2 * i + par + 1)
                    pool.sem_inc(pool_seen, 1)
                    pool.affine_select(out=decay[par], in_=decay[par], compare_op=ALU.is_ge, fill=0.0, base=0,
                                       pattern=[[0, XH], [1, S]], channel_multiplier=-1).then_inc(masked, 1)

            with pool.Fori(0, QUADS) as i:
                pool.wait_ge(sumsq_ready, i + 1)
                pool.tensor_tensor(rsq[:, :], ssq[:, :], neghalf[:, :], ALU.pow).then_inc(rsq_ready, 1)
                for k in range(2):
                    pool.wait_ge(var4_ready, 2 * i + k + 1)
                    pool.tensor_tensor(rstd4[:, :], ve4[:, :], neghalf[:, 0:4], ALU.pow).then_inc(rstd4_ready, 1)

            pool.wait_ge(logits_read, QUADS)
            pool.iota(em8[:, :], [[1, E]], base=-E, channel_multiplier=0,
                      allow_small_or_imprecise_dtypes=True).then_inc(consts_ready, 1)
            pool.iota(io128[:, :], [[P, MAX_E_TILES]], base=0, channel_multiplier=0,
                      allow_small_or_imprecise_dtypes=True).then_inc(consts_ready, 1)
            pool.iota(iotile[:, :], [[1, N_TILES]], base=0, channel_multiplier=0,
                      allow_small_or_imprecise_dtypes=True).then_inc(consts_ready, 1)
            pool.memset(tri, 1.0).then_inc(tri_ready, 1)
            pool.memset(ones, 1.0).then_inc(tri_ready, 1)
            pool.wait_ge(tri_ready, 2)
            pool.affine_select(out=tri, in_=tri, compare_op=ALU.is_gt, fill=0.0, base=0, pattern=[[1, P]],
                               channel_multiplier=-1).then_inc(tri_ready, 1)

            pool.wait_ge(route_ready, 1)
            pool.wait_ge(xn_kept, QUADS)
            for b in range(B):
                for k in range(2):
                    pool.indirect_dma_start(xg_dram, bass.IndirectOffsetOnAxis(ap=slot[:, k, b:b + 1], axis=0),
                                            xn_all[:, b, :], None).then_inc(scattered, 16)

            for par in range(2):
                pool.wait_ge(y_stored[par], 16 * (N_TILES // 2 + 1))
            pool.indirect_dma_start(yz, None, y_dram, bass.IndirectOffsetOnAxis(ap=zslot[:, 0:1], axis=0))\
                .then_inc(z_gathered, 16)
            for b in range(B):
                for k in range(2):
                    pool.indirect_dma_start(y_all[:, k, b, :], None, y_dram,
                                            bass.IndirectOffsetOnAxis(ap=slot[:, k, b:b + 1], axis=0))\
                        .then_inc(gathered[b // 4], 16)
            for q in range(QUADS):
                pool.wait_ge(var4_ready, 2 * QUADS + q + 1)
                pool.tensor_tensor(rstd4[:, :], ve4[:, :], neghalf[:, 0:4], ALU.pow).then_inc(rstd4_ready, 1)

        @block.tensor
        def _(pe):
            uses = Chain(pe, None)

            def unit(kind, *a):
                n = uses.k
                if kind == "o":
                    b, half = a
                    pe.wait_ge(o_normed, pe_at[0] * STEPS + 4 * half + 2 * b + 2)
                pe.wait_ge(proj_copied, uses.base + n - 1) if not (isinstance(uses.base, int) and uses.base + n < 2) else None
                dst = ps_proj[n % 2]
                uses.k += 1
                if kind == "x":
                    for c in range(KC):
                        last = pe.transpose(dst[:, c * P:(c + 1) * P], xs[:, a[0], c * P:(c + 1) * P], ident[:, :])
                elif kind in "qk":
                    g, = a
                    w = wq_sb if kind == "q" else wkv_sb
                    for j in range(2):
                        ch = 2 * g + j
                        for c in range(KC):
                            last = pe.matmul(dst[:, j * 2 * S:(j + 1) * 2 * S], w[:, c, ch * P:(ch + 1) * P],
                                             xT[:, c, :], start=c == 0, stop=c == KC - 1)
                elif kind == "v":
                    b, half = a
                    for c in range(KC):
                        last = pe.matmul(dst[:, :], xT[:, c, b * S:(b + 1) * S],
                                         wkv_sb[:, c, INNER + half * 512:INNER + (half + 1) * 512],
                                         start=c == 0, stop=c == KC - 1)
                else:
                    b, half = a
                    for c in range(4):
                        last = pe.transpose(dst[:, c * P:(c + 1) * P],
                                            o_sb[:, b, (4 * half + c) * P:(4 * half + c + 1) * P], ident[:, :])
                last.then_inc(proj_done, 1)

            pe_at = [0]

            def scores(s):
                half, b, odd = step(s)
                r = HD * odd
                for h in range(4):
                    ch = 4 * half + h
                    last = pe.matmul(ps_score[s % 2][:, h * S:(h + 1) * S],
                                     qT[r:r + HD, ch, b * S:(b + 1) * S],
                                     kT[r:r + HD, ch, b * S:(b + 1) * S], start=True, stop=True)
                last.then_inc(scores_done, 1)

            def pair(i, more):
                pe_at[0] = i
                base = N_FIRST + i * N_USES
                uses.start(base)
                for s in range(STEPS):
                    half, b, odd = step(s)
                    for u in fillers(s, more):
                        if u == ("x", 0):
                            pe.wait_ge(xs_loaded, (i + 2) * 16)
                        if u == ("q", 0):
                            pe.wait_ge(proj_copied, base + uses.k)
                        unit(*u)
                    pe.wait_ge(exp_done, i * STEPS + s + 1)
                    for h in range(4):
                        last = pe.transpose(ps_pT[:, h * S:(h + 1) * S], probs[:, s % 2, h * S:(h + 1) * S], ident[:, :])
                    last.then_inc(pT_done, 1)
                    if s + 1 == 4:
                        pe.wait_ge(proj_copied, base + uses_upto(more))
                    if s + 1 < STEPS:
                        scores(s + 1)
                    pe.wait_ge(pT_copied, i * STEPS + s + 1)
                    for h in range(4):
                        last = pe.matmul(ps_pv[s % 2][:, h * (HD + 1):(h + 1) * (HD + 1)], pT[:, h * S:(h + 1) * S],
                                         v_sb[:, b, 8 * half + 2 * h + odd, :], start=True, stop=True)
                    last.then_inc(pv_done, 1)
                tails = tail_units(more)
                for u in tails[:-1]:
                    unit(*u)
                if more:
                    scores(0)
                unit(*tails[-1])
                for b in range(2):
                    pe.wait_ge(proj_copied, base + uses.k - 1 + b)
                    pe.wait_ge(wo_read, 2 * i + b + 1)
                    for c in range(IC):
                        last = pe.matmul(ps_wo[:, 0:D], oT[:, b, c, :], wo_sb[:, c, :], start=c == 0, stop=c == IC - 1)
                    last.then_inc(wo_done, 1)

            pe.wait_ge(ident_ready, 3)
            pe.wait_ge(xs_loaded, 16)
            uses.start(0)
            for u in FIRST:
                if u == ("q", 0):
                    pe.wait_ge(wq_loaded, 16)
                    pe.wait_ge(proj_copied, 2)
                if u == ("k", 0):
                    pe.wait_ge(wk_loaded, 16)
                if u == ("v", 0, 0):
                    pe.wait_ge(wv_loaded, 16)
                unit(*u)
            pe.wait_ge(proj_copied, N_FIRST)
            pe.wait_ge(ones_ready, 1)
            scores(0)
            pe.wait_ge(wo_loaded, 16)
            with pe.Fori(0, PAIRS - 1) as i:
                pair(i, True)
            pair(PAIRS - 1, False)

            pe.wait_ge(gws_ready, 1)
            with pe.Fori(0, PAIRS) as i:
                pe.wait_ge(st1_loaded, 32 * i + 32)
                for src, bk, done in ((x1s, bank[0], xT_done), (cs_, bank[1], ctxT_done)):
                    for c in range(KC):
                        for b in range(2):
                            last = pe.transpose(bk[:, (2 * c + b) * P:(2 * c + b + 1) * P],
                                                src[:, b, c * P:(c + 1) * P], ident[:, :])
                    last.then_inc(done, 1)
                pe.wait_ge(st_copied, 2 * i + 2)
                pe.wait_ge(xT_copied, i + 1)
                pe.wait_ge(ctxT_copied, i + 1)
                for c in range(KC):
                    pe.matmul(bank[2][0:2 * XH, 0:2 * S], gw[:, c, :], x1T[:, c, :], start=c == 0, stop=False)
                for c in range(KC):
                    last = pe.matmul(bank[2][0:2 * XH, 0:2 * S], gws[:, c, :], ctxT[:, c, :],
                                     start=False, stop=c == KC - 1)
                last.then_inc(gates_done, 1)
                for b in range(2):
                    for h in range(XH):
                        odd, c = h % 2, h // 2
                        r = HD * odd
                        last = pe.matmul(bank[3 + odd][:, (2 * b + c) * S:(2 * b + c + 1) * S],
                                         ctxT[r:r + HD, c, b * S:(b + 1) * S], x1T[r:r + HD, c, b * S:(b + 1) * S],
                                         start=True, stop=True)
                last.then_inc(st_done, 1)
            pe.wait_ge(em_ready, 1)
            pe.transpose(bank[5][:, 0:BH], gdiff, ident[0:BH, 0:BH])
            pe.transpose(bank[6][:, 0:BH], tln, ident[0:BH, 0:BH]).then_inc(gtok_done, 1)
            pe.wait_ge(ctx_loaded, 16 * B)
            pe.wait_ge(aug_ready, 2)
            with pe.Fori(0, PAIRS) as i:
                for par in range(2):
                    pe.wait_ge(ct_done, 2 * i + par + 1)
                    for h in range(XH):
                        last = pe.matmul(bank[par][:, h * (HD + 1):(h + 1) * (HD + 1)], ctmp[par][:, h, :],
                                         ctx_aug[:, 2 * i + par, h, :], start=True, stop=True)
                    last.then_inc(u_done, 1)

            with pe.Fori(0, QUADS) as i:
                pe.wait_ge(xn_ready, i + 1)
                for c in range(KC):
                    for b in range(4):
                        last = pe.transpose(bank[2 + c][:, b * S:(b + 1) * S], xns[:, b, c * P:(c + 1) * P], ident[:, :])
                last.then_inc(xnT_done, 1)
                pe.wait_ge(xnT_copied, i + 1)
                for b in range(4):
                    for c in range(KC):
                        last = pe.matmul(bank[4][:, b * E:(b + 1) * E], xnT[:, c, b * S:(b + 1) * S], wr_sb[:, c, :],
                                         start=c == 0, stop=c == KC - 1)
                last.then_inc(logits_done, 1)

            pe.wait_ge(counts_in, 1)
            pe.wait_ge(tri_ready, 3)
            chosen = rt[7].rearrange("p b e -> p (b e)")
            pe.matmul(bank[0][:, 0:ROUT], tri, chosen, start=True, stop=True)
            pe.matmul(bank[1][:, 0:ROUT], ones, chosen, start=True, stop=True).then_inc(counts_out, 1)

            def slot_transposes(j, par):
                pe.wait_ge(xg_loaded[par], 16 * (j // 2) + 16 if isinstance(j, int) else 8 * (j - par) + 16)
                for c in range(KC):
                    last = pe.transpose(bank[0][:, c * P:(c + 1) * P], xg[par][:, c * P:(c + 1) * P], ident[:, :])
                last.then_inc(xgT_done, 1)

            def hidden(j, par, half, e):
                if half == 0:
                    pe.wait_ge(xgT_copied, j + 1)
                if not isinstance(j, int) or j > 0:
                    pe.wait_ge(hid_biased, 2 * j + half - 1)
                for c in range(KC):
                    last = pe.matmul(bank[1 + half][:, :], xgT[par][:, c, :],
                                     w1_sb[:, e, c, half * 512:(half + 1) * 512], start=c == 0, stop=c == KC - 1)
                last.then_inc(hid_done, 1)

            def hidden_transposes(j, par):
                for half in range(2):
                    pe.wait_ge(hid_biased, 2 * j + half + 1)
                    for c in range(4):
                        f = (4 * half + c) * P
                        last = pe.transpose(bank[3 + half][:, c * P:(c + 1) * P], hid[par][:, f:f + P], ident[:, :])
                    last.then_inc(hidT_done, 1)

            def expert_out(j, par, e):
                for half in range(2):
                    pe.wait_ge(hidT_copied, 2 * j + half + 1)
                    for c in range(4 * half, 4 * half + 4):
                        last = pe.matmul(bank[5 + par][:, 0:D], hidT[par][:, c, :], w2_sb[:, e, c, :],
                                         start=c == 0, stop=c == FC - 1)
                last.then_inc(y_done, 1)

            def expert_of(j):
                return pe.value_load(tile_e[0:1, bass.ds(j, 1)], min_val=0, max_val=E - 1)

            def tile(j, par, more, e, e_next):
                if more:
                    slot_transposes(j + 1, 1 - par)
                    hidden(j + 1, 1 - par, 0, e_next)
                hidden_transposes(j, par)
                if more:
                    hidden(j + 1, 1 - par, 1, e_next)
                expert_out(j, par, e)

            pe.wait_ge(route_ready, 1)
            pe.wait_ge(w1_loaded, 16)
            slot_transposes(0, 0)
            for half in range(2):
                hidden(0, 0, half, expert_of(0))
            pe.wait_ge(w2_loaded, 16)
            with pe.Fori(0, N_TILES // 2 - 1) as t:
                e0, e1, e2 = (expert_of(2 * t + k) for k in range(3))
                tile(2 * t, 0, True, e0, e1)
                tile(2 * t + 1, 1, True, e1, e2)
            e0, e1 = expert_of(N_TILES - 2), expert_of(N_TILES - 1)
            tile(N_TILES - 2, 0, True, e0, e1)
            tile(N_TILES - 1, 1, False, e1, None)

            for g in range(QUADS):
                for b in range(4):
                    last = pe.transpose(bank[g % 2][0:E, b * S:(b + 1) * S], wgt[:, 4 * g + b, :], ident[:, :])
                last.then_inc(wgtT_done, 1)
                pe.wait_ge(wgtT_copied, g + 1)
            pe.wait_ge(c_ready, 1)
            pe.matmul(bank[2][0:E, 0:D], ones[0:E, 0:E], dterm, start=True, stop=True).then_inc(csum_done, 1)
            pe.wait_ge(dterm_ready, 1)
            for b in range(B):
                if b >= 4:
                    pe.wait_ge(part_read, b - 3)
                pe.matmul(bank[3 + b % 4][:, 0:D], wgtT[:, b * S:(b + 1) * S], yz, start=True, stop=True)\
                    .then_inc(part_done, 1)

        @block.scalar
        def _(act):
            def copy_unit(n, kind, *a):
                act.wait_ge(proj_done, n + 1)
                src = ps_proj[copy_at[0] % 2]
                copy_at[0] += 1
                if kind == "x":
                    o, i_ = xT[:, :, a[0] * S:(a[0] + 1) * S], src[:, 0:KC * P].rearrange("p (c t) -> p c t", c=KC)
                elif kind in "qk":
                    o = (qT if kind == "q" else kT)[:, 2 * a[0]:2 * a[0] + 2, :]
                    i_ = src[:, :].rearrange("p (c t) -> p c t", c=2)
                elif kind == "v":
                    o = v_sb[:, a[0], 8 * a[1]:8 * a[1] + 8, 0:HD]
                    i_ = src[:, :].rearrange("p (h e) -> p h e", h=8)
                else:
                    o = oT[:, a[0], 4 * a[1]:4 * a[1] + 4, :]
                    i_ = src[:, :].rearrange("p (c t) -> p c t", c=4)
                nc.scalar.copy(o, i_).then_inc(proj_copied, 1)

            copy_at = [0]
            for n, u in enumerate(FIRST):
                copy_unit(n, *u)

            def pair(i, more):
                n = N_FIRST + i * N_USES
                k = 0
                copy_at[0] = 0
                for s in range(STEPS):
                    act.wait_ge(shifted, i * STEPS + s + 1)
                    nc.scalar.activation(probs[:, s % 2, :], probs[:, s % 2, :], ACT.Exp, scale=SCALE)\
                        .then_inc(exp_done, 1)
                    for u in fillers(s, more):
                        copy_unit(n + k, *u)
                        k += 1
                    act.wait_ge(pT_done, i * STEPS + s + 1)
                    nc.scalar.copy(pT, ps_pT[:, :]).then_inc(pT_copied, 1)
                for u in tail_units(more):
                    copy_unit(n + k, *u)
                    k += 1

            with act.Fori(0, PAIRS - 1) as i:
                pair(i, True)
            pair(PAIRS - 1, False)

            act.wait_ge(x1_ready, PAIRS)
            act.dma_start(w2_sb, w2.rearrange("e (c p) n -> p e c n", p=P)).then_inc(w2_loaded, 16)
            with act.Fori(0, PAIRS) as i:
                act.wait_ge(xT_done, i + 1)
                nc.scalar.copy(x1T, bank[0][:, :].rearrange("p (c t) -> p c t", c=KC)).then_inc(xT_copied, 1)
                act.wait_ge(ctxT_done, i + 1)
                nc.scalar.copy(ctxT, bank[1][:, :].rearrange("p (c t) -> p c t", c=KC)).then_inc(ctxT_copied, 1)

            act.wait_ge(absf_done, 1)
            nc.scalar.activation(tln, logf, ACT.Exp).then_inc(expf_done, 1)
            act.wait_ge(expf_done, 1)
            nc.scalar.activation(tln, tln, ACT.Ln, bias=1.0).then_inc(lnf_done, 1)
            act.wait_ge(m_ready, 1)
            nc.scalar.activation(tln, logf, ACT.Exp, scale=-1.0).then_inc(em_ready, 1)

            act.wait_ge(tok_ready, 1)
            with act.Fori(0, PAIRS) as i:
                for par in range(2):
                    act.wait_ge(mrep_loaded[par], 16 * i + 16)
                    act.wait_ge(decay_used, 2 * i + par + 1)
                    act.sem_inc(act_seen, 1)
                    for h in range(XH):
                        last = nc.scalar.activation(decay[par][:, h, :], mrep[par][:, h, :], ACT.Exp,
                                                    bias=g_tok[:, bass.ds(2 * i + (h * B + par), 1)], scale=-1.0)
                    last.then_inc(decay_done, 1)

            with act.Fori(0, QUADS) as i:
                act.wait_ge(h_ready, i + 1)
                nc.scalar.activation(sq, hq, ACT.Square).then_inc(sq_done, 1)
                act.wait_ge(xn_ready, i + 1)
                act.sem_inc(act_seen, 1)
                nc.scalar.copy(xn_all[:, bass.ds(4 * i, 4), :], xns).then_inc(xn_kept, 1)
                act.wait_ge(xnT_done, i + 1)
                for c in range(KC):
                    last = nc.scalar.copy(xnT[:, c, :], bank[2 + c][:, :])
                last.then_inc(xnT_copied, 1)
            act.wait_ge(route_exp_in, 1)
            nc.scalar.activation(rt[1], rt[0], ACT.Exp).then_inc(route_exp_out, 1)

            def tile(j, par):
                act.wait_ge(xgT_done, j + 1)
                nc.scalar.copy(xgT[par], bank[0][:, 0:KC * P].rearrange("p (c t) -> p c t", c=KC)).then_inc(xgT_copied, 1)

            def relu(j, par):
                for half in range(2):
                    act.wait_ge(hidT_done, 2 * j + half + 1)
                    nc.scalar.activation(hidT[par][:, 4 * half:4 * half + 4, :],
                                         bank[3 + half][:, :].rearrange("p (c t) -> p c t", c=4), ACT.Relu)\
                        .then_inc(hidT_copied, 1)

            tile(0, 0)
            with act.Fori(0, N_TILES // 2 - 1) as t:
                tile(2 * t + 1, 1)
                relu(2 * t, 0)
                tile(2 * t + 2, 0)
                relu(2 * t + 1, 1)
            tile(N_TILES - 1, 1)
            relu(N_TILES - 2, 0)
            relu(N_TILES - 1, 1)
            for par in range(2):
                act.wait_ge(y_stored[par], 16 * (N_TILES // 2 + 1))
            act.dma_start(b2_sb, b2).then_inc(b2_loaded, 16)
            for g in range(QUADS):
                act.wait_ge(wgtT_done, g + 1)
                nc.scalar.copy(wgtT[:, 4 * g * S:4 * (g + 1) * S], bank[g % 2][0:E, :]).then_inc(wgtT_copied, 1)

        @block.vector
        def _(dve):
            chain = Chain(dve, dve_step)

            def soften(n, s):
                dve.wait_ge(scores_done, n + 1)
                sc = ps_score[s % 2][:, :].rearrange("p (h t) -> p h t", h=4)
                chain.link(nc.vector.tensor_reduce(mx[:, s % 2, :], sc, AX.X, ALU.max))
                m = mx[:, s % 2, :].unsqueeze(2).broadcast_to([P, 4, S])
                nc.vector.tensor_tensor(probs[:, s % 2, :].rearrange("p (h t) -> p h t", h=4), sc, m,
                                        ALU.subtract).then_inc(shifted, 1)

            def norm(n, s):
                half, b, odd = step(s)
                dve.wait_ge(pv_done, n + 1)
                pv = ps_pv[s % 2][:, 0:4 * (HD + 1)].rearrange("p (h e) -> p h e", h=4)
                chain.link(nc.vector.reciprocal(rsum[:, s % 2, :], pv[:, :, HD]))
                r = rsum[:, s % 2, :].unsqueeze(2).broadcast_to([P, 4, HD])
                o = o_sb[:, b, half * 512:(half + 1) * 512].rearrange("p (h z e) -> p h z e", h=4, z=2)[:, :, odd, :]
                nc.vector.tensor_tensor(o, pv[:, :, 0:HD], r, ALU.mult).then_inc(o_normed, 1)

            def layernorm(i):
                for b in range(2):
                    dve.wait_ge(wo_done, 2 * i + b + 1)
                    nc.vector.tensor_tensor(yln[:, b, :], ps_wo[:, 0:D], bo_rep[:, :], ALU.add).then_inc(wo_read, 1)
                    dve.wait_ge(wo_read, 2 * i + b + 2)
                    chain.link(nc.vector.tensor_tensor(yln[:, b, :], yln[:, b, :], xres[:, 2 * i + b, :], ALU.add))
                    chain.link(nc.vector.bn_stats(stats[:, b, :], yln[:, b, :]))
                    dve.sem_inc(stats_seen, 1)
                    chain.link(nc.vector.bn_aggr(mv[:, b, :], stats[:, b, :]))
                nc.vector.tensor_scalar(ve[:, :], mv[:, :, 1], LN_EPS, None, ALU.add).then_inc(var_ready, 1)
                dve.wait_ge(rstd_ready, i + 1)
                for b in range(2):
                    last = nc.vector.tensor_scalar(xres[:, 2 * i + b, :], yln[:, b, :], mv[:, b, 0:1],
                                                   rstd[:, b:b + 1], ALU.subtract, ALU.mult)
                last.then_inc(x1_ready, 1)

            PER = 2 * STEPS + 6
            dve.sem_inc(wo_read, 1)
            soften(0, 0)

            def pair(i, more):
                chain.start(1 + i * PER)
                for s in range(STEPS):
                    if s + 1 < STEPS:
                        soften(i * STEPS + s + 1, s + 1)
                    norm(i * STEPS + s, s)
                if more:
                    soften((i + 1) * STEPS, 0)
                layernorm(i)
                assert chain.k == (PER if more else PER - 1)

            dve.wait_ge(bo_loaded, 16)
            dve.wait_ge(x_loaded, 16)
            with dve.Fori(0, PAIRS - 1) as i:
                pair(i, True)
            pair(PAIRS - 1, False)

            dve.wait_ge(small_loaded, 16 * 7)
            dve.tensor_tensor(gws[:, :, :], gw[:, KC:2 * KC, :], gw[:, 2 * KC:3 * KC, :], ALU.add).then_inc(gws_ready, 1)
            dve.sem_inc(st_copied, 2)
            with dve.Fori(0, PAIRS) as i:
                dve.wait_ge(gates_done, i + 1)
                dve.wait_ge(gates_stored, 16 * i + 16)
                dve.tensor_scalar(gates, bank[2][0:2 * XH, 0:2 * S], gb[:, 0:1], None, ALU.add).then_inc(gates_ready, 1)
                dve.wait_ge(st_done, i + 1)
                dve.sem_inc(dve_seen, 1)
                for odd in range(2):
                    dst = st_all[:, bass.ds(2 * i, 2), :, :].rearrange("p b (c z) t -> p b c z t", z=2)[:, :, :, odd, :]
                    dve.tensor_copy(dst, bank[3 + odd][:, :].rearrange("p (b c t) -> p b c t", b=2, c=2))\
                        .then_inc(st_copied, 1)

            chain.start(PAIRS * PER)
            dve.wait_ge(gates_loaded, 32)
            chain.link(dve.tensor_scalar(logf, gf, -1.0, None, ALU.mult))
            dve.tensor_tensor(logf, logf, gf, ALU.min).then_inc(absf_done, 1)
            chain.link(dve.tensor_scalar(gf, gf, 0.0, None, ALU.min))
            dve.wait_ge(lnf_done, 1)
            chain.link(dve.tensor_tensor(logf, gf, tln, ALU.subtract))
            dve.wait_ge(aug_ready, 2)
            chain.link(dve.tensor_tensor_scan(cum, ones_bh, logf, 0.0, ALU.mult, ALU.add))
            chain.link(dve.tensor_tensor(gdiff, gi, cum, ALU.subtract))
            dve.tensor_tensor_scan(gmax, ones_bh, gdiff, -3.0e38, ALU.mult, ALU.max).then_inc(gmax_ready, 1)
            dve.wait_ge(gmax_ready, 1)
            dve.tensor_tensor(logf, cum, gmax, ALU.add).then_inc(m_ready, 1)
            dve.wait_ge(gtok_done, 1)
            chain.link(dve.tensor_copy(g_tok[:, :], bank[5][:, 0:BH]))
            dve.wait_ge(gmax_stored, 16)
            dve.tensor_copy(em_tok[:, :], bank[6][:, 0:BH]).then_inc(tok_ready, 1)

            dve.sem_inc(decay_used, 2)
            with dve.Fori(0, PAIRS) as i:
                for par in range(2):
                    dve.wait_ge(masked, 2 * i + par + 1)
                    dve.scalar_tensor_tensor(ctmp[par], st_all[:, 2 * i + par, :, :], float(HD) ** -0.5, decay[par],
                                             ALU.mult, ALU.mult).then_inc(ct_done, 1)
                    dve.wait_ge(ct_done, 2 * i + par + 1)
                    dve.sem_inc(decay_used, 1)
                for par in range(2):
                    dve.wait_ge(u_done, 2 * i + par + 1)
                    dve.sem_inc(dve_seen, 1)
                    dve.tensor_copy(u_all[:, 2 * i + par, :], bank[par][:, 0:XH * (HD + 1)]).then_inc(u_copied, 1)

            def norm4(n, mean_of, write):
                dve.sem_inc(dve_seen, 1)
                for b in range(4):
                    last = dve.bn_stats(stats4[:, b, :], mean_of(b))
                chain.link(last)
                dve.sem_inc(dve_seen, 1)
                for b in range(4):
                    last = dve.bn_aggr(mv4[:, b, :], stats4[:, b, :])
                chain.link(last)
                dve.tensor_scalar(ve4[:, :], mv4[:, :, 1], LN_EPS, None, ALU.add).then_inc(var4_ready, 1)
                dve.wait_ge(rstd4_ready, n + 1)
                dve.sem_inc(dve_seen, 1)
                for b in range(4):
                    last = write(b, mv4[:, b, 0:1], rstd4[:, b:b + 1])
                return last

            rms1 = rms_rep[:, :].unsqueeze(1).broadcast_to([P, 16, HD])
            chain.link(dve.tensor_scalar(rms_rep[:, :], rms_rep[:, :], 1.0, None, ALU.add))
            dve.wait_ge(gamma_loaded, 32)
            dve.wait_ge(u_copied, B)
            C1 = PAIRS * PER + chain.k
            QPER = 14
            with dve.Fori(0, QUADS) as i:
                chain.start(C1 + i * QPER)
                u4 = u_all[:, bass.ds(4 * i, 4), :].rearrange("p b (h e) -> p b h e", h=XH)
                em4 = em_tok[:, :].rearrange("p (h b) -> p b h", b=B)[:, bass.ds(4 * i, 4), :]
                d4 = den[:, :].rearrange("p (b h) -> p b h", b=4)
                h4 = hq.rearrange("p (n e) -> p n e", e=HD)
                chain.link(dve.tensor_tensor(d4, u4[:, :, :, HD], em4, ALU.max))
                chain.link(dve.tensor_scalar(den[:, :], den[:, :], MLSTM_EPS, None, ALU.add))
                chain.link(dve.reciprocal(rden[:, :], den[:, :]))
                r4 = rden[:, :].rearrange("p (b h) -> p b h", b=4).unsqueeze(3).broadcast_to([P, 4, XH, HD])
                dve.tensor_tensor(hq.rearrange("p (b h e) -> p b h e", b=4, h=XH), u4[:, :, :, 0:HD], r4, ALU.mult)\
                    .then_inc(h_ready, 1)
                dve.wait_ge(sq_done, i + 1)
                chain.link(dve.tensor_reduce(ssq[:, :], sq.rearrange("p (n e) -> p n e", e=HD), AX.X, ALU.add))
                dve.tensor_scalar(ssq[:, :], ssq[:, :], 1.0 / HD, RMS_EPS, ALU.mult, ALU.add).then_inc(sumsq_ready, 1)
                dve.wait_ge(rsq_ready, i + 1)
                chain.link(dve.tensor_tensor(h4, h4, rsq[:, :].unsqueeze(2).broadcast_to([P, 16, HD]), ALU.mult))
                chain.link(dve.tensor_tensor(h4, h4, rms1, ALU.mult))
                hb = hq.rearrange("p (b d) -> p b d", b=4)
                chain.link(dve.tensor_tensor(hb, hb, xres[:, bass.ds(4 * i, 4), :], ALU.add))
                chain.link(norm4(2 * i, lambda b: hb[:, b, :], lambda b, m, r: dve.tensor_scalar(
                    xres[:, 4 * i + b, :], hb[:, b, :], m, r, ALU.subtract, ALU.mult)))
                chain.link(norm4(2 * i + 1, lambda b: xres[:, 4 * i + b, :], lambda b, m, r: dve.tensor_scalar(
                    xns[:, b, :], xres[:, 4 * i + b, :], m, r, ALU.subtract, ALU.mult)))
                chain.link(dve.tensor_tensor(xns, xns, gamma_rep.unsqueeze(1).broadcast_to([P, 4, D]), ALU.mult))
                dve.tensor_tensor(xns, xns, beta_rep.unsqueeze(1).broadcast_to([P, 4, D]), ALU.add)\
                    .then_inc(xn_ready, 1)
                dve.wait_ge(logits_done, i + 1)
                dve.wait_ge(xn_kept, i + 1)
                dve.sem_inc(dve_seen, 1)
                dve.tensor_tensor(lg_all[:, bass.ds(4 * i, 4), :], bank[4][:, 0:4 * E].rearrange("p (b e) -> p b e", b=4),
                                  br_rep[:, :].unsqueeze(1).broadcast_to([P, 4, E]), ALU.add).then_inc(logits_read, 1)
                assert chain.k == QPER, chain.k
            chain.start(C1 + QUADS * QPER)

            def over_e(v):
                return v.unsqueeze(2).broadcast_to([P, B, E])

            def over_b(v):
                return v.unsqueeze(1).broadcast_to([P, B, E])

            dve.wait_ge(logits_read, QUADS)
            top, idx, tot, inv = (rsmall[:, k, :] for k in range(4))
            chain.link(dve.tensor_reduce(top, lg_all[:, :, :], AX.X, ALU.max))
            dve.tensor_tensor(rt[0], lg_all[:, :, :], over_e(top), ALU.subtract).then_inc(route_exp_in, 1)
            dve.wait_ge(route_exp_out, 1)
            chain.link(dve.tensor_reduce(tot, rt[1], AX.X, ALU.add))
            chain.link(dve.reciprocal(inv, tot))
            chain.link(dve.tensor_tensor(rt[1], rt[1], over_e(inv), ALU.mult))
            dve.wait_ge(consts_ready, 3)
            for k in range(2):
                sc_k, hot = score[:, k, :], rt[2 + k]
                chain.link(dve.tensor_reduce(sc_k, rt[1], AX.X, ALU.max))
                chain.link(dve.tensor_tensor(rt[4], rt[1], over_e(sc_k), ALU.is_equal))
                chain.link(dve.tensor_tensor(rt[4], rt[4], over_b(em8[:, :]), ALU.mult))
                chain.link(dve.tensor_reduce(idx, rt[4], AX.X, ALU.min))
                chain.link(dve.tensor_tensor(hot, over_b(em8[:, :]), over_e(idx), ALU.is_equal))
                if k == 0:
                    chain.link(dve.scalar_tensor_tensor(rt[1], hot, -2.0, rt[1], ALU.mult, ALU.add))
            dve.tensor_tensor(rt[7], rt[2], rt[3], ALU.add).then_inc(counts_in, 1)
            chain.link(dve.tensor_tensor(wgt[:, :, :], rt[2], over_e(score[:, 0, :]), ALU.mult))
            chain.link(dve.tensor_tensor(rt[4], rt[3], over_e(score[:, 1, :]), ALU.mult))
            chain.link(dve.tensor_tensor(wgt[:, :, :], wgt[:, :, :], rt[4], ALU.add))

            dve.wait_ge(counts_out, 1)
            totals = bank[1][:, 0:ROUT].rearrange("p (b e) -> p b e", e=E)
            chain.link(dve.tensor_copy(rt[0], totals))
            cur, nxt = rt[0], rt[4]
            d = 1
            while d < B:
                chain.link(dve.tensor_copy(nxt[:, 0:d, :], cur[:, 0:d, :]))
                chain.link(dve.tensor_tensor(nxt[:, d:, :], cur[:, d:, :], cur[:, 0:B - d, :], ALU.add))
                cur, nxt = nxt, cur
                d *= 2
            before = rt[5]
            chain.link(dve.tensor_tensor(before, cur, totals, ALU.subtract))
            n1, tiles_e, ends, ends2 = (esmall[:, k, :] for k in range(4))
            chain.link(dve.tensor_scalar(n1, cur[:, B - 1, :], 1.0, None, ALU.add))
            w_cnt = wide[:, 0:E * MAX_E_TILES].rearrange("p (e j) -> p e j", e=E)
            chain.link(dve.tensor_tensor(w_cnt, n1.unsqueeze(2).broadcast_to([P, E, MAX_E_TILES]),
                                         io128[:, :].unsqueeze(1).broadcast_to([P, E, MAX_E_TILES]), ALU.is_gt))
            chain.link(dve.tensor_reduce(tiles_e, w_cnt, AX.X, ALU.add))
            chain.link(dve.tensor_copy(ends, tiles_e))
            cur_e, nxt_e = ends, ends2
            d = 1
            while d < E:
                chain.link(dve.tensor_copy(nxt_e[:, 0:d], cur_e[:, 0:d]))
                chain.link(dve.tensor_tensor(nxt_e[:, d:], cur_e[:, d:], cur_e[:, 0:E - d], ALU.add))
                cur_e, nxt_e = nxt_e, cur_e
                d *= 2
            w_tile = wide.rearrange("p (j e) -> p j e", e=E)
            chain.link(dve.tensor_tensor(w_tile, cur_e.unsqueeze(1).broadcast_to([P, N_TILES, E]),
                                         iotile[:, :].unsqueeze(2).broadcast_to([P, N_TILES, E]), ALU.is_le))
            chain.link(dve.tensor_reduce(tile_f[:, :], w_tile, AX.X, ALU.add))
            chain.link(dve.tensor_scalar(tile_e[:, :], tile_f[:, :], float(E - 1), None, ALU.min))
            first = n1
            chain.link(dve.tensor_tensor(first, cur_e, tiles_e, ALU.subtract))
            chain.link(dve.tensor_scalar(first, first, float(P), None, ALU.mult))
            chain.link(dve.tensor_tensor(ends[0:E, :] if cur_e is ends2 else ends2[0:E, :], first[0:E, :],
                                         ident[0:E, 0:E], ALU.mult))
            chain.link(dve.tensor_reduce(zslot_f[:, :], (ends if cur_e is ends2 else ends2)[0:E, :], AX.X, ALU.add))
            chain.link(dve.tensor_copy(zslot[:, :], zslot_f[:, :]))
            chain.link(dve.tensor_tensor(before, before, over_b(first), ALU.add))
            chain.link(dve.scalar_tensor_tensor(before, bank[0][:, 0:ROUT].rearrange("p (b e) -> p b e", e=E), 1.0,
                                                before, ALU.add, ALU.add))
            for k in range(2):
                chain.link(dve.tensor_tensor(rt[6], before, rt[2 + k], ALU.mult))
                chain.link(dve.tensor_reduce(slot_f[:, k, :], rt[6], AX.X, ALU.add))
            dve.tensor_copy(slot[:, :, :], slot_f[:, :, :]).then_inc(route_ready, 1)

            def bias(j, par, e):
                for half in range(2):
                    dve.wait_ge(hid_done, 2 * j + half + 1)
                    dve.tensor_tensor(hid[par][:, half * 512:(half + 1) * 512], bank[1 + half][:, :],
                                      b1_rep[:, e, half * 512:(half + 1) * 512], ALU.add).then_inc(hid_biased, 1)

            def rows_out(j, par):
                dve.wait_ge(y_done, j + 1)
                dve.wait_ge(y_stored[par], 8 * (j - par) + 16)
                dve.tensor_copy(ysb[par], bank[5 + par][:, 0:D]).then_inc(y_copied, 1)

            def expert_of(j):
                return dve.value_load(tile_e[0:1, bass.ds(j, 1)], min_val=0, max_val=E - 1)

            dve.wait_ge(route_ready, 1)
            dve.wait_ge(scattered, 16 * 2 * B)
            dve.wait_ge(b1_loaded, 16)
            for par in range(2):
                dve.sem_inc(y_stored[par], 16)
            bias(0, 0, expert_of(0))
            with dve.Fori(0, N_TILES // 2 - 1) as t:
                bias(2 * t + 1, 1, expert_of(2 * t + 1))
                rows_out(2 * t, 0)
                bias(2 * t + 2, 0, expert_of(2 * t + 2))
                rows_out(2 * t + 1, 1)
            bias(N_TILES - 1, 1, expert_of(N_TILES - 1))
            rows_out(N_TILES - 2, 0)
            rows_out(N_TILES - 1, 1)

            dve.wait_ge(z_gathered, 16)
            dve.wait_ge(b2_loaded, 16)
            dve.tensor_tensor(dterm, yz, b2_sb, ALU.add).then_inc(c_ready, 1)
            dve.wait_ge(csum_done, 1)
            chain.link(dve.tensor_tensor(b2_sb, b2_sb, dterm, ALU.subtract))
            dve.tensor_tensor(yz, b2_sb, bank[2][0:E, 0:D], ALU.add).then_inc(dterm_ready, 1)
            for q in range(QUADS):
                dve.wait_ge(gathered[q], 16 * 8)
                if q:
                    dve.wait_ge(out_ready, q)
                for b in range(4 * q, 4 * q + 4):
                    dve.wait_ge(part_done, b + 1)
                    dve.scalar_tensor_tensor(zout[:, b % 4, :], y_all[:, 0, b, :], score[:, 0, b:b + 1],
                                             bank[3 + b % 4][:, 0:D], ALU.mult, ALU.add).then_inc(part_read, 1)
                    dve.wait_ge(part_read, b + 1)
                    chain.link(dve.scalar_tensor_tensor(zout[:, b % 4, :], y_all[:, 1, b, :], score[:, 1, b:b + 1],
                                                        zout[:, b % 4, :], ALU.mult, ALU.add))
                z_flat = zout.rearrange("p b d -> p (b d)")
                chain.link(dve.scalar_tensor_tensor(z_flat, xres[:, 4 * q:4 * q + 4, :].rearrange("p b d -> p (b d)"),
                                                    2.0, z_flat, ALU.mult, ALU.add))
                norm4(2 * QUADS + q, lambda b: zout[:, b, :], lambda b, m, r: dve.tensor_scalar(
                    xres[:, 4 * q + b, :], zout[:, b, :], m, r, ALU.subtract, ALU.mult)).then_inc(out_ready, 1)


_INS = ['x', 'ctx_1024', 'L0_attn_Wq', 'L0_attn_Wkv', 'L0_attn_Wo', 'L0_attn_bo', 'L0_xattn_igate_kernel',
        'L0_xattn_igate_bias', 'L0_xattn_fgate_kernel', 'L0_xattn_fgate_bias', 'L0_xattn_rms_scale',
        'L0_ffn_gamma', 'L0_ffn_beta', 'L0_ffn_Wr', 'L0_ffn_br', 'L0_ffn_W1', 'L0_ffn_b1', 'L0_ffn_W2', 'L0_ffn_b2']
_OUTS = [((16, 128, 256), 'float32')]


def kernel(**inputs):
    import numpy as _np
    import concourse.bacc as _bacc
    from concourse import mybir as _mybir
    from concourse.bass_utils import run_bass_kernel_spmd as _run

    nc = _bacc.Bacc("TRN2", target_bir_lowering=False, num_devices=1)
    arrays, args = {}, []
    for name in _INS:
        a = _np.ascontiguousarray(inputs[name])
        arrays[f"in_{name}_dram"] = a
        args.append(nc.dram_tensor(f"in_{name}_dram", a.shape, _mybir.dt.from_np(a.dtype), kind="ExternalInput").ap())
    for i, (shape, dtype) in enumerate(_OUTS):
        dt = _mybir.dt.from_np(_np.dtype(dtype))
        args.append(nc.dram_tensor(f"out_{i}_dram", shape, dt, kind="ExternalOutput").ap())
    decoder_layer(nc, *args)
    r = _run(nc, [arrays], core_ids=[0])
    got = tuple(r.results[0][f"out_{i}_dram"] for i in range(len(_OUTS)))
    return got[0]
```

```python
from contextlib import ExitStack

import concourse.bass as bass
from concourse import mybir

F32 = mybir.dt.float32
F32R = mybir.dt.float32r
I32 = mybir.dt.int32
U32 = mybir.dt.uint32
ALU = mybir.AluOpType
ACT = mybir.ActivationFunctionType
AX = mybir.AxisListType

P = 128
LN_EPS = 1e-5
MLSTM_EPS = 1e-6
RMS_EPS = 1e-6


class Chain:

    def __init__(self, eng, sem):
        self.eng, self.sem, self.base, self.k = eng, sem, 0, 0

    def start(self, base):
        self.base, self.k = base, 0

    def link(self, ins):
        self.k += 1
        ins.then_inc(self.sem, 1)
        self.eng.wait_ge(self.sem, self.base + self.k)


def decoder_layer(nc, x, ctx, wq, wkv, wo, bo, ig_w, ig_b, fg_w, fg_b, rms, gamma, beta,
                  wr, br, w1, b1, w2, b2, out):
    B, S, D = x.shape
    INNER = wq.shape[1]
    HD = 64
    NH = INNER // HD
    KC = D // P
    PAIRS = B // 2
    HG = NH // 4
    STEPS = 2 * HG
    IC = INNER // P
    SCALE = float(HD) ** -0.5
    XH = ig_w.shape[1]
    E, _, F = w1.shape
    FC = F // P
    QUADS = B // 4
    N_TILES = (2 * B * S + E + E * (P - 1)) // P
    N_SLOTS = N_TILES * P
    MAX_E_TILES = B * S // P + 1
    assert S == P and D == 2 * P and NH == 16 and XH == 4 and XH * HD == D and N_TILES % 2 == 0

    es = ExitStack()
    with es:
        def sb(name, shape, dt=F32):
            return es.enter_context(nc.sbuf_tensor(name, shape, dt))

        def sem(name):
            return es.enter_context(nc.semaphore(name))

        ident = sb("ident", [P, P])
        xres = sb("xres", [P, B, D])
        neghalf = sb("neghalf", [P, 16])
        def over(area, base, name, words):
            return nc.alloc_sbuf_tensor_at(name, [P, words], F32R, offset=base + area)

        W_WORDS = KC * F + FC * D
        arena_at = nc.sbuf_base
        arena = sb("arena", [P, 4 * W_WORDS])
        w_hi = over(0, arena_at, "w_hi", 2 * W_WORDS)[:, :].rearrange("p (z n) -> p z n", z=2)
        w_lo = over(8 * W_WORDS, arena_at, "w_lo", 2 * W_WORDS)[:, :].rearrange("p (z n) -> p z n", z=2)
        arena2 = sb("arena2", [P, E * F])
        arena3_at = nc.sbuf_base
        arena3 = sb("arena3", [P, B * XH * (HD + 1)])
        hidT_hi = over(8 * F, arena3_at, "hidT_hi", 2 * F)[:, :].rearrange("p (z c t) -> p z c t", z=2, c=FC)
        work_at = nc.sbuf_base
        work = sb("work", [P, 3072])
        xgT_hi = over(16 * D, work_at, "xgT_hi", 2 * D)[:, :].rearrange("p (z c t) -> p z c t", z=2, c=KC)
        xgT_lo = over(24 * D, work_at, "xgT_lo", 2 * D)[:, :].rearrange("p (z c t) -> p z c t", z=2, c=KC)
        norms_at = nc.sbuf_base
        norms = sb("norms", [P, 2 * 4 * D + 2 * D])
        hidT_lo = over(0, norms_at, "hidT_lo", 2 * F)[:, :].rearrange("p (z c t) -> p z c t", z=2, c=FC)
        w_raw = sb("w_raw", [P, W_WORDS])

        off = [0]

        def carve(area, n):
            v = area[:, off[0]:off[0] + n]
            off[0] += n
            return v

        wq_sb = carve(arena, KC * INNER).rearrange("p (c n) -> p c n", c=KC)
        wkv_sb = carve(arena, KC * 2 * INNER).rearrange("p (c n) -> p c n", c=KC)
        wo_sb = carve(arena, IC * D).rearrange("p (c n) -> p c n", c=IC)
        qT = carve(arena, IC * 2 * S).rearrange("p (c t) -> p c t", c=IC)
        kT = carve(arena, IC * 2 * S).rearrange("p (c t) -> p c t", c=IC)
        v_sb = carve(arena, 2 * NH * (HD + 1)).rearrange("p (b h e) -> p b h e", b=2, h=NH)
        pT = carve(arena, 512)
        off[0] = 0
        xs = carve(arena2, 2 * D).rearrange("p (b d) -> p b d", b=2)
        xT = carve(arena2, KC * 2 * S).rearrange("p (c t) -> p c t", c=KC)
        o_sb = carve(arena2, 2 * INNER).rearrange("p (b n) -> p b n", b=2)
        oT = carve(arena2, 2 * IC * S).rearrange("p (b c t) -> p b c t", b=2, c=IC)
        probs = carve(arena2, 2 * 512).rearrange("p (u n) -> p u n", u=2)
        yln = carve(arena2, 2 * D).rearrange("p (b d) -> p b d", b=2)
        bo_rep = carve(arena2, D)

        ctx_aug = arena3[:, :].rearrange("p (b h e) -> p b h e", b=B, h=XH)
        st_all = arena2[:, :].rearrange("p (b h t) -> p b h t", b=B, h=XH)
        u_all = st_all.rearrange("p b h t -> p b (h t)")[:, :, 0:XH * (HD + 1)]
        off[0] = 0
        x1s = carve(work, 2 * D).rearrange("p (b d) -> p b d", b=2)
        cs_ = carve(work, 2 * D).rearrange("p (b d) -> p b d", b=2)
        x1T = carve(work, KC * 2 * S).rearrange("p (c t) -> p c t", c=KC)
        ctxT = carve(work, KC * 2 * S).rearrange("p (c t) -> p c t", c=KC)
        gates = carve(work, 2 * S)[0:2 * XH, :]
        off[0] = 2048
        BH = B * XH
        gi, gf, logf, tln, cum, gdiff, gmax, ones_bh = [carve(work, S)[0:BH, :] for _ in range(8)]
        off[0] = 0
        mrep = [carve(work, XH * S).rearrange("p (h t) -> p h t", h=XH) for _ in range(2)]
        decay = [carve(work, XH * S).rearrange("p (h t) -> p h t", h=XH) for _ in range(2)]
        ctmp = [carve(work, XH * S).rearrange("p (h t) -> p h t", h=XH) for _ in range(2)]
        off[0] = 0
        hq = carve(norms, 4 * D)
        sq = carve(norms, 4 * D)
        gamma_rep = carve(norms, D)
        beta_rep = carve(norms, D)
        xn_all = arena3[:, 0:B * D].rearrange("p (b d) -> p b d", b=B)

        off[0] = 0
        ROUT = B * E
        rt = [carve(work, ROUT).rearrange("p (b e) -> p b e", e=E) for _ in range(8)]
        wide = carve(work, E * N_TILES)
        em8, io128, iotile, tile_f = (carve(work, n) for n in (E, MAX_E_TILES, N_TILES, N_TILES))
        rsmall = carve(work, 4 * B).rearrange("p (k b) -> p k b", b=B)
        esmall = carve(work, 4 * E).rearrange("p (k e) -> p k e", e=E)
        slot_f = carve(work, 2 * B).rearrange("p (k b) -> p k b", b=B)
        off[0] = 2560
        tri = carve(work, P)
        ones = carve(work, P)

        b1_rep = arena2[:, :].rearrange("p (e f) -> p e f", e=E)
        off[0] = 0
        xg = [carve(work, D) for _ in range(2)]
        ysb = [carve(work, D) for _ in range(2)]
        off[0] = 0
        hid = [carve(arena3, F) for _ in range(2)]
        off[0] = 0
        y_all = carve(arena, 2 * B * D).rearrange("p (k b d) -> p k b d", k=2, b=B)
        yz, b2_sb, dterm = [carve(arena, D)[0:E, :] for _ in range(3)]
        zout = carve(arena, 4 * D).rearrange("p (b d) -> p b d", b=4)

        gw = sb("gw", [P, 3 * KC, 2 * XH])
        gws = sb("gws", [P, KC, 2 * XH])
        gb = sb("gb", [2 * XH, 1])
        wr_sb = sb("wr_sb", [P, KC, E])
        br_rep = sb("br_rep", [P, E])
        rms_rep = sb("rms_rep", [P, HD])
        tok = sb("tok", [P, 2 * BH])
        g_tok, em_tok = tok[:, 0:BH], tok[:, BH:]
        xnT = sb("xnT", [P, KC, 4 * S])
        den = sb("den", [P, 16])
        rden = sb("rden", [P, 16])
        ssq = sb("ssq", [P, 16])
        rsq = sb("rsq", [P, 16])
        stats4 = sb("stats4", [P, 4, 6])
        mv4 = sb("mv4", [P, 4, 2])
        ve4 = sb("ve4", [P, 4])
        rstd4 = sb("rstd4", [P, 4])
        lg_all = sb("lg_all", [P, B, E])
        score = sb("score", [P, 2, B])
        slot = sb("slot", [P, 2, B], U32)
        tile_e = sb("tile_e", [P, N_TILES], I32)
        tile_end = sb("tile_end", [P, E], I32)
        zslot_f = sb("zslot_f", [E, 1])
        zslot = sb("zslot", [E, 1], U32)
        wgt = tok[:, :].rearrange("p (b e) -> p b e", e=E)
        off[0] = 0
        wgtT = carve(work, B * S)[0:E, :]

        gates_dram = nc.dram_tensor("gates_dram", [2 * XH, B * S], F32, kind="Internal").ap()
        gmax_dram = nc.dram_tensor("gmax_dram", [BH, S], F32, kind="Internal").ap()
        xg_dram = nc.dram_tensor("xg_dram", [N_SLOTS, D], F32, kind="Internal").ap()
        y_dram = nc.dram_tensor("y_dram", [N_SLOTS, D], F32, kind="Internal").ap()

        mx = sb("mx", [P, 2, 4])
        rsum = sb("rsum", [P, 2, 4])
        stats = sb("stats", [P, 2, 6])
        mv = sb("mv", [P, 2, 2])
        ve = sb("ve", [P, 2])
        rstd = sb("rstd", [P, 2])

        bank = [es.enter_context(nc.psum_tensor(f"bank{i}", [P, 512], F32)) for i in range(8)]
        ps_proj = bank[0:2]
        ps_score = bank[2:4]
        ps_pT = bank[4]
        ps_pv = bank[5:7]
        ps_wo = bank[7]

        ident_ready = sem("ident_ready")
        x0_loaded = sem("x0_loaded")
        x_loaded = sem("x_loaded")
        xs_loaded = sem("xs_loaded")
        wq_loaded = sem("wq_loaded")
        wk_loaded = sem("wk_loaded")
        wv_loaded = sem("wv_loaded")
        wo_loaded = sem("wo_loaded")
        bo_loaded = sem("bo_loaded")
        ones_ready = sem("ones_ready")
        proj_done = sem("proj_done")
        proj_copied = sem("proj_copied")
        scores_done = sem("scores_done")
        shifted = sem("shifted")
        exp_done = sem("exp_done")
        pT_done = sem("pT_done")
        pT_copied = sem("pT_copied")
        pv_done = sem("pv_done")
        o_normed = sem("o_normed")
        wo_done = sem("wo_done")
        wo_read = sem("wo_read")
        var_ready = sem("var_ready")
        rstd_ready = sem("rstd_ready")
        x1_ready = sem("x1_ready")
        dve_step = sem("dve_step")
        stats_seen = sem("stats_seen")
        stored = sem("stored")
        zeros_ready = sem("zeros_ready")
        zeros_stored = sem("zeros_stored")
        aug_ready = sem("aug_ready")
        ctx_loaded = sem("ctx_loaded")
        small_loaded = sem("small_loaded")
        gws_ready = sem("gws_ready")
        st1_loaded = sem("st1_loaded")
        xT_done = sem("xT_done")
        xT_copied = sem("xT_copied")
        ctxT_done = sem("ctxT_done")
        ctxT_copied = sem("ctxT_copied")
        gates_done = sem("gates_done")
        gates_ready = sem("gates_ready")
        gates_stored = sem("gates_stored")
        st_done = sem("st_done")
        st_copied = sem("st_copied")
        gates_loaded = sem("gates_loaded")
        absf_done = sem("absf_done")
        expf_done = sem("expf_done")
        lnf_done = sem("lnf_done")
        gmax_ready = sem("gmax_ready")
        gmax_stored = sem("gmax_stored")
        gtok_done = sem("gtok_done")
        m_ready = sem("m_ready")
        em_ready = sem("em_ready")
        decay_done = sem("decay_done")
        decay_used = sem("decay_used")
        masked = sem("masked")
        ct_done = sem("ct_done")
        u_done = sem("u_done")
        u_copied = sem("u_copied")
        tok_ready = sem("tok_ready")
        act_seen = sem("act_seen")
        dve_seen = sem("dve_seen")
        pool_seen = sem("pool_seen")
        gamma_loaded = sem("gamma_loaded")
        h_ready = sem("h_ready")
        sq_done = sem("sq_done")
        sumsq_ready = sem("sumsq_ready")
        rsq_ready = sem("rsq_ready")
        var4_ready = sem("var4_ready")
        rstd4_ready = sem("rstd4_ready")
        xn_ready = sem("xn_ready")
        xn_normed = sem("xn_normed")
        xn_scaled = sem("xn_scaled")
        xnT_done = sem("xnT_done")
        xnT_copied = sem("xnT_copied")
        logits_done = sem("logits_done")
        logits_read = sem("logits_read")
        route_exp_in = sem("route_exp_in")
        route_exp_out = sem("route_exp_out")
        counts_in = sem("counts_in")
        counts_out = sem("counts_out")
        route_ready = sem("route_ready")
        scattered = sem("scattered")
        b1_loaded = sem("b1_loaded")
        w_loaded = sem("w_loaded")
        w_rounded = sem("w_rounded")
        w_split = sem("w_split")
        xgT_rounded = sem("xgT_rounded")
        xgT_split = sem("xgT_split")
        hidT_rounded = sem("hidT_rounded")
        hidT_split = sem("hidT_split")
        xgT_done = sem("xgT_done")
        hid_done = sem("hid_done")
        hid_biased = sem("hid_biased")
        hidT_done = sem("hidT_done")
        y_done = sem("y_done")
        y_copied = sem("y_copied")
        z_gathered = sem("z_gathered")
        b2_loaded = sem("b2_loaded")
        c_ready = sem("c_ready")
        csum_done = sem("csum_done")
        dterm_ready = sem("dterm_ready")
        wgtT_done = sem("wgtT_done")
        wgtT_copied = sem("wgtT_copied")
        part_done = sem("part_done")
        part_read = sem("part_read")
        out_ready = sem("out_ready")
        consts_ready = sem("consts_ready")
        tri_ready = sem("tri_ready")
        mrep_loaded = [sem(f"mrep_loaded{k}") for k in range(2)]
        xg_loaded = [sem(f"xg_loaded{k}") for k in range(2)]
        y_stored = [sem(f"y_stored{k}") for k in range(2)]
        gathered = [sem(f"gathered{k}") for k in range(QUADS)]

        def fillers(s, more):
            own = {0: [("q", 2), ("k", 2)], 1: [("q", 3), ("k", 3)], 2: [("v", 0, 1)], 3: [("v", 1, 1)],
                   4: [("o", 0, 0)], 5: [("o", 1, 0)], 7: [("o", 0, 1)]}.get(s, [])
            nxt = {3: [("x", 0), ("x", 1)], 4: [("q", 0)], 5: [("k", 0)], 6: [("q", 1)],
                   7: [("k", 1), ("v", 0, 0)]}.get(s, [])
            return own + (nxt if more else [])

        def tail_units(more):
            return ([("v", 1, 0)] if more else []) + [("o", 1, 1)]

        def step(s):
            return s // 4, s // 2 % 2, s % 2

        FIRST = [("x", 0), ("x", 1)] + [(w, g) for g in range(2) for w in "qk"] + [("v", b, 0) for b in range(2)]
        def uses_upto(more):
            return 6

        N_FIRST = len(FIRST)
        SCHEDULE = [u for s in range(STEPS) for u in fillers(s, True)] + tail_units(True)
        N_USES = len(SCHEDULE)
        assert N_USES % 2 == 0 and N_FIRST % 2 == 0

        block = es.enter_context(nc.Block())

        @block.sync
        def _(sp):
            sp.dma_start(xs[:, :, :], x[0:2].rearrange("b s d -> s b d")).then_inc(xs_loaded, 16)
            sp.dma_start(wq_sb, wq.rearrange("(c p) n -> p c n", p=P)).then_inc(wq_loaded, 16)
            wkv_v = wkv.rearrange("(c p) n -> p c n", p=P)
            sp.dma_start(wkv_sb[:, :, 0:INNER], wkv_v[:, :, 0:INNER]).then_inc(wk_loaded, 16)
            sp.dma_start(wkv_sb[:, :, INNER:], wkv_v[:, :, INNER:]).then_inc(wv_loaded, 16)
            sp.dma_start(wo_sb, wo.rearrange("(c p) n -> p c n", p=P)).then_inc(wo_loaded, 16)
            sp.dma_start(bo_rep[:, :], bo[None, :].broadcast_to([P, D])).then_inc(bo_loaded, 16)
            sp.dma_start(xres[:, :, :], x.rearrange("b s d -> s b d")).then_inc(x_loaded, 16)
            for w, b, r in ((ig_w, ig_b, 0), (fg_w, fg_b, XH)):
                sp.dma_start(gw[:, :, r:r + XH], w.rearrange("(c p) n -> p c n", p=P)).then_inc(small_loaded, 16)
                sp.dma_start(gb[r:r + XH, :], b[:, None]).then_inc(small_loaded, 16)
            sp.dma_start(wr_sb[:, :, :], wr.rearrange("(c p) n -> p c n", p=P)).then_inc(small_loaded, 16)
            sp.dma_start(br_rep[:, :], br[None, :].broadcast_to([P, E])).then_inc(small_loaded, 16)
            sp.dma_start(rms_rep[:, :], rms[None, :].broadcast_to([P, HD])).then_inc(small_loaded, 16)
            sp.dma_start(gamma_rep, gamma[None, :].broadcast_to([P, D])).then_inc(gamma_loaded, 16)
            sp.dma_start(beta_rep, beta[None, :].broadcast_to([P, D])).then_inc(gamma_loaded, 16)
            sp.wait_ge(proj_done, 2)
            sp.dma_start(xs[:, :, :], x[2:4].rearrange("b s d -> s b d")).then_inc(xs_loaded, 16)
            X_POS = SCHEDULE.index(("x", 1)) + 1
            with sp.Fori(0, PAIRS - 2) as i:
                sp.wait_ge(proj_done, N_FIRST + i * N_USES + X_POS)
                sp.dma_start(xs[:, :, :], x[bass.ds(2 * i + 4, 2)].rearrange("b s d -> s b d"))\
                    .then_inc(xs_loaded, 16)

            sp.wait_ge(zeros_ready, 1)
            ROW = N_SLOTS * D // P
            for c in range(4):
                sp.dma_start(xg_dram.rearrange("(p r) d -> p (r d)", p=P)[:, c * ROW // 4:(c + 1) * ROW // 4],
                             arena3[:, 0:ROW // 4]).then_inc(zeros_stored, 16)
            sp.wait_ge(zeros_stored, 64)
            for b in range(B):
                sp.dma_start(ctx_aug[:, b, :, 0:HD], ctx[b].rearrange("s (h e) -> s h e", h=XH)).then_inc(ctx_loaded, 16)
            sp.wait_ge(x1_ready, PAIRS)
            sp.dma_start(x1s, xres[:, 0:2, :]).then_inc(st1_loaded, 16)
            sp.dma_start(cs_, ctx[0:2].rearrange("b s d -> s b d")).then_inc(st1_loaded, 16)
            sp.sem_inc(gates_stored, 16)
            with sp.Fori(0, PAIRS - 1) as i:
                sp.wait_ge(ctxT_done, i + 1)
                sp.dma_start(x1s, xres[:, bass.ds(2 * i + 2, 2), :]).then_inc(st1_loaded, 16)
                sp.dma_start(cs_, ctx[bass.ds(2 * i + 2, 2)].rearrange("b s d -> s b d")).then_inc(st1_loaded, 16)
                sp.wait_ge(gates_ready, i + 1)
                sp.dma_start(gates_dram[:, bass.ds(2 * S * i, 2 * S)], gates).then_inc(gates_stored, 16)
            sp.wait_ge(gates_ready, PAIRS)
            sp.dma_start(gates_dram[:, 2 * S * (PAIRS - 1):], gates).then_inc(gates_stored, 16)
            sp.wait_ge(gates_stored, 16 * (PAIRS + 1))
            sp.dma_start(gi, gates_dram[0:XH].rearrange("h (b t) -> (h b) t", b=B)).then_inc(gates_loaded, 16)
            sp.dma_start(gf, gates_dram[XH:].rearrange("h (b t) -> (h b) t", b=B)).then_inc(gates_loaded, 16)
            sp.wait_ge(gmax_ready, 1)
            sp.dma_start(gmax_dram, gmax).then_inc(gmax_stored, 16)
            sp.wait_ge(gmax_stored, 16)
            gm_v = gmax_dram.rearrange("(h b) t -> b h t", b=B)

            def load_mrep(b, par):
                sp.dma_start(mrep[par], gm_v[b][None, :, :].broadcast_to([P, XH, S]) if isinstance(b, int) else
                             gm_v[bass.ds(b, 1)].broadcast_to([P, XH, S])).then_inc(mrep_loaded[par], 16)

            sp.wait_ge(tok_ready, 1)
            for par in range(2):
                load_mrep(par, par)
            with sp.Fori(0, PAIRS - 1) as i:
                for par in range(2):
                    sp.wait_ge(decay_done, 2 * i + par + 1)
                    load_mrep(2 * i + par + 2, par)

            sp.wait_ge(xn_ready, QUADS)
            sp.dma_start(b1_rep, b1[None, :, :].broadcast_to([P, E, F])).then_inc(b1_loaded, 16)
            sp.wait_ge(scattered, 16 * 2 * B)
            for par in range(2):
                sp.dma_start(xg[par], xg_dram[par * P:(par + 1) * P, :]).then_inc(xg_loaded[par], 16)
            for par in range(2):
                sp.wait_ge(xgT_done, par + 1)
                sp.dma_start(xg[par], xg_dram[(2 + par) * P:(3 + par) * P, :]).then_inc(xg_loaded[par], 16)

            def slots(j, par, more):
                if more:
                    sp.wait_ge(xgT_done, j + 3)
                    sp.dma_start(xg[par], xg_dram[bass.ds((j + 4) * P, P), :]).then_inc(xg_loaded[par], 16)
                sp.wait_ge(y_copied, j + 1)
                sp.dma_start(y_dram[bass.ds(j * P, P), :], ysb[par]).then_inc(y_stored[par], 16)

            with sp.Fori(0, N_TILES // 2 - 2) as t:
                for par in range(2):
                    slots(2 * t + par, par, True)
            for j in range(N_TILES - 4, N_TILES):
                slots(j, j % 2, False)

            for q in range(QUADS):
                sp.wait_ge(out_ready, q + 1)
                sp.dma_start(out[4 * q:4 * q + 4].rearrange("b s d -> s b d"), xres[:, 4 * q:4 * q + 4, :])\
                    .then_inc(stored, 16)
            sp.wait_ge(stored, 16 * QUADS)

        @block.gpsimd
        def _(pool):
            pool.memset(ident[:, :], 0.0).then_inc(ident_ready, 1)
            pool.memset(neghalf[:, :], -0.5).then_inc(ident_ready, 1)
            pool.wait_ge(ident_ready, 2)
            pool.affine_select(out=ident[:, :], in_=ident[:, :], compare_op=ALU.not_equal, fill=1.0,
                               base=0, pattern=[[-1, P]], channel_multiplier=1).then_inc(ident_ready, 1)
            pool.memset(v_sb[:, :, :, HD:HD + 1], 1.0).then_inc(ones_ready, 1)
            pool.memset(arena3[:, 0:N_SLOTS * D // P // 4], 0.0).then_inc(zeros_ready, 1)

            def load_weights(e):
                pool.dma_start(w_raw[:, 0:KC * F].rearrange("p (c f) -> p c f", c=KC),
                               w1[bass.ds(e, 1)].rearrange("e (c p) f -> p (e c) f", p=P)).then_inc(w_loaded, 16)
                pool.dma_start(w_raw[:, KC * F:].rearrange("p (c n) -> p c n", c=FC),
                               w2[bass.ds(e, 1)].rearrange("e (c p) n -> p (e c) n", p=P)).then_inc(w_loaded, 16)

            def split_weights(e, z):
                pool.wait_ge(w_loaded, 32 * e + 32)
                pool.sem_inc(pool_seen, 1)
                pool.tensor_copy(w_hi[:, z, :], w_raw[:, :]).then_inc(w_rounded, 1)
                pool.wait_ge(w_rounded, e + 1)
                pool.tensor_tensor(w_lo[:, z, :], w_raw[:, :], w_hi[:, z, :].bitcast(F32), ALU.subtract)\
                    .then_inc(w_split, 1)

            load_weights(0)
            with pool.Fori(0, PAIRS) as i:
                pool.wait_ge(var_ready, i + 1)
                pool.tensor_tensor(rstd[:, :], ve[:, :], neghalf[:, 0:2], ALU.pow).then_inc(rstd_ready, 1)

            pool.wait_ge(zeros_stored, 64)
            pool.memset(ctx_aug[:, :, :, HD:HD + 1], 1.0).then_inc(aug_ready, 1)
            pool.memset(ones_bh, 1.0).then_inc(aug_ready, 1)
            pool.wait_ge(x1_ready, PAIRS)
            for e in range(2):
                split_weights(e, e)
                pool.wait_ge(w_split, e + 1)
                load_weights(e + 1)

            def mask(n):
                pool.wait_ge(decay_done, n + 1)
                pool.affine_select(out=decay[n % 2], in_=decay[n % 2], compare_op=ALU.is_ge, fill=0.0, base=0,
                                   pattern=[[0, XH], [1, S]], channel_multiplier=-1).then_inc(masked, 1)

            def rstd_of(n):
                pool.wait_ge(var4_ready, n + 1)
                pool.tensor_tensor(rstd4[:, :], ve4[:, :], neghalf[:, 0:4], ALU.pow).then_inc(rstd4_ready, 1)

            pool.wait_ge(gamma_loaded, 32)
            mask(0)
            mask(1)
            for q in range(-1, QUADS):
                n = 4 * (q + 1)
                if q >= 0:
                    pool.wait_ge(sumsq_ready, q + 1)
                    pool.tensor_tensor(rsq[:, :], ssq[:, :], neghalf[:, :], ALU.pow).then_inc(rsq_ready, 1)
                if n < B:
                    mask(n + 2)
                if q >= 0:
                    rstd_of(2 * q)
                if n < B:
                    mask(n + 3)
                if n + 4 < B:
                    mask(n + 4)
                if q >= 0:
                    rstd_of(2 * q + 1)
                if n + 4 < B:
                    mask(n + 5)
                if q >= 0:
                    xn4 = xn_all[:, 4 * q:4 * q + 4, :]
                    pool.wait_ge(xn_normed, q + 1)
                    pool.tensor_tensor(xn4, xn4, gamma_rep.unsqueeze(1).broadcast_to([P, 4, D]), ALU.mult)\
                        .then_inc(xn_scaled, 1)
                    pool.wait_ge(xn_scaled, q + 1)
                    pool.tensor_tensor(xn4, xn4, beta_rep.unsqueeze(1).broadcast_to([P, 4, D]), ALU.add)\
                        .then_inc(xn_ready, 1)

            pool.wait_ge(logits_read, QUADS)
            pool.iota(em8[:, :], [[1, E]], base=-E, channel_multiplier=0,
                      allow_small_or_imprecise_dtypes=True).then_inc(consts_ready, 1)
            pool.iota(io128[:, :], [[P, MAX_E_TILES]], base=0, channel_multiplier=0,
                      allow_small_or_imprecise_dtypes=True).then_inc(consts_ready, 1)
            pool.iota(iotile[:, :], [[1, N_TILES]], base=0, channel_multiplier=0,
                      allow_small_or_imprecise_dtypes=True).then_inc(consts_ready, 1)
            pool.memset(tri, 1.0).then_inc(tri_ready, 1)
            pool.memset(ones, 1.0).then_inc(tri_ready, 1)
            pool.wait_ge(tri_ready, 2)
            pool.affine_select(out=tri, in_=tri, compare_op=ALU.is_gt, fill=0.0, base=0, pattern=[[1, P]],
                               channel_multiplier=-1).then_inc(tri_ready, 1)

            pool.wait_ge(route_ready, 1)
            for b in range(B):
                for k in range(2):
                    pool.indirect_dma_start(xg_dram, bass.IndirectOffsetOnAxis(ap=slot[:, k, b:b + 1], axis=0),
                                            xn_all[:, b, :], None).then_inc(scattered, 16)

            def next_weights(e, z, more):
                pool.wait_ge(y_done, pool.value_load(tile_end[0:1, bass.ds(e - 2, 1)], min_val=1, max_val=N_TILES))
                split_weights(e, z)
                if more:
                    pool.wait_ge(w_split, e + 1)
                    load_weights(e + 1)

            with pool.Fori(1, E // 2 - 1) as t:
                for z in range(2):
                    next_weights(2 * t + z, z, True)
            next_weights(E - 2, 0, True)
            next_weights(E - 1, 1, False)

            for par in range(2):
                pool.wait_ge(y_stored[par], 16 * (N_TILES // 2 + 1))
            pool.indirect_dma_start(yz, None, y_dram, bass.IndirectOffsetOnAxis(ap=zslot[:, 0:1], axis=0))\
                .then_inc(z_gathered, 16)
            for b in range(B):
                for k in range(2):
                    pool.indirect_dma_start(y_all[:, k, b, :], None, y_dram,
                                            bass.IndirectOffsetOnAxis(ap=slot[:, k, b:b + 1], axis=0))\
                        .then_inc(gathered[b // 4], 16)
            for q in range(QUADS):
                pool.wait_ge(var4_ready, 2 * QUADS + q + 1)
                pool.tensor_tensor(rstd4[:, :], ve4[:, :], neghalf[:, 0:4], ALU.pow).then_inc(rstd4_ready, 1)

        @block.tensor
        def _(pe):
            uses = Chain(pe, None)

            def unit(kind, *a):
                n = uses.k
                if kind == "o":
                    b, half = a
                    pe.wait_ge(o_normed, pe_at[0] * STEPS + 4 * half + 2 * b + 2)
                pe.wait_ge(proj_copied, uses.base + n - 1) if not (isinstance(uses.base, int) and uses.base + n < 2) else None
                dst = ps_proj[n % 2]
                uses.k += 1
                if kind == "x":
                    for c in range(KC):
                        last = pe.transpose(dst[:, c * P:(c + 1) * P], xs[:, a[0], c * P:(c + 1) * P], ident[:, :])
                elif kind in "qk":
                    g, = a
                    w = wq_sb if kind == "q" else wkv_sb
                    for j in range(2):
                        ch = 2 * g + j
                        for c in range(KC):
                            last = pe.matmul(dst[:, j * 2 * S:(j + 1) * 2 * S], w[:, c, ch * P:(ch + 1) * P],
                                             xT[:, c, :], start=c == 0, stop=c == KC - 1)
                elif kind == "v":
                    b, half = a
                    for c in range(KC):
                        last = pe.matmul(dst[:, :], xT[:, c, b * S:(b + 1) * S],
                                         wkv_sb[:, c, INNER + half * 512:INNER + (half + 1) * 512],
                                         start=c == 0, stop=c == KC - 1)
                else:
                    b, half = a
                    for c in range(4):
                        last = pe.transpose(dst[:, c * P:(c + 1) * P],
                                            o_sb[:, b, (4 * half + c) * P:(4 * half + c + 1) * P], ident[:, :])
                last.then_inc(proj_done, 1)

            pe_at = [0]

            def scores(s):
                half, b, odd = step(s)
                r = HD * odd
                for h in range(4):
                    ch = 4 * half + h
                    last = pe.matmul(ps_score[s % 2][:, h * S:(h + 1) * S],
                                     qT[r:r + HD, ch, b * S:(b + 1) * S],
                                     kT[r:r + HD, ch, b * S:(b + 1) * S], start=True, stop=True)
                last.then_inc(scores_done, 1)

            def pair(i, more):
                pe_at[0] = i
                base = N_FIRST + i * N_USES
                uses.start(base)
                for s in range(STEPS):
                    half, b, odd = step(s)
                    for u in fillers(s, more):
                        if u == ("x", 0):
                            pe.wait_ge(xs_loaded, (i + 2) * 16)
                        if u == ("q", 0):
                            pe.wait_ge(proj_copied, base + uses.k)
                        unit(*u)
                    pe.wait_ge(exp_done, i * STEPS + s + 1)
                    for h in range(4):
                        last = pe.transpose(ps_pT[:, h * S:(h + 1) * S], probs[:, s % 2, h * S:(h + 1) * S], ident[:, :])
                    last.then_inc(pT_done, 1)
                    if s + 1 == 4:
                        pe.wait_ge(proj_copied, base + uses_upto(more))
                    if s + 1 < STEPS:
                        scores(s + 1)
                    pe.wait_ge(pT_copied, i * STEPS + s + 1)
                    for h in range(4):
                        last = pe.matmul(ps_pv[s % 2][:, h * (HD + 1):(h + 1) * (HD + 1)], pT[:, h * S:(h + 1) * S],
                                         v_sb[:, b, 8 * half + 2 * h + odd, :], start=True, stop=True)
                    last.then_inc(pv_done, 1)
                tails = tail_units(more)
                for u in tails[:-1]:
                    unit(*u)
                if more:
                    scores(0)
                unit(*tails[-1])
                for b in range(2):
                    pe.wait_ge(proj_copied, base + uses.k - 1 + b)
                    pe.wait_ge(wo_read, 2 * i + b + 1)
                    for c in range(IC):
                        last = pe.matmul(ps_wo[:, 0:D], oT[:, b, c, :], wo_sb[:, c, :], start=c == 0, stop=c == IC - 1)
                    last.then_inc(wo_done, 1)

            pe.wait_ge(ident_ready, 3)
            pe.wait_ge(xs_loaded, 16)
            uses.start(0)
            for u in FIRST:
                if u == ("q", 0):
                    pe.wait_ge(wq_loaded, 16)
                    pe.wait_ge(proj_copied, 2)
                if u == ("k", 0):
                    pe.wait_ge(wk_loaded, 16)
                if u == ("v", 0, 0):
                    pe.wait_ge(wv_loaded, 16)
                unit(*u)
            pe.wait_ge(proj_copied, N_FIRST)
            pe.wait_ge(ones_ready, 1)
            scores(0)
            pe.wait_ge(wo_loaded, 16)
            with pe.Fori(0, PAIRS - 1) as i:
                pair(i, True)
            pair(PAIRS - 1, False)

            pe.wait_ge(gws_ready, 1)
            with pe.Fori(0, PAIRS) as i:
                pe.wait_ge(st1_loaded, 32 * i + 32)
                for src, bk, done in ((x1s, bank[0], xT_done), (cs_, bank[1], ctxT_done)):
                    for c in range(KC):
                        for b in range(2):
                            last = pe.transpose(bk[:, (2 * c + b) * P:(2 * c + b + 1) * P],
                                                src[:, b, c * P:(c + 1) * P], ident[:, :])
                    last.then_inc(done, 1)
                pe.wait_ge(st_copied, 2 * i + 2)
                pe.wait_ge(xT_copied, i + 1)
                pe.wait_ge(ctxT_copied, i + 1)
                for c in range(KC):
                    pe.matmul(bank[2][0:2 * XH, 0:2 * S], gw[:, c, :], x1T[:, c, :], start=c == 0, stop=False)
                for c in range(KC):
                    last = pe.matmul(bank[2][0:2 * XH, 0:2 * S], gws[:, c, :], ctxT[:, c, :],
                                     start=False, stop=c == KC - 1)
                last.then_inc(gates_done, 1)
                for b in range(2):
                    for h in range(XH):
                        odd, c = h % 2, h // 2
                        r = HD * odd
                        last = pe.matmul(bank[3 + odd][:, (2 * b + c) * S:(2 * b + c + 1) * S],
                                         ctxT[r:r + HD, c, b * S:(b + 1) * S], x1T[r:r + HD, c, b * S:(b + 1) * S],
                                         start=True, stop=True)
                last.then_inc(st_done, 1)
            pe.wait_ge(em_ready, 1)
            pe.transpose(bank[5][:, 0:BH], gdiff, ident[0:BH, 0:BH])
            pe.transpose(bank[6][:, 0:BH], tln, ident[0:BH, 0:BH]).then_inc(gtok_done, 1)
            pe.wait_ge(ctx_loaded, 16 * B)
            pe.wait_ge(aug_ready, 2)

            def weighted(n):
                pe.wait_ge(ct_done, n + 1)
                for h in range(XH):
                    last = pe.matmul(bank[n % 2][:, h * (HD + 1):(h + 1) * (HD + 1)], ctmp[n % 2][:, h, :],
                                     ctx_aug[:, n, h, :], start=True, stop=True)
                last.then_inc(u_done, 1)

            def xn_transposes(q):
                pe.wait_ge(xn_ready, q + 1)
                for c in range(KC):
                    for b in range(4):
                        last = pe.transpose(bank[2 + c][:, b * S:(b + 1) * S], xn_all[:, 4 * q + b, c * P:(c + 1) * P],
                                            ident[:, :])
                last.then_inc(xnT_done, 1)

            def logits(q):
                pe.wait_ge(xnT_copied, q + 1)
                for b in range(4):
                    for c in range(KC):
                        last = pe.matmul(bank[4][:, b * E:(b + 1) * E], xnT[:, c, b * S:(b + 1) * S], wr_sb[:, c, :],
                                         start=c == 0, stop=c == KC - 1)
                last.then_inc(logits_done, 1)

            for q in range(-1, QUADS):
                n = 4 * (q + 1)
                if n < B:
                    weighted(n)
                    weighted(n + 1)
                if q >= 1:
                    xn_transposes(q - 1)
                if n < B:
                    weighted(n + 2)
                if q >= 1:
                    logits(q - 1)
                if n < B:
                    weighted(n + 3)
            xn_transposes(QUADS - 1)
            logits(QUADS - 1)

            pe.wait_ge(counts_in, 1)
            pe.wait_ge(tri_ready, 3)
            chosen = rt[7].rearrange("p b e -> p (b e)")
            pe.matmul(bank[0][:, 0:ROUT], tri, chosen, start=True, stop=True)
            pe.matmul(bank[1][:, 0:ROUT], ones, chosen, start=True, stop=True).then_inc(counts_out, 1)

            def slot_transposes(j, par):
                pe.wait_ge(xg_loaded[par], 8 * (j - par) + 16)
                for c in range(KC):
                    last = pe.transpose(bank[0][:, c * P:(c + 1) * P], xg[par][:, c * P:(c + 1) * P], ident[:, :])
                last.then_inc(xgT_done, 1)

            def hidden(j, par, half, e):
                if half == 0:
                    pe.wait_ge(xgT_split, j + 1)
                    pe.wait_ge(w_split, e + 1)
                if not isinstance(j, int) or j > 0:
                    pe.wait_ge(hid_biased, 2 * j + half - 1)
                z = e % 2
                for c in range(KC):
                    f = c * F + half * 512
                    hi, lo = w_hi[:, z, f:f + 512], w_lo[:, z, f:f + 512]
                    pe.matmul(bank[1 + half][:, :], xgT_hi[:, par, c, :], hi, start=c == 0, stop=False)
                    pe.matmul(bank[1 + half][:, :], xgT_hi[:, par, c, :], lo, start=False, stop=False)
                    last = pe.matmul(bank[1 + half][:, :], xgT_lo[:, par, c, :], hi, start=False, stop=c == KC - 1)
                last.then_inc(hid_done, 1)

            def hidden_transposes(j, par):
                for half in range(2):
                    pe.wait_ge(hid_biased, 2 * j + half + 1)
                    for c in range(4):
                        f = (4 * half + c) * P
                        last = pe.transpose(bank[3 + half][:, c * P:(c + 1) * P], hid[par][:, f:f + P], ident[:, :])
                    last.then_inc(hidT_done, 1)

            def expert_out(j, par, e):
                z = e % 2
                y = bank[5 + par][:, 0:D]
                for half in range(2):
                    pe.wait_ge(hidT_split, 2 * j + half + 1)
                    for c in range(4 * half, 4 * half + 4):
                        f = KC * F + c * D
                        hi, lo = w_hi[:, z, f:f + D], w_lo[:, z, f:f + D]
                        pe.matmul(y, hidT_hi[:, par, c, :], hi, start=c == 0, stop=False)
                        pe.matmul(y, hidT_hi[:, par, c, :], lo, start=False, stop=False)
                        last = pe.matmul(y, hidT_lo[:, par, c, :], hi, start=False, stop=c == FC - 1)
                last.then_inc(y_done, 1)

            def expert_of(j):
                return pe.value_load(tile_e[0:1, bass.ds(j, 1)], min_val=0, max_val=E - 1)

            def tile(j, par, ahead, e, e_next):
                if ahead >= 1:
                    hidden(j + 1, 1 - par, 0, e_next)
                hidden_transposes(j, par)
                if ahead >= 1:
                    hidden(j + 1, 1 - par, 1, e_next)
                if ahead >= 2:
                    pe.wait_ge(xgT_split, j + 2)
                    slot_transposes(j + 2, par)
                expert_out(j, par, e)

            pe.wait_ge(route_ready, 1)
            slot_transposes(0, 0)
            e0 = expert_of(0)
            for half in range(2):
                hidden(0, 0, half, e0)
            slot_transposes(1, 1)
            with pe.Fori(0, N_TILES // 2 - 1) as t:
                e0, e1, e2 = (expert_of(2 * t + k) for k in range(3))
                tile(2 * t, 0, 2, e0, e1)
                tile(2 * t + 1, 1, 2, e1, e2)
            e0, e1 = expert_of(N_TILES - 2), expert_of(N_TILES - 1)
            tile(N_TILES - 2, 0, 1, e0, e1)
            tile(N_TILES - 1, 1, 0, e1, None)

            for g in range(QUADS):
                for b in range(4):
                    last = pe.transpose(bank[g % 2][0:E, b * S:(b + 1) * S], wgt[:, 4 * g + b, :], ident[:, :])
                last.then_inc(wgtT_done, 1)
                pe.wait_ge(wgtT_copied, g + 1)
            pe.wait_ge(c_ready, 1)
            pe.matmul(bank[2][0:E, 0:D], ones[0:E, 0:E], dterm, start=True, stop=True).then_inc(csum_done, 1)
            pe.wait_ge(dterm_ready, 1)
            for b in range(B):
                if b >= 4:
                    pe.wait_ge(part_read, b - 3)
                pe.matmul(bank[3 + b % 4][:, 0:D], wgtT[:, b * S:(b + 1) * S], yz, start=True, stop=True)\
                    .then_inc(part_done, 1)

        @block.scalar
        def _(act):
            def copy_unit(n, kind, *a):
                act.wait_ge(proj_done, n + 1)
                src = ps_proj[copy_at[0] % 2]
                copy_at[0] += 1
                if kind == "x":
                    o, i_ = xT[:, :, a[0] * S:(a[0] + 1) * S], src[:, 0:KC * P].rearrange("p (c t) -> p c t", c=KC)
                elif kind in "qk":
                    o = (qT if kind == "q" else kT)[:, 2 * a[0]:2 * a[0] + 2, :]
                    i_ = src[:, :].rearrange("p (c t) -> p c t", c=2)
                elif kind == "v":
                    o = v_sb[:, a[0], 8 * a[1]:8 * a[1] + 8, 0:HD]
                    i_ = src[:, :].rearrange("p (h e) -> p h e", h=8)
                else:
                    o = oT[:, a[0], 4 * a[1]:4 * a[1] + 4, :]
                    i_ = src[:, :].rearrange("p (c t) -> p c t", c=4)
                nc.scalar.copy(o, i_).then_inc(proj_copied, 1)

            copy_at = [0]
            for n, u in enumerate(FIRST):
                copy_unit(n, *u)

            def pair(i, more):
                n = N_FIRST + i * N_USES
                k = 0
                copy_at[0] = 0
                for s in range(STEPS):
                    act.wait_ge(shifted, i * STEPS + s + 1)
                    nc.scalar.activation(probs[:, s % 2, :], probs[:, s % 2, :], ACT.Exp, scale=SCALE)\
                        .then_inc(exp_done, 1)
                    for u in fillers(s, more):
                        copy_unit(n + k, *u)
                        k += 1
                    act.wait_ge(pT_done, i * STEPS + s + 1)
                    nc.scalar.copy(pT, ps_pT[:, :]).then_inc(pT_copied, 1)
                for u in tail_units(more):
                    copy_unit(n + k, *u)
                    k += 1

            with act.Fori(0, PAIRS - 1) as i:
                pair(i, True)
            pair(PAIRS - 1, False)

            with act.Fori(0, PAIRS) as i:
                act.wait_ge(xT_done, i + 1)
                nc.scalar.copy(x1T, bank[0][:, :].rearrange("p (c t) -> p c t", c=KC)).then_inc(xT_copied, 1)
                act.wait_ge(ctxT_done, i + 1)
                nc.scalar.copy(ctxT, bank[1][:, :].rearrange("p (c t) -> p c t", c=KC)).then_inc(ctxT_copied, 1)

            act.wait_ge(absf_done, 1)
            nc.scalar.activation(tln, logf, ACT.Exp).then_inc(expf_done, 1)
            act.wait_ge(expf_done, 1)
            nc.scalar.activation(tln, tln, ACT.Ln, bias=1.0).then_inc(lnf_done, 1)
            act.wait_ge(m_ready, 1)
            nc.scalar.activation(tln, logf, ACT.Exp, scale=-1.0).then_inc(em_ready, 1)

            act.wait_ge(tok_ready, 1)
            def decays(n):
                act.wait_ge(mrep_loaded[n % 2], 16 * (n // 2) + 16)
                if n >= 2:
                    act.wait_ge(decay_used, n - 1)
                for h in range(XH):
                    last = nc.scalar.activation(decay[n % 2][:, h, :], mrep[n % 2][:, h, :], ACT.Exp,
                                                bias=g_tok[:, h * B + n:h * B + n + 1], scale=-1.0)
                last.then_inc(decay_done, 1)

            def router_copies(q):
                act.wait_ge(xnT_done, q + 1)
                for c in range(KC):
                    last = nc.scalar.copy(xnT[:, c, :], bank[2 + c][:, :])
                last.then_inc(xnT_copied, 1)
                act.wait_ge(logits_done, q + 1)
                nc.scalar.copy(lg_all[:, 4 * q:4 * q + 4, :], bank[4][:, 0:4 * E].rearrange("p (b e) -> p b e", b=4))\
                    .then_inc(logits_read, 1)

            decays(0)
            decays(1)
            for q in range(-1, QUADS):
                n = 4 * (q + 1)
                if q >= 0:
                    act.wait_ge(h_ready, q + 1)
                    nc.scalar.activation(sq, hq, ACT.Square).then_inc(sq_done, 1)
                if n < B:
                    decays(n + 2)
                    decays(n + 3)
                if q >= 1:
                    router_copies(q - 1)
                if n + 4 < B:
                    decays(n + 4)
                    decays(n + 5)
            router_copies(QUADS - 1)
            act.wait_ge(route_exp_in, 1)
            nc.scalar.activation(rt[1], rt[0], ACT.Exp).then_inc(route_exp_out, 1)

            def round_xg(j, par):
                act.wait_ge(xgT_done, j + 1)
                nc.scalar.copy(xgT_hi[:, par, :, :], bank[0][:, 0:KC * P].rearrange("p (c t) -> p c t", c=KC))\
                    .then_inc(xgT_rounded, 1)

            def relu(j, par):
                for half in range(2):
                    act.wait_ge(hidT_done, 2 * j + half + 1)
                    nc.scalar.activation(hidT_hi[:, par, 4 * half:4 * half + 4, :],
                                         bank[3 + half][:, :].rearrange("p (c t) -> p c t", c=4), ACT.Relu)\
                        .then_inc(hidT_rounded, 1)

            act.wait_ge(scattered, 16 * 2 * B)
            round_xg(0, 0)
            round_xg(1, 1)
            with act.Fori(0, N_TILES // 2 - 1) as t:
                for par in range(2):
                    relu(2 * t + par, par)
                    round_xg(2 * t + par + 2, par)
            relu(N_TILES - 2, 0)
            relu(N_TILES - 1, 1)
            for par in range(2):
                act.wait_ge(y_stored[par], 16 * (N_TILES // 2 + 1))
            act.dma_start(b2_sb, b2).then_inc(b2_loaded, 16)
            for g in range(QUADS):
                act.wait_ge(wgtT_done, g + 1)
                nc.scalar.copy(wgtT[:, 4 * g * S:4 * (g + 1) * S], bank[g % 2][0:E, :]).then_inc(wgtT_copied, 1)

        @block.vector
        def _(dve):
            chain = Chain(dve, dve_step)

            def soften(n, s):
                dve.wait_ge(scores_done, n + 1)
                sc = ps_score[s % 2][:, :].rearrange("p (h t) -> p h t", h=4)
                chain.link(nc.vector.tensor_reduce(mx[:, s % 2, :], sc, AX.X, ALU.max))
                m = mx[:, s % 2, :].unsqueeze(2).broadcast_to([P, 4, S])
                nc.vector.tensor_tensor(probs[:, s % 2, :].rearrange("p (h t) -> p h t", h=4), sc, m,
                                        ALU.subtract).then_inc(shifted, 1)

            def norm(n, s):
                half, b, odd = step(s)
                dve.wait_ge(pv_done, n + 1)
                pv = ps_pv[s % 2][:, 0:4 * (HD + 1)].rearrange("p (h e) -> p h e", h=4)
                chain.link(nc.vector.reciprocal(rsum[:, s % 2, :], pv[:, :, HD]))
                r = rsum[:, s % 2, :].unsqueeze(2).broadcast_to([P, 4, HD])
                o = o_sb[:, b, half * 512:(half + 1) * 512].rearrange("p (h z e) -> p h z e", h=4, z=2)[:, :, odd, :]
                nc.vector.tensor_tensor(o, pv[:, :, 0:HD], r, ALU.mult).then_inc(o_normed, 1)

            def layernorm(i):
                for b in range(2):
                    dve.wait_ge(wo_done, 2 * i + b + 1)
                    nc.vector.tensor_tensor(yln[:, b, :], ps_wo[:, 0:D], bo_rep[:, :], ALU.add).then_inc(wo_read, 1)
                    dve.wait_ge(wo_read, 2 * i + b + 2)
                    chain.link(nc.vector.tensor_tensor(yln[:, b, :], yln[:, b, :], xres[:, 2 * i + b, :], ALU.add))
                    chain.link(nc.vector.bn_stats(stats[:, b, :], yln[:, b, :]))
                    dve.sem_inc(stats_seen, 1)
                    chain.link(nc.vector.bn_aggr(mv[:, b, :], stats[:, b, :]))
                nc.vector.tensor_scalar(ve[:, :], mv[:, :, 1], LN_EPS, None, ALU.add).then_inc(var_ready, 1)
                dve.wait_ge(rstd_ready, i + 1)
                for b in range(2):
                    last = nc.vector.tensor_scalar(xres[:, 2 * i + b, :], yln[:, b, :], mv[:, b, 0:1],
                                                   rstd[:, b:b + 1], ALU.subtract, ALU.mult)
                last.then_inc(x1_ready, 1)

            PER = 2 * STEPS + 6
            dve.sem_inc(wo_read, 1)
            soften(0, 0)

            def pair(i, more):
                chain.start(1 + i * PER)
                for s in range(STEPS):
                    if s + 1 < STEPS:
                        soften(i * STEPS + s + 1, s + 1)
                    norm(i * STEPS + s, s)
                if more:
                    soften((i + 1) * STEPS, 0)
                layernorm(i)
                assert chain.k == (PER if more else PER - 1)

            dve.wait_ge(bo_loaded, 16)
            dve.wait_ge(x_loaded, 16)
            with dve.Fori(0, PAIRS - 1) as i:
                pair(i, True)
            pair(PAIRS - 1, False)

            dve.wait_ge(small_loaded, 16 * 7)
            dve.tensor_tensor(gws[:, :, :], gw[:, KC:2 * KC, :], gw[:, 2 * KC:3 * KC, :], ALU.add).then_inc(gws_ready, 1)
            dve.sem_inc(st_copied, 2)
            with dve.Fori(0, PAIRS) as i:
                dve.wait_ge(gates_done, i + 1)
                dve.wait_ge(gates_stored, 16 * i + 16)
                dve.tensor_scalar(gates, bank[2][0:2 * XH, 0:2 * S], gb[:, 0:1], None, ALU.add).then_inc(gates_ready, 1)
                dve.wait_ge(st_done, i + 1)
                dve.sem_inc(dve_seen, 1)
                for odd in range(2):
                    dst = st_all[:, bass.ds(2 * i, 2), :, :].rearrange("p b (c z) t -> p b c z t", z=2)[:, :, :, odd, :]
                    dve.tensor_copy(dst, bank[3 + odd][:, :].rearrange("p (b c t) -> p b c t", b=2, c=2))\
                        .then_inc(st_copied, 1)

            chain.start(PAIRS * PER)
            dve.wait_ge(gates_loaded, 32)
            chain.link(dve.tensor_scalar(logf, gf, -1.0, None, ALU.mult))
            dve.tensor_tensor(logf, logf, gf, ALU.min).then_inc(absf_done, 1)
            chain.link(dve.tensor_scalar(gf, gf, 0.0, None, ALU.min))
            dve.wait_ge(lnf_done, 1)
            chain.link(dve.tensor_tensor(logf, gf, tln, ALU.subtract))
            dve.wait_ge(aug_ready, 2)
            chain.link(dve.tensor_tensor_scan(cum, ones_bh, logf, 0.0, ALU.mult, ALU.add))
            chain.link(dve.tensor_tensor(gdiff, gi, cum, ALU.subtract))
            dve.tensor_tensor_scan(gmax, ones_bh, gdiff, -3.0e38, ALU.mult, ALU.max).then_inc(gmax_ready, 1)
            dve.wait_ge(gmax_ready, 1)
            dve.tensor_tensor(logf, cum, gmax, ALU.add).then_inc(m_ready, 1)
            dve.wait_ge(gtok_done, 1)
            chain.link(dve.tensor_copy(g_tok[:, :], bank[5][:, 0:BH]))
            dve.wait_ge(gmax_stored, 16)
            dve.tensor_copy(em_tok[:, :], bank[6][:, 0:BH]).then_inc(tok_ready, 1)

            chain.link(dve.tensor_scalar(rms_rep[:, :], rms_rep[:, :], 1.0, None, ALU.add))
            rms1 = rms_rep[:, :].unsqueeze(1).broadcast_to([P, 16, HD])

            def weigh(n):
                dve.wait_ge(masked, n + 1)
                dve.scalar_tensor_tensor(ctmp[n % 2], st_all[:, n, :, :], float(HD) ** -0.5, decay[n % 2],
                                         ALU.mult, ALU.mult).then_inc(ct_done, 1)
                dve.wait_ge(ct_done, n + 1)
                dve.sem_inc(decay_used, 1)

            def keep_u(n):
                dve.wait_ge(u_done, n + 1)
                dve.tensor_copy(u_all[:, n, :], bank[n % 2][:, 0:XH * (HD + 1)]).then_inc(u_copied, 1)

            def variance4(of):
                for b in range(4):
                    last = dve.bn_stats(stats4[:, b, :], of(b))
                chain.link(last)
                for b in range(4):
                    last = dve.bn_aggr(mv4[:, b, :], stats4[:, b, :])
                chain.link(last)
                dve.tensor_scalar(ve4[:, :], mv4[:, :, 1], LN_EPS, None, ALU.add).then_inc(var4_ready, 1)

            def normed4(n, of, to):
                dve.wait_ge(rstd4_ready, n + 1)
                for b in range(4):
                    last = dve.tensor_scalar(to(b), of(b), mv4[:, b, 0:1], rstd4[:, b:b + 1], ALU.subtract, ALU.mult)
                return last

            h4 = hq.rearrange("p (n e) -> p n e", e=HD)
            hb = hq.rearrange("p (b d) -> p b d", b=4)
            for q in range(-1, QUADS):
                n = 4 * (q + 1)
                four = slice(4 * q, 4 * q + 4)
                if q >= 0:
                    dve.wait_ge(u_copied, 4 * q + 4)
                    u4 = u_all[:, four, :].rearrange("p b (h e) -> p b h e", h=XH)
                    em4 = em_tok[:, :].rearrange("p (h b) -> p b h", b=B)[:, four, :]
                    d4 = den[:, :].rearrange("p (b h) -> p b h", b=4)
                    chain.link(dve.tensor_tensor(d4, u4[:, :, :, HD], em4, ALU.max))
                    chain.link(dve.tensor_scalar(den[:, :], den[:, :], MLSTM_EPS, None, ALU.add))
                    chain.link(dve.reciprocal(rden[:, :], den[:, :]))
                    r4 = rden[:, :].rearrange("p (b h) -> p b h", b=4).unsqueeze(3).broadcast_to([P, 4, XH, HD])
                    dve.tensor_tensor(hq.rearrange("p (b h e) -> p b h e", b=4, h=XH), u4[:, :, :, 0:HD], r4, ALU.mult)\
                        .then_inc(h_ready, 1)
                if n < B:
                    weigh(n)
                if q >= 0:
                    dve.wait_ge(sq_done, q + 1)
                    chain.link(dve.tensor_reduce(ssq[:, :], sq.rearrange("p (n e) -> p n e", e=HD), AX.X, ALU.add))
                    dve.tensor_scalar(ssq[:, :], ssq[:, :], 1.0 / HD, RMS_EPS, ALU.mult, ALU.add)\
                        .then_inc(sumsq_ready, 1)
                if n < B:
                    weigh(n + 1)
                    keep_u(n)
                if q >= 0:
                    dve.wait_ge(rsq_ready, q + 1)
                    chain.link(dve.tensor_tensor(h4, h4, rsq[:, :].unsqueeze(2).broadcast_to([P, 16, HD]), ALU.mult))
                    chain.link(dve.tensor_tensor(h4, h4, rms1, ALU.mult))
                    chain.link(dve.tensor_tensor(hb, hb, xres[:, four, :], ALU.add))
                    variance4(lambda b: hb[:, b, :])
                if n < B:
                    keep_u(n + 1)
                    weigh(n + 2)
                if q >= 0:
                    chain.link(normed4(2 * q, lambda b: hb[:, b, :], lambda b: xres[:, 4 * q + b, :]))
                    variance4(lambda b: xres[:, 4 * q + b, :])
                if n < B:
                    weigh(n + 3)
                    keep_u(n + 2)
                if q >= 0:
                    normed4(2 * q + 1, lambda b: xres[:, 4 * q + b, :], lambda b: xn_all[:, 4 * q + b, :])\
                        .then_inc(xn_normed, 1)
                if n < B:
                    keep_u(n + 3)

            def over_e(v):
                return v.unsqueeze(2).broadcast_to([P, B, E])

            def over_b(v):
                return v.unsqueeze(1).broadcast_to([P, B, E])

            dve.wait_ge(logits_read, QUADS)
            top, idx, tot, inv = (rsmall[:, k, :] for k in range(4))
            chain.link(dve.tensor_tensor(lg_all[:, :, :], lg_all[:, :, :], over_b(br_rep[:, :]), ALU.add))
            chain.link(dve.tensor_reduce(top, lg_all[:, :, :], AX.X, ALU.max))
            dve.tensor_tensor(rt[0], lg_all[:, :, :], over_e(top), ALU.subtract).then_inc(route_exp_in, 1)
            dve.wait_ge(route_exp_out, 1)
            chain.link(dve.tensor_reduce(tot, rt[1], AX.X, ALU.add))
            chain.link(dve.reciprocal(inv, tot))
            chain.link(dve.tensor_tensor(rt[1], rt[1], over_e(inv), ALU.mult))
            dve.wait_ge(consts_ready, 3)
            for k in range(2):
                sc_k, hot = score[:, k, :], rt[2 + k]
                chain.link(dve.tensor_reduce(sc_k, rt[1], AX.X, ALU.max))
                chain.link(dve.tensor_tensor(rt[4], rt[1], over_e(sc_k), ALU.is_equal))
                chain.link(dve.tensor_tensor(rt[4], rt[4], over_b(em8[:, :]), ALU.mult))
                chain.link(dve.tensor_reduce(idx, rt[4], AX.X, ALU.min))
                chain.link(dve.tensor_tensor(hot, over_b(em8[:, :]), over_e(idx), ALU.is_equal))
                if k == 0:
                    chain.link(dve.scalar_tensor_tensor(rt[1], hot, -2.0, rt[1], ALU.mult, ALU.add))
            dve.tensor_tensor(rt[7], rt[2], rt[3], ALU.add).then_inc(counts_in, 1)
            chain.link(dve.tensor_tensor(wgt[:, :, :], rt[2], over_e(score[:, 0, :]), ALU.mult))
            chain.link(dve.tensor_tensor(rt[4], rt[3], over_e(score[:, 1, :]), ALU.mult))
            chain.link(dve.tensor_tensor(wgt[:, :, :], wgt[:, :, :], rt[4], ALU.add))

            dve.wait_ge(counts_out, 1)
            totals = bank[1][:, 0:ROUT].rearrange("p (b e) -> p b e", e=E)
            chain.link(dve.tensor_copy(rt[0], totals))
            cur, nxt = rt[0], rt[4]
            d = 1
            while d < B:
                chain.link(dve.tensor_copy(nxt[:, 0:d, :], cur[:, 0:d, :]))
                chain.link(dve.tensor_tensor(nxt[:, d:, :], cur[:, d:, :], cur[:, 0:B - d, :], ALU.add))
                cur, nxt = nxt, cur
                d *= 2
            before = rt[5]
            chain.link(dve.tensor_tensor(before, cur, totals, ALU.subtract))
            n1, tiles_e, ends, ends2 = (esmall[:, k, :] for k in range(4))
            chain.link(dve.tensor_scalar(n1, cur[:, B - 1, :], 1.0, None, ALU.add))
            w_cnt = wide[:, 0:E * MAX_E_TILES].rearrange("p (e j) -> p e j", e=E)
            chain.link(dve.tensor_tensor(w_cnt, n1.unsqueeze(2).broadcast_to([P, E, MAX_E_TILES]),
                                         io128[:, :].unsqueeze(1).broadcast_to([P, E, MAX_E_TILES]), ALU.is_gt))
            chain.link(dve.tensor_reduce(tiles_e, w_cnt, AX.X, ALU.add))
            chain.link(dve.tensor_copy(ends, tiles_e))
            cur_e, nxt_e = ends, ends2
            d = 1
            while d < E:
                chain.link(dve.tensor_copy(nxt_e[:, 0:d], cur_e[:, 0:d]))
                chain.link(dve.tensor_tensor(nxt_e[:, d:], cur_e[:, d:], cur_e[:, 0:E - d], ALU.add))
                cur_e, nxt_e = nxt_e, cur_e
                d *= 2
            w_tile = wide.rearrange("p (j e) -> p j e", e=E)
            chain.link(dve.tensor_tensor(w_tile, cur_e.unsqueeze(1).broadcast_to([P, N_TILES, E]),
                                         iotile[:, :].unsqueeze(2).broadcast_to([P, N_TILES, E]), ALU.is_le))
            chain.link(dve.tensor_reduce(tile_f[:, :], w_tile, AX.X, ALU.add))
            chain.link(dve.tensor_scalar(tile_e[:, :], tile_f[:, :], float(E - 1), None, ALU.min))
            chain.link(dve.tensor_copy(tile_end[:, :], cur_e))
            first = n1
            chain.link(dve.tensor_tensor(first, cur_e, tiles_e, ALU.subtract))
            chain.link(dve.tensor_scalar(first, first, float(P), None, ALU.mult))
            chain.link(dve.tensor_tensor(ends[0:E, :] if cur_e is ends2 else ends2[0:E, :], first[0:E, :],
                                         ident[0:E, 0:E], ALU.mult))
            chain.link(dve.tensor_reduce(zslot_f[:, :], (ends if cur_e is ends2 else ends2)[0:E, :], AX.X, ALU.add))
            chain.link(dve.tensor_copy(zslot[:, :], zslot_f[:, :]))
            chain.link(dve.tensor_tensor(before, before, over_b(first), ALU.add))
            chain.link(dve.scalar_tensor_tensor(before, bank[0][:, 0:ROUT].rearrange("p (b e) -> p b e", e=E), 1.0,
                                                before, ALU.add, ALU.add))
            for k in range(2):
                chain.link(dve.tensor_tensor(rt[6], before, rt[2 + k], ALU.mult))
                chain.link(dve.tensor_reduce(slot_f[:, k, :], rt[6], AX.X, ALU.add))
            dve.tensor_copy(slot[:, :, :], slot_f[:, :, :]).then_inc(route_ready, 1)

            def bias(j, par, e, half):
                dve.wait_ge(hid_done, 2 * j + half + 1)
                dve.tensor_tensor(hid[par][:, half * 512:(half + 1) * 512], bank[1 + half][:, :],
                                  b1_rep[:, e, half * 512:(half + 1) * 512], ALU.add).then_inc(hid_biased, 1)

            def rows_out(j, par):
                dve.wait_ge(y_done, j + 1)
                dve.wait_ge(y_stored[par], 8 * (j - par) + 16)
                dve.tensor_copy(ysb[par], bank[5 + par][:, 0:D]).then_inc(y_copied, 1)

            def expert_of(j):
                return dve.value_load(tile_e[0:1, bass.ds(j, 1)], min_val=0, max_val=E - 1)

            dve.wait_ge(route_ready, 1)
            dve.wait_ge(scattered, 16 * 2 * B)
            dve.wait_ge(b1_loaded, 16)
            for par in range(2):
                dve.sem_inc(y_stored[par], 16)

            def rest_xg(j, par):
                dve.wait_ge(xgT_rounded, j + 1)
                dve.tensor_tensor(xgT_lo[:, par, :, :], bank[0][:, 0:KC * P].rearrange("p (c t) -> p c t", c=KC),
                                  xgT_hi[:, par, :, :].bitcast(F32), ALU.subtract).then_inc(xgT_split, 1)

            def rest_hidden(j, par):
                for half in range(2):
                    dve.wait_ge(hidT_rounded, 2 * j + half + 1)
                    hi = hidT_hi[:, par, 4 * half:4 * half + 4, :].rearrange("p c t -> p (c t)")
                    lo = hidT_lo[:, par, 4 * half:4 * half + 4, :].rearrange("p c t -> p (c t)")
                    dve.scalar_tensor_tensor(lo, bank[3 + half][:, :], 0.0, hi.bitcast(F32), ALU.max, ALU.subtract)\
                        .then_inc(hidT_split, 1)

            def tile(j, par, ahead):
                if ahead >= 1:
                    e = expert_of(j + 1)
                    bias(j + 1, 1 - par, e, 0)
                rest_hidden(j, par)
                if ahead >= 1:
                    bias(j + 1, 1 - par, e, 1)
                if ahead >= 2:
                    rest_xg(j + 2, par)
                rows_out(j, par)

            rest_xg(0, 0)
            e0 = expert_of(0)
            for half in range(2):
                bias(0, 0, e0, half)
            rest_xg(1, 1)
            with dve.Fori(0, N_TILES // 2 - 1) as t:
                tile(2 * t, 0, 2)
                tile(2 * t + 1, 1, 2)
            tile(N_TILES - 2, 0, 1)
            tile(N_TILES - 1, 1, 0)

            dve.wait_ge(z_gathered, 16)
            dve.wait_ge(b2_loaded, 16)
            dve.tensor_tensor(dterm, yz, b2_sb, ALU.add).then_inc(c_ready, 1)
            dve.wait_ge(csum_done, 1)
            chain.link(dve.tensor_tensor(b2_sb, b2_sb, dterm, ALU.subtract))
            dve.tensor_tensor(yz, b2_sb, bank[2][0:E, 0:D], ALU.add).then_inc(dterm_ready, 1)
            for q in range(QUADS):
                dve.wait_ge(gathered[q], 16 * 8)
                if q:
                    dve.wait_ge(out_ready, q)
                for b in range(4 * q, 4 * q + 4):
                    dve.wait_ge(part_done, b + 1)
                    dve.scalar_tensor_tensor(zout[:, b % 4, :], y_all[:, 0, b, :], score[:, 0, b:b + 1],
                                             bank[3 + b % 4][:, 0:D], ALU.mult, ALU.add).then_inc(part_read, 1)
                    dve.wait_ge(part_read, b + 1)
                    chain.link(dve.scalar_tensor_tensor(zout[:, b % 4, :], y_all[:, 1, b, :], score[:, 1, b:b + 1],
                                                        zout[:, b % 4, :], ALU.mult, ALU.add))
                z_flat = zout.rearrange("p b d -> p (b d)")
                chain.link(dve.scalar_tensor_tensor(z_flat, xres[:, 4 * q:4 * q + 4, :].rearrange("p b d -> p (b d)"),
                                                    2.0, z_flat, ALU.mult, ALU.add))
                variance4(lambda b: zout[:, b, :])
                normed4(2 * QUADS + q, lambda b: zout[:, b, :], lambda b: xres[:, 4 * q + b, :]).then_inc(out_ready, 1)


_INS = ['x', 'ctx_1024', 'L0_attn_Wq', 'L0_attn_Wkv', 'L0_attn_Wo', 'L0_attn_bo', 'L0_xattn_igate_kernel',
        'L0_xattn_igate_bias', 'L0_xattn_fgate_kernel', 'L0_xattn_fgate_bias', 'L0_xattn_rms_scale',
        'L0_ffn_gamma', 'L0_ffn_beta', 'L0_ffn_Wr', 'L0_ffn_br', 'L0_ffn_W1', 'L0_ffn_b1', 'L0_ffn_W2', 'L0_ffn_b2']
_OUTS = [((16, 128, 256), 'float32')]


def kernel(**inputs):
    import numpy as _np
    import concourse.bacc as _bacc
    from concourse import mybir as _mybir
    from concourse.bass_utils import run_bass_kernel_spmd as _run

    nc = _bacc.Bacc("TRN2", target_bir_lowering=False, num_devices=1)
    arrays, args = {}, []
    for name in _INS:
        a = _np.ascontiguousarray(inputs[name])
        arrays[f"in_{name}_dram"] = a
        args.append(nc.dram_tensor(f"in_{name}_dram", a.shape, _mybir.dt.from_np(a.dtype), kind="ExternalInput").ap())
    for i, (shape, dtype) in enumerate(_OUTS):
        dt = _mybir.dt.from_np(_np.dtype(dtype))
        args.append(nc.dram_tensor(f"out_{i}_dram", shape, dt, kind="ExternalOutput").ap())
    decoder_layer(nc, *args)
    r = _run(nc, [arrays], core_ids=[0])
    got = tuple(r.results[0][f"out_{i}_dram"] for i in range(len(_OUTS)))
    return got[0]
```

```python
from contextlib import ExitStack

import concourse.bass as bass
from concourse import mybir

F32 = mybir.dt.float32
F32R = mybir.dt.float32r
I32 = mybir.dt.int32
U32 = mybir.dt.uint32
ALU = mybir.AluOpType
ACT = mybir.ActivationFunctionType
AX = mybir.AxisListType

P = 128
LN_EPS = 1e-5
MLSTM_EPS = 1e-6
RMS_EPS = 1e-6


class Chain:

    def __init__(self, eng, sem):
        self.eng, self.sem, self.base, self.k = eng, sem, 0, 0

    def start(self, base):
        self.base, self.k = base, 0

    def link(self, ins):
        self.k += 1
        ins.then_inc(self.sem, 1)
        self.eng.wait_ge(self.sem, self.base + self.k)


def decoder_layer(nc, x, ctx, wq, wkv, wo, bo, ig_w, ig_b, fg_w, fg_b, rms, gamma, beta,
                  wr, br, w1, b1, w2, b2, out):
    B, S, D = x.shape
    INNER = wq.shape[1]
    HD = 64
    NH = INNER // HD
    KC = D // P
    PAIRS = B // 2
    HG = NH // 4
    STEPS = 2 * HG
    IC = INNER // P
    SCALE = float(HD) ** -0.5
    XH = ig_w.shape[1]
    E, _, F = w1.shape
    FC = F // P
    QUADS = B // 4
    N_TILES = (2 * B * S + E + E * (P - 1)) // P
    N_SLOTS = N_TILES * P
    MAX_E_TILES = B * S // P + 1
    assert S == P and D == 2 * P and NH == 16 and XH == 4 and XH * HD == D and N_TILES % 2 == 0

    es = ExitStack()
    with es:
        def sb(name, shape, dt=F32):
            return es.enter_context(nc.sbuf_tensor(name, shape, dt))

        def sem(name):
            return es.enter_context(nc.semaphore(name))

        ident = sb("ident", [P, P])
        xres = sb("xres", [P, B, D])
        neghalf = sb("neghalf", [P, 16])
        def over(area, base, name, words):
            return nc.alloc_sbuf_tensor_at(name, [P, words], F32R, offset=base + area)

        W_WORDS = KC * F + FC * D
        arena_at = nc.sbuf_base
        arena = sb("arena", [P, 4 * W_WORDS])
        w_pair = over(0, arena_at, "w_pair", 4 * W_WORDS)[:, :].rearrange("p (z n) -> p z n", z=2)
        arena2_at = nc.sbuf_base
        arena2 = sb("arena2", [P, E * F])
        arena3_at = nc.sbuf_base
        arena3 = sb("arena3", [P, B * XH * (HD + 1)])
        hidT_hi = over(8 * F, arena3_at, "hidT_hi", 2 * F)[:, :].rearrange("p (z c t) -> p z c t", z=2, c=FC)
        work_at = nc.sbuf_base
        work = sb("work", [P, 3072])
        xgT_hi = over(16 * D, work_at, "xgT_hi", 2 * D)[:, :].rearrange("p (z c t) -> p z c t", z=2, c=KC)
        xgT_lo = over(24 * D, work_at, "xgT_lo", 2 * D)[:, :].rearrange("p (z c t) -> p z c t", z=2, c=KC)
        norms_at = nc.sbuf_base
        norms = sb("norms", [P, 2 * 4 * D + 2 * D])
        hidT_lo = over(0, norms_at, "hidT_lo", 2 * F)[:, :].rearrange("p (z c t) -> p z c t", z=2, c=FC)
        w_raw_at = nc.sbuf_base
        w_raw = sb("w_raw", [P, W_WORDS])
        wq_lo = sb("wq_lo", [P, KC, INNER], F32R)
        wo_lo = sb("wo_lo", [P, IC, D], F32R)
        wkv_lo = over(0, w_raw_at, "wkv_lo", 2 * KC * INNER)[:, :].rearrange("p (c n) -> p c n", c=KC)
        wq_hi, wkv_hi, wo_hi = (
            over(4 * at, arena_at, name, n)[:, :].rearrange("p (c n) -> p c n", c=c)
            for at, name, n, c in ((0, "wq_hi", KC * INNER, KC), (KC * INNER, "wkv_hi", 2 * KC * INNER, KC),
                                   (3 * KC * INNER, "wo_hi", IC * D, IC)))
        wq_raw = arena3[:, 0:KC * INNER].rearrange("p (c n) -> p c n", c=KC)
        wo_raw = arena3[:, KC * INNER:KC * INNER + IC * D].rearrange("p (c n) -> p c n", c=IC)
        wk_raw = work[:, 0:KC * INNER].rearrange("p (c n) -> p c n", c=KC)
        wv_raw = norms[:, 0:KC * INNER].rearrange("p (c n) -> p c n", c=KC)

        off = [0]

        def carve(area, n):
            v = area[:, off[0]:off[0] + n]
            off[0] += n
            return v

        carve(arena, 3 * KC * INNER + IC * D)
        qT = carve(arena, IC * 2 * S).rearrange("p (c t) -> p c t", c=IC)
        kT = carve(arena, IC * 2 * S).rearrange("p (c t) -> p c t", c=IC)
        v_sb = carve(arena, 2 * NH * (HD + 1)).rearrange("p (b h e) -> p b h e", b=2, h=NH)
        pT = carve(arena, 512)
        off[0] = 0
        xs = carve(arena2, 2 * D).rearrange("p (b d) -> p b d", b=2)
        xT_hi, xT_lo = (over(4 * (off[0] + k * KC * 2 * S), arena2_at, name, KC * 2 * S)[:, :]
                        .rearrange("p (c t) -> p c t", c=KC) for k, name in enumerate(("xT_hi", "xT_lo")))
        carve(arena2, 2 * KC * 2 * S)
        o_sb = carve(arena2, 2 * INNER).rearrange("p (b n) -> p b n", b=2)
        oT_hi, oT_lo = (over(4 * at, base, name, 2 * IC * S)[:, :].rearrange("p (b c t) -> p b c t", b=2, c=IC)
                        for at, base, name in ((off[0], arena2_at, "oT_hi"), (0, norms_at, "oT_lo")))
        carve(arena2, 2 * IC * S)
        probs = carve(arena2, 2 * 512).rearrange("p (u n) -> p u n", u=2)
        yln = carve(arena2, 2 * D).rearrange("p (b d) -> p b d", b=2)
        bo_rep = carve(arena2, D)

        ctx_aug = arena3[:, :].rearrange("p (b h e) -> p b h e", b=B, h=XH)
        st_all = arena2[:, :].rearrange("p (b h t) -> p b h t", b=B, h=XH)
        u_all = st_all.rearrange("p b h t -> p b (h t)")[:, :, 0:XH * (HD + 1)]
        off[0] = 0
        pairs_of = {}
        for area in (work, norms):
            off[0] = 0
            for name in ("x1s", "cs_"):
                pairs_of.setdefault(name, []).append(carve(area, 2 * D).rearrange("p (b d) -> p b d", b=2))
            for name in ("x1T", "ctxT"):
                pairs_of.setdefault(name, []).append(carve(area, KC * 2 * S).rearrange("p (c t) -> p c t", c=KC))
        x1s, cs_, x1T, ctxT = (pairs_of[name] for name in ("x1s", "cs_", "x1T", "ctxT"))
        gates = carve(work, 2 * S)[0:2 * XH, :]
        off[0] = 2048
        BH = B * XH
        gi, gf, logf, tln, cum, gdiff, gmax, ones_bh = [carve(work, S)[0:BH, :] for _ in range(8)]
        off[0] = 0
        BATCH_TILES = 6
        tiles = [carve(work, XH * S).rearrange("p (h t) -> p h t", h=XH) for _ in range(BATCH_TILES)]
        off[0] = 0
        hq = carve(norms, 4 * D)
        sq = carve(norms, 4 * D)
        gamma_rep = carve(norms, D)
        beta_rep = carve(norms, D)
        xn_all = arena3[:, 0:B * D].rearrange("p (b d) -> p b d", b=B)

        off[0] = 0
        ROUT = B * E
        rt = [carve(work, ROUT).rearrange("p (b e) -> p b e", e=E) for _ in range(8)]
        wide = carve(work, E * N_TILES)
        em8, io128, iotile, tile_f = (carve(work, n) for n in (E, MAX_E_TILES, N_TILES, N_TILES))
        rsmall = carve(work, 4 * B).rearrange("p (k b) -> p k b", b=B)
        esmall = carve(work, 4 * E).rearrange("p (k e) -> p k e", e=E)
        slot_f = carve(work, 2 * B).rearrange("p (k b) -> p k b", b=B)
        off[0] = 2560
        tri = carve(work, P)
        ones = carve(work, P)

        b1_rep = arena2[:, :].rearrange("p (e f) -> p e f", e=E)
        off[0] = 0
        xg = [carve(work, D) for _ in range(2)]
        ysb = [carve(work, D) for _ in range(2)]
        off[0] = 0
        hid = [carve(arena3, F) for _ in range(2)]
        off[0] = 0
        y_all = carve(arena, 2 * B * D).rearrange("p (k b d) -> p k b d", k=2, b=B)
        yz, b2_sb, dterm = [carve(arena, D)[0:E, :] for _ in range(3)]
        zout = carve(arena, 4 * D).rearrange("p (b d) -> p b d", b=4)

        gw = sb("gw", [P, 3 * KC, 2 * XH])
        gws = sb("gws", [P, KC, 2 * XH])
        gb = sb("gb", [2 * XH, 1])
        wr_sb = sb("wr_sb", [P, KC, E])
        br_rep = sb("br_rep", [P, E])
        rms_rep = sb("rms_rep", [P, HD])
        tok = sb("tok", [P, 2 * BH])
        g_tok, em_tok = tok[:, 0:BH], tok[:, BH:]
        xnT = sb("xnT", [P, KC, 4 * S])
        den = sb("den", [P, 16])
        rden = sb("rden", [P, 16])
        ssq = sb("ssq", [P, 16])
        rsq = sb("rsq", [P, 16])
        stats4 = sb("stats4", [P, 4, 6])
        mv4 = sb("mv4", [P, 4, 2])
        ve4 = sb("ve4", [P, 4])
        rstd4 = sb("rstd4", [P, 4])
        shift4 = sb("shift4", [P, 4])
        lg_all = sb("lg_all", [P, B, E])
        score = sb("score", [P, 2, B])
        slot = sb("slot", [P, 2, B], U32)
        tile_e = sb("tile_e", [P, N_TILES], I32)
        tile_end = sb("tile_end", [P, E], I32)
        zslot_f = sb("zslot_f", [E, 1])
        zslot = sb("zslot", [E, 1], U32)
        wgt = tok[:, :].rearrange("p (b e) -> p b e", e=E)
        off[0] = 0
        wgtT = carve(norms, B * S)[0:E, :]
        twice = tri

        gates_dram = nc.dram_tensor("gates_dram", [2 * XH, B * S], F32, kind="Internal").ap()
        gmax_dram = nc.dram_tensor("gmax_dram", [BH, S], F32, kind="Internal").ap()
        xg_dram = nc.dram_tensor("xg_dram", [N_SLOTS, D], F32, kind="Internal").ap()
        y_dram = nc.dram_tensor("y_dram", [N_SLOTS, D], F32, kind="Internal").ap()

        mx = sb("mx", [P, 2, 4])
        rsum = sb("rsum", [P, 2, 4])
        stats = sb("stats", [P, 2, 6])
        mv = sb("mv", [P, 2, 2])
        ve = sb("ve", [P, 2])
        rstd = sb("rstd", [P, 2])

        bank = [es.enter_context(nc.psum_tensor(f"bank{i}", [P, 512], F32)) for i in range(8)]
        ps_proj = bank[0:2]
        ps_score = bank[2:4]
        ps_pT = bank[4]
        ps_pv = bank[5:7]
        ps_wo = bank[7]
        wgt_banks = (bank[0], bank[1], bank[2], bank[7])
        pair_banks = ((bank[0], bank[1]), (bank[5], bank[6]))

        ident_ready = sem("ident_ready")
        x_loaded = sem("x_loaded")
        xs_loaded = sem("xs_loaded")
        wq_loaded = sem("wq_loaded")
        attn_rounded = sem("attn_rounded")
        attn_split = sem("attn_split")
        wo_rounded = sem("wo_rounded")
        wo_split = sem("wo_split")
        lo_done = sem("lo_done")
        wk_loaded = sem("wk_loaded")
        wv_loaded = sem("wv_loaded")
        wo_loaded = sem("wo_loaded")
        bo_loaded = sem("bo_loaded")
        ones_ready = sem("ones_ready")
        proj_done = sem("proj_done")
        proj_copied = sem("proj_copied")
        scores_done = sem("scores_done")
        shifted = sem("shifted")
        exp_done = sem("exp_done")
        pT_done = sem("pT_done")
        pT_copied = sem("pT_copied")
        pv_done = sem("pv_done")
        o_normed = sem("o_normed")
        wo_done = sem("wo_done")
        wo_read = sem("wo_read")
        var_ready = sem("var_ready")
        rstd_ready = sem("rstd_ready")
        x1_ready = sem("x1_ready")
        dve_step = sem("dve_step")
        stats_seen = sem("stats_seen")
        stored = sem("stored")
        zeros_ready = sem("zeros_ready")
        zeros_stored = sem("zeros_stored")
        aug_ready = sem("aug_ready")
        ctx_loaded = sem("ctx_loaded")
        small_loaded = sem("small_loaded")
        gws_ready = sem("gws_ready")
        staged = [sem(f"staged{k}") for k in range(2)]
        xT_done = sem("xT_done")
        xT_copied = sem("xT_copied")
        ctxT_done = sem("ctxT_done")
        ctxT_copied = sem("ctxT_copied")
        gates_done = sem("gates_done")
        gates_ready = sem("gates_ready")
        gates_stored = sem("gates_stored")
        st_done = sem("st_done")
        st_copied = sem("st_copied")
        gates_loaded = sem("gates_loaded")
        absf_done = sem("absf_done")
        expf_done = sem("expf_done")
        lnf_done = sem("lnf_done")
        gmax_ready = sem("gmax_ready")
        gmax_stored = sem("gmax_stored")
        gtok_done = sem("gtok_done")
        m_ready = sem("m_ready")
        em_ready = sem("em_ready")
        decay_done = sem("decay_done")
        masked = sem("masked")
        ct_done = sem("ct_done")
        u_done = sem("u_done")
        u_copied = sem("u_copied")
        tok_ready = sem("tok_ready")
        dve_seen = sem("dve_seen")
        pool_seen = sem("pool_seen")
        gamma_loaded = sem("gamma_loaded")
        sq_done = sem("sq_done")
        sumsq_ready = sem("sumsq_ready")
        rsq_ready = sem("rsq_ready")
        var4_ready = sem("var4_ready")
        rstd4_ready = sem("rstd4_ready")
        xn_ready = sem("xn_ready")
        xn_normed = sem("xn_normed")
        xn_scaled = sem("xn_scaled")
        xnT_done = sem("xnT_done")
        xnT_copied = sem("xnT_copied")
        logits_done = sem("logits_done")
        logits_read = sem("logits_read")
        route_exp_in = sem("route_exp_in")
        route_exp_out = sem("route_exp_out")
        counts_in = sem("counts_in")
        counts_out = sem("counts_out")
        route_ready = sem("route_ready")
        scattered = sem("scattered")
        b1_loaded = sem("b1_loaded")
        w_loaded = [sem(f"w{k + 1}_loaded") for k in range(2)]
        w_rounded = sem("w_rounded")
        w_split = sem("w_split")
        xgT_rounded = sem("xgT_rounded")
        xgT_split = sem("xgT_split")
        hidT_rounded = sem("hidT_rounded")
        hidT_split = sem("hidT_split")
        xgT_done = sem("xgT_done")
        hid_done = sem("hid_done")
        hid_biased = sem("hid_biased")
        hidT_done = sem("hidT_done")
        y_done = sem("y_done")
        y_copied = sem("y_copied")
        z_gathered = sem("z_gathered")
        b2_loaded = sem("b2_loaded")
        c_ready = sem("c_ready")
        csum_done = sem("csum_done")
        dterm_ready = sem("dterm_ready")
        wgtT_done = sem("wgtT_done")
        wgtT_copied = sem("wgtT_copied")
        part_done = sem("part_done")
        part_read = sem("part_read")
        out_ready = sem("out_ready")
        consts_ready = sem("consts_ready")
        tri_ready = sem("tri_ready")
        mrep_loaded = [sem(f"mrep_loaded{k}") for k in range(BATCH_TILES)]
        xg_loaded = [sem(f"xg_loaded{k}") for k in range(2)]
        y_stored = [sem(f"y_stored{k}") for k in range(2)]
        gathered = [sem(f"gathered{k}") for k in range(PAIRS)]
        shift_ready = sem("shift_ready")
        two_ready = sem("two_ready")

        def fillers(s, more):
            own = {0: ([], [("k", 2)]), 1: ([("q", 3)], [("v", 1, 0)]), 2: ([("k", 3)], [("v", 0, 1)]),
                   3: ([("v", 1, 1)], []), 4: ([("o", 0, 0)], []), 6: ([], [("o", 1, 0), ("w", 0, 0)]),
                   7: ([("o", 0, 1)], [("w", 0, 1)])}.get(s, ([], []))
            nxt = {3: ([], [("x", 0), ("x", 1)]), 4: ([], [("q", 0)]), 5: ([("k", 0)], [("q", 1)]),
                   6: ([("k", 1)], []), 7: ([("v", 0, 0)], [])}.get(s, ([], [])) if more else ([], [])
            return own[0] + nxt[0], own[1] + nxt[1]

        def tail(more):
            return [("w", 1, 0), ("o", 1, 1)] + ([("scores", 1), ("q", 2)] if more else []) + [("w", 1, 1)]

        def step(s):
            return s // 4, s // 2 % 2, s % 2

        def schedule(more):
            units = [u for s in range(STEPS) for part in fillers(s, more) for u in part] + tail(more)
            return [u for u in units if u[0] not in ("w", "scores")]

        def los(units):
            return sum(u[0] in "xo" for u in units)

        FIRST = [("x", 0), ("x", 1), ("q", 0), ("q", 1), ("k", 0), ("k", 1), ("v", 0, 0), ("q", 2)]
        N_FIRST, N_USES, N_LOS = len(FIRST), len(schedule(True)), los(schedule(True))
        assert N_USES % 2 == 0

        def ring(n):
            return ps_proj[(N_FIRST + n) % 2]

        block = es.enter_context(nc.Block())

        @block.sync
        def _(sp):
            sp.dma_start(xs[:, :, :], x[0:2].rearrange("b s d -> s b d")).then_inc(xs_loaded, 16)
            sp.dma_start(wq_raw, wq.rearrange("(c p) n -> p c n", p=P)).then_inc(wq_loaded, 16)
            wkv_v = wkv.rearrange("(c p) n -> p c n", p=P)
            sp.dma_start(wk_raw, wkv_v[:, :, 0:INNER]).then_inc(wk_loaded, 16)
            sp.dma_start(wv_raw, wkv_v[:, :, INNER:]).then_inc(wv_loaded, 16)
            sp.dma_start(wo_raw, wo.rearrange("(c p) n -> p c n", p=P)).then_inc(wo_loaded, 16)
            sp.dma_start(bo_rep[:, :], bo[None, :].broadcast_to([P, D])).then_inc(bo_loaded, 16)
            sp.dma_start(xres[:, :, :], x.rearrange("b s d -> s b d")).then_inc(x_loaded, 16)
            for w, b, r in ((ig_w, ig_b, 0), (fg_w, fg_b, XH)):
                sp.dma_start(gw[:, :, r:r + XH], w.rearrange("(c p) n -> p c n", p=P)).then_inc(small_loaded, 16)
                sp.dma_start(gb[r:r + XH, :], b[:, None]).then_inc(small_loaded, 16)
            sp.dma_start(wr_sb[:, :, :], wr.rearrange("(c p) n -> p c n", p=P)).then_inc(small_loaded, 16)
            sp.dma_start(br_rep[:, :], br[None, :].broadcast_to([P, E])).then_inc(small_loaded, 16)
            sp.dma_start(rms_rep[:, :], rms[None, :].broadcast_to([P, HD])).then_inc(small_loaded, 16)
            sp.dma_start(gamma_rep, gamma[None, :].broadcast_to([P, D])).then_inc(gamma_loaded, 16)
            sp.dma_start(beta_rep, beta[None, :].broadcast_to([P, D])).then_inc(gamma_loaded, 16)
            sp.wait_ge(proj_done, 2)
            sp.dma_start(xs[:, :, :], x[2:4].rearrange("b s d -> s b d")).then_inc(xs_loaded, 16)
            X_POS = schedule(True).index(("x", 1)) + 1
            with sp.Fori(0, PAIRS - 2) as i:
                sp.wait_ge(proj_done, N_FIRST + i * N_USES + X_POS)
                sp.dma_start(xs[:, :, :], x[bass.ds(2 * i + 4, 2)].rearrange("b s d -> s b d"))\
                    .then_inc(xs_loaded, 16)

            sp.wait_ge(zeros_ready, 1)
            ROW = N_SLOTS * D // P
            for c in range(4):
                sp.dma_start(xg_dram.rearrange("(p r) d -> p (r d)", p=P)[:, c * ROW // 4:(c + 1) * ROW // 4],
                             arena3[:, 0:ROW // 4]).then_inc(zeros_stored, 16)
            sp.wait_ge(zeros_stored, 64)
            for b in range(B):
                sp.dma_start(ctx_aug[:, b, :, 0:HD], ctx[b].rearrange("s (h e) -> s h e", h=XH))\
                    .then_inc(ctx_loaded, 16)
            sp.wait_ge(x1_ready, PAIRS)
            def stage(p, par):
                sp.dma_start(x1s[par], xres[:, bass.ds(2 * p, 2), :]).then_inc(staged[par], 16)
                sp.dma_start(cs_[par], ctx[bass.ds(2 * p, 2)].rearrange("b s d -> s b d")).then_inc(staged[par], 16)

            def store_gates(p):
                sp.wait_ge(gates_ready, p + 1)
                sp.dma_start(gates_dram[:, bass.ds(2 * S * p, 2 * S)], gates).then_inc(gates_stored, 16)

            for par in range(2):
                stage(par, par)
            sp.sem_inc(gates_stored, 16)
            with sp.Fori(0, PAIRS // 2 - 1) as t:
                for par in range(2):
                    sp.wait_ge(ctxT_done, 2 * t + par + 1)
                    stage(2 * t + par + 2, par)
                    store_gates(2 * t + par)
            for p in range(PAIRS - 2, PAIRS):
                store_gates(p)
            sp.wait_ge(gates_stored, 16 * (PAIRS + 1))
            sp.dma_start(gi, gates_dram[0:XH].rearrange("h (b t) -> (h b) t", b=B)).then_inc(gates_loaded, 16)
            sp.dma_start(gf, gates_dram[XH:].rearrange("h (b t) -> (h b) t", b=B)).then_inc(gates_loaded, 16)
            sp.wait_ge(gmax_ready, 1)
            sp.dma_start(gmax_dram, gmax).then_inc(gmax_stored, 16)
            sp.wait_ge(gmax_stored, 16)
            gm_v = gmax_dram.rearrange("(h b) t -> b h t", b=B)

            sp.wait_ge(tok_ready, 1)
            for b in range(B):
                if b >= BATCH_TILES:
                    sp.wait_ge(u_done, b - BATCH_TILES + 1)
                sp.dma_start(tiles[b % BATCH_TILES], gm_v[b][None, :, :].broadcast_to([P, XH, S]))\
                    .then_inc(mrep_loaded[b % BATCH_TILES], 16)

            sp.wait_ge(xn_ready, QUADS)
            sp.dma_start(b1_rep, b1[None, :, :].broadcast_to([P, E, F])).then_inc(b1_loaded, 16)
            sp.wait_ge(scattered, 16 * 2 * B)
            for par in range(2):
                sp.dma_start(xg[par], xg_dram[par * P:(par + 1) * P, :]).then_inc(xg_loaded[par], 16)
            for par in range(2):
                sp.wait_ge(xgT_done, par + 1)
                sp.dma_start(xg[par], xg_dram[(2 + par) * P:(3 + par) * P, :]).then_inc(xg_loaded[par], 16)

            def slots(j, par, more):
                if more:
                    sp.wait_ge(xgT_done, j + 3)
                    sp.dma_start(xg[par], xg_dram[bass.ds((j + 4) * P, P), :]).then_inc(xg_loaded[par], 16)
                sp.wait_ge(y_copied, j + 1)
                sp.dma_start(y_dram[bass.ds(j * P, P), :], ysb[par]).then_inc(y_stored[par], 16)

            with sp.Fori(0, N_TILES // 2 - 2) as t:
                for par in range(2):
                    slots(2 * t + par, par, True)
            for j in range(N_TILES - 4, N_TILES):
                slots(j, j % 2, False)

            for q in range(QUADS):
                sp.wait_ge(out_ready, 2 * q + 2)
                sp.dma_start(out[4 * q:4 * q + 4].rearrange("b s d -> s b d"), xres[:, 4 * q:4 * q + 4, :])\
                    .then_inc(stored, 16)
            sp.wait_ge(stored, 16 * QUADS)

        @block.gpsimd
        def _(pool):
            pool.memset(ident[:, :], 0.0).then_inc(ident_ready, 1)
            pool.memset(neghalf[:, :], -0.5).then_inc(ident_ready, 1)
            pool.wait_ge(ident_ready, 2)
            pool.affine_select(out=ident[:, :], in_=ident[:, :], compare_op=ALU.not_equal, fill=1.0,
                               base=0, pattern=[[-1, P]], channel_multiplier=1).then_inc(ident_ready, 1)
            pool.memset(v_sb[:, :, :, HD:HD + 1], 1.0).then_inc(ones_ready, 1)
            pool.wait_ge(wo_loaded, 16)
            pool.tensor_copy(wo_hi, wo_raw).then_inc(wo_rounded, 1)
            pool.wait_ge(wo_rounded, 1)
            pool.tensor_tensor(wo_lo[:, :, :], wo_raw, wo_hi.bitcast(F32), ALU.subtract).then_inc(wo_split, 1)
            pool.wait_ge(wo_split, 1)
            pool.wait_ge(attn_split, 3)
            pool.memset(arena3[:, 0:N_SLOTS * D // P // 4], 0.0).then_inc(zeros_ready, 1)

            def load_weights(e, part):
                if part == 0:
                    pool.dma_start(w_raw[:, 0:KC * F].rearrange("p (c f) -> p c f", c=KC),
                                   w1[bass.ds(e, 1)].rearrange("e (c p) f -> p (e c) f", p=P))\
                        .then_inc(w_loaded[0], 16)
                else:
                    pool.dma_start(w_raw[:, KC * F:].rearrange("p (c n) -> p c n", c=FC),
                                   w2[bass.ds(e, 1)].rearrange("e (c p) n -> p (e c) n", p=P))\
                        .then_inc(w_loaded[1], 16)

            def split_weights(e, z, more):
                pair = w_pair[:, z, 2 * KC * F:].rearrange("p (c k n) -> p c k n", c=FC, k=2)
                parts = ((w_raw[:, 0:KC * F], w_pair[:, z, 0:KC * F], w_pair[:, z, KC * F:2 * KC * F]),
                         (w_raw[:, KC * F:].rearrange("p (c n) -> p c n", c=FC), pair[:, :, 0, :], pair[:, :, 1, :]))
                for part, (raw, hi, lo) in enumerate(parts):
                    pool.wait_ge(w_loaded[part], 16 * e + 16)
                    pool.sem_inc(pool_seen, 1)
                    pool.tensor_copy(hi, raw).then_inc(w_rounded, 1)
                    pool.wait_ge(w_rounded, 2 * e + part + 1)
                    pool.tensor_tensor(lo, raw, hi.bitcast(F32), ALU.subtract).then_inc(w_split, 1)
                    if more:
                        pool.wait_ge(w_split, 2 * e + part + 1)
                        pool.sem_inc(pool_seen, 1)
                        load_weights(e + 1, part)

            with pool.Fori(0, PAIRS) as i:
                pool.wait_ge(var_ready, i + 1)
                pool.tensor_tensor(rstd[:, :], ve[:, :], neghalf[:, 0:2], ALU.pow).then_inc(rstd_ready, 1)

            pool.wait_ge(zeros_stored, 64)
            pool.memset(ctx_aug[:, :, :, HD:HD + 1], 1.0).then_inc(aug_ready, 1)
            pool.memset(ones_bh, 1.0).then_inc(aug_ready, 1)
            pool.wait_ge(x1_ready, PAIRS)
            for part in range(2):
                load_weights(0, part)
            for e in range(2):
                split_weights(e, e, True)

            def mask(n):
                pool.wait_ge(decay_done, n + 1)
                decay = tiles[n % BATCH_TILES]
                pool.affine_select(out=decay, in_=decay, compare_op=ALU.is_ge, fill=0.0, base=0,
                                   pattern=[[0, XH], [1, S]], channel_multiplier=-1).then_inc(masked, 1)

            def rstd_of(n):
                pool.wait_ge(var4_ready, n + 1)
                pool.tensor_tensor(rstd4[:, :], ve4[:, :], neghalf[:, 0:4], ALU.pow).then_inc(rstd4_ready, 1)

            pool.wait_ge(gamma_loaded, 32)
            for n in range(4):
                mask(n)
            for q in range(-1, QUADS):
                n = 4 * (q + 1)
                if q >= 0:
                    pool.wait_ge(sumsq_ready, q + 1)
                    pool.tensor_tensor(rsq[:, :], ssq[:, :], neghalf[:, :], ALU.pow).then_inc(rsq_ready, 1)
                if q >= 1:
                    xn4 = xn_all[:, 4 * q - 4:4 * q, :]
                    pool.wait_ge(xn_normed, q)
                    pool.tensor_tensor(xn4, xn4, gamma_rep.unsqueeze(1).broadcast_to([P, 4, D]), ALU.mult)\
                        .then_inc(xn_scaled, 1)
                    pool.wait_ge(xn_scaled, q)
                    pool.tensor_tensor(xn4, xn4, beta_rep.unsqueeze(1).broadcast_to([P, 4, D]), ALU.add)\
                        .then_inc(xn_ready, 1)
                if q >= 0:
                    rstd_of(2 * q)
                    rstd_of(2 * q + 1)
                for b in range(n + 4, min(n + 8, B)):
                    mask(b)

            pool.wait_ge(logits_read, QUADS)
            pool.iota(em8[:, :], [[1, E]], base=-E, channel_multiplier=0,
                      allow_small_or_imprecise_dtypes=True).then_inc(consts_ready, 1)
            pool.iota(io128[:, :], [[P, MAX_E_TILES]], base=0, channel_multiplier=0,
                      allow_small_or_imprecise_dtypes=True).then_inc(consts_ready, 1)
            pool.iota(iotile[:, :], [[1, N_TILES]], base=0, channel_multiplier=0,
                      allow_small_or_imprecise_dtypes=True).then_inc(consts_ready, 1)
            pool.memset(tri, 1.0).then_inc(tri_ready, 1)
            pool.memset(ones, 1.0).then_inc(tri_ready, 1)
            pool.wait_ge(tri_ready, 2)
            pool.affine_select(out=tri, in_=tri, compare_op=ALU.is_gt, fill=0.0, base=0, pattern=[[1, P]],
                               channel_multiplier=-1).then_inc(tri_ready, 1)

            pool.wait_ge(route_ready, 1)
            for b in range(B):
                for k in range(2):
                    pool.indirect_dma_start(xg_dram, bass.IndirectOffsetOnAxis(ap=slot[:, k, b:b + 1], axis=0),
                                            xn_all[:, b, :], None).then_inc(scattered, 16)

            def next_weights(e, z, more):
                pool.wait_ge(y_done, pool.value_load(tile_end[0:1, bass.ds(e - 2, 1)], min_val=1, max_val=N_TILES))
                split_weights(e, z, more)

            with pool.Fori(1, E // 2 - 1) as t:
                for z in range(2):
                    next_weights(2 * t + z, z, True)
            next_weights(E - 2, 0, True)
            next_weights(E - 1, 1, False)

            for par in range(2):
                pool.wait_ge(y_stored[par], 16 * (N_TILES // 2 + 1))
            pool.indirect_dma_start(yz, None, y_dram, bass.IndirectOffsetOnAxis(ap=zslot[:, 0:1], axis=0))\
                .then_inc(z_gathered, 16)
            for b in range(B):
                if b % 4 == 0 and b >= 8:
                    rstd_of(2 * QUADS + b // 4 - 2)
                for k in range(2):
                    pool.indirect_dma_start(y_all[:, k, b, :], None, y_dram,
                                            bass.IndirectOffsetOnAxis(ap=slot[:, k, b:b + 1], axis=0))\
                        .then_inc(gathered[b // 2], 16)
            for q in range(2, QUADS):
                rstd_of(2 * QUADS + q)

        @block.tensor
        def _(pe):
            def three(out, l_hi, l_lo, r_hi, r_lo, start, stop):
                pe.matmul(out, l_hi, r_hi, start=start, stop=False)
                pe.matmul(out, l_hi, r_lo, start=False, stop=False)
                return pe.matmul(out, l_lo, r_hi, start=False, stop=stop)

            def unit(dst, kind, *a):
                if kind == "x":
                    for c in range(KC):
                        last = pe.transpose(dst[:, c * P:(c + 1) * P], xs[:, a[0], c * P:(c + 1) * P], ident[:, :])
                elif kind in "qk":
                    g, = a
                    hi, lo = (wq_hi, wq_lo) if kind == "q" else (wkv_hi, wkv_lo)
                    for j in range(2):
                        n = slice((2 * g + j) * P, (2 * g + j + 1) * P)
                        for c in range(KC):
                            last = three(dst[:, j * 2 * S:(j + 1) * 2 * S], hi[:, c, n], lo[:, c, n],
                                         xT_hi[:, c, :], xT_lo[:, c, :], c == 0, c == KC - 1)
                elif kind == "v":
                    b, half = a
                    t, n = slice(b * S, (b + 1) * S), slice(INNER + half * 512, INNER + (half + 1) * 512)
                    for c in range(KC):
                        last = three(dst[:, :], xT_hi[:, c, t], xT_lo[:, c, t], wkv_hi[:, c, n], wkv_lo[:, c, n],
                                     c == 0, c == KC - 1)
                else:
                    b, half = a
                    for c in range(4):
                        last = pe.transpose(dst[:, c * P:(c + 1) * P],
                                            o_sb[:, b, (4 * half + c) * P:(4 * half + c + 1) * P], ident[:, :])
                last.then_inc(proj_done, 1)

            def scores(s):
                half, b, odd = step(s)
                r = HD * odd
                for h in range(4):
                    ch = 4 * half + h
                    last = pe.matmul(ps_score[s % 2][:, h * S:(h + 1) * S],
                                     qT[r:r + HD, ch, b * S:(b + 1) * S],
                                     kT[r:r + HD, ch, b * S:(b + 1) * S], start=True, stop=True)
                last.then_inc(scores_done, 1)

            def pair(i, more):
                base = N_FIRST + i * N_USES
                lo_base = 2 + i * N_LOS
                units = schedule(more)
                at = [0]

                def run(part):
                    for u in part:
                        if u[0] == "scores":
                            scores(u[1])
                            continue
                        if u[0] == "w":
                            b, half = u[1:]
                            pe.wait_ge(lo_done, lo_base + los(units[:units.index(("o", b, half)) + 1]))
                            if half == 0:
                                pe.wait_ge(wo_read, 2 * i + b + 1)
                            for c in range(4 * half, 4 * half + 4):
                                last = three(ps_wo[:, 0:D], oT_hi[:, b, c, :], oT_lo[:, b, c, :],
                                             wo_hi[:, c, :], wo_lo[:, c, :], c == 0, c == IC - 1)
                            if half == 1:
                                last.then_inc(wo_done, 1)
                            continue
                        n = at[0]
                        at[0] += 1
                        pe.wait_ge(proj_copied, base + n - 1)
                        if n >= 2 and units[n - 2][0] in "xo":
                            pe.wait_ge(lo_done, lo_base + los(units[:n - 1]))
                        if u[0] == "o":
                            b, half = u[1:]
                            pe.wait_ge(o_normed, i * STEPS + 4 * half + 2 * b + 2)
                        if u == ("x", 0):
                            pe.wait_ge(xs_loaded, (i + 2) * 16)
                        if u == ("q", 0):
                            pe.wait_ge(lo_done, lo_base + los(units[:units.index(("x", 1)) + 1]))
                        unit(ring(n), *u)

                def copied(u):
                    pe.wait_ge(proj_copied, base + units.index(u) + 1)

                for s in range(STEPS):
                    half, b, odd = step(s)
                    if s + 1 == STEPS // 2:
                        copied(("k", 3))
                    if 1 < s + 1 < STEPS:
                        scores(s + 1)
                    elif s + 1 == STEPS and more:
                        copied(("k", 1))
                        scores(0)
                    before, after = fillers(s, more)
                    run(before)
                    pe.wait_ge(exp_done, i * STEPS + s + 1)
                    for h in range(4):
                        last = pe.transpose(ps_pT[:, h * S:(h + 1) * S], probs[:, s % 2, h * S:(h + 1) * S],
                                            ident[:, :])
                    last.then_inc(pT_done, 1)
                    run(after)
                    if s == 0:
                        pe.wait_ge(proj_copied, base)
                    elif s % 2 == 0:
                        copied(("v", b, half))
                    pe.wait_ge(pT_copied, i * STEPS + s + 1)
                    for h in range(4):
                        last = pe.matmul(ps_pv[s % 2][:, h * (HD + 1):(h + 1) * (HD + 1)], pT[:, h * S:(h + 1) * S],
                                         v_sb[:, b, 8 * half + 2 * h + odd, :], start=True, stop=True)
                    last.then_inc(pv_done, 1)
                run(tail(more))

            pe.wait_ge(ident_ready, 3)
            pe.wait_ge(xs_loaded, 16)
            for n, u in enumerate(FIRST):
                if n >= 2:
                    pe.wait_ge(proj_copied, n - 1)
                    pe.wait_ge(lo_done, 2)
                if u in (("q", 0), ("k", 0), ("v", 0, 0)):
                    pe.wait_ge(attn_split, "qkv".index(u[0]) + 1)
                unit(ps_proj[n % 2], *u)
            pe.wait_ge(proj_copied, N_FIRST)
            pe.wait_ge(ones_ready, 1)
            scores(0)
            scores(1)
            pe.wait_ge(wo_split, 1)
            with pe.Fori(0, PAIRS - 1) as i:
                pair(i, True)
            pair(PAIRS - 1, False)

            pe.wait_ge(gws_ready, 1)
            def transposes(p, par):
                pe.wait_ge(staged[par], 16 * (p - par) + 32)
                for src, bk, done in zip((x1s[par], cs_[par]), pair_banks[par], (xT_done, ctxT_done)):
                    for c in range(KC):
                        for b in range(2):
                            last = pe.transpose(bk[:, (2 * c + b) * P:(2 * c + b + 1) * P],
                                                src[:, b, c * P:(c + 1) * P], ident[:, :])
                    last.then_inc(done, 1)

            def gates_and_scores(p, par):
                pe.wait_ge(st_copied, 2 * p + 2)
                pe.wait_ge(xT_copied, p + 1)
                pe.wait_ge(ctxT_copied, p + 1)
                for c in range(KC):
                    pe.matmul(bank[2][0:2 * XH, 0:2 * S], gw[:, c, :], x1T[par][:, c, :], start=c == 0, stop=False)
                for c in range(KC):
                    last = pe.matmul(bank[2][0:2 * XH, 0:2 * S], gws[:, c, :], ctxT[par][:, c, :],
                                     start=False, stop=c == KC - 1)
                last.then_inc(gates_done, 1)
                for b in range(2):
                    for h in range(XH):
                        odd, c = h % 2, h // 2
                        r = HD * odd
                        last = pe.matmul(bank[3 + odd][:, (2 * b + c) * S:(2 * b + c + 1) * S],
                                         ctxT[par][r:r + HD, c, b * S:(b + 1) * S],
                                         x1T[par][r:r + HD, c, b * S:(b + 1) * S], start=True, stop=True)
                last.then_inc(st_done, 1)

            transposes(0, 0)
            with pe.Fori(0, PAIRS // 2 - 1) as t:
                for par in range(2):
                    transposes(2 * t + par + 1, 1 - par)
                    gates_and_scores(2 * t + par, par)
            transposes(PAIRS - 1, 1)
            for par in range(2):
                gates_and_scores(PAIRS - 2 + par, par)
            pe.wait_ge(em_ready, 1)
            pe.transpose(bank[5][:, 0:BH], gdiff, ident[0:BH, 0:BH])
            pe.transpose(bank[6][:, 0:BH], tln, ident[0:BH, 0:BH]).then_inc(gtok_done, 1)
            pe.wait_ge(ctx_loaded, 16 * B)
            pe.wait_ge(aug_ready, 2)

            def weighted(n):
                pe.wait_ge(ct_done, n + 1)
                if n >= 2:
                    pe.wait_ge(u_copied, n - 1)
                for h in range(XH):
                    last = pe.matmul(bank[n % 2][:, h * (HD + 1):(h + 1) * (HD + 1)], tiles[n % BATCH_TILES][:, h, :],
                                     ctx_aug[:, n, h, :], start=True, stop=True)
                last.then_inc(u_done, 1)

            def xn_transposes(q):
                pe.wait_ge(xn_ready, q + 1)
                for c in range(KC):
                    for b in range(4):
                        last = pe.transpose(bank[2 + c][:, b * S:(b + 1) * S], xn_all[:, 4 * q + b, c * P:(c + 1) * P],
                                            ident[:, :])
                last.then_inc(xnT_done, 1)

            def logits(q):
                pe.wait_ge(xnT_copied, q + 1)
                for b in range(4):
                    for c in range(KC):
                        last = pe.matmul(bank[4][:, b * E:(b + 1) * E], xnT[:, c, b * S:(b + 1) * S], wr_sb[:, c, :],
                                         start=c == 0, stop=c == KC - 1)
                last.then_inc(logits_done, 1)

            for q in range(-1, QUADS):
                n = 4 * (q + 1)
                for b in range(n, min(n + 4, B)):
                    weighted(b)
                if q >= 1:
                    xn_transposes(q - 1)
                    logits(q - 1)
            xn_transposes(QUADS - 1)
            logits(QUADS - 1)

            pe.wait_ge(counts_in, 1)
            pe.wait_ge(tri_ready, 3)
            chosen = rt[7].rearrange("p b e -> p (b e)")
            pe.matmul(bank[0][:, 0:ROUT], tri, chosen, start=True, stop=True)
            pe.matmul(bank[1][:, 0:ROUT], ones, chosen, start=True, stop=True).then_inc(counts_out, 1)

            def slot_transposes(j, par):
                pe.wait_ge(xg_loaded[par], 8 * (j - par) + 16)
                for c in range(KC):
                    last = pe.transpose(bank[0][:, c * P:(c + 1) * P], xg[par][:, c * P:(c + 1) * P], ident[:, :])
                last.then_inc(xgT_done, 1)

            def hidden(j, par, half, e):
                if half == 0:
                    pe.wait_ge(xgT_split, j + 1)
                    pe.wait_ge(w_split, 2 * e + 1)
                if not isinstance(j, int) or j > 0:
                    pe.wait_ge(hid_biased, 2 * j + half - 1)
                z = e % 2
                for c in range(KC):
                    f = c * F + half * 512
                    hi, lo = w_pair[:, z, f:f + 512], w_pair[:, z, KC * F + f:KC * F + f + 512]
                    pe.matmul(bank[1 + half][:, :], xgT_hi[:, par, c, :], hi, start=c == 0, stop=False)
                    pe.matmul(bank[1 + half][:, :], xgT_hi[:, par, c, :], lo, start=False, stop=False)
                    last = pe.matmul(bank[1 + half][:, :], xgT_lo[:, par, c, :], hi, start=False, stop=c == KC - 1)
                last.then_inc(hid_done, 1)

            def hidden_transposes(j, par):
                for half in range(2):
                    pe.wait_ge(hid_biased, 2 * j + half + 1)
                    for c in range(4):
                        f = (4 * half + c) * P
                        last = pe.transpose(bank[3 + half][:, c * P:(c + 1) * P], hid[par][:, f:f + P], ident[:, :])
                    last.then_inc(hidT_done, 1)

            def expert_out(j, par, e):
                z = e % 2
                y = bank[5 + par]
                pe.wait_ge(w_split, 2 * e + 2)
                for half in range(2):
                    pe.wait_ge(hidT_split, 2 * j + half + 1)
                    for c in range(4 * half, 4 * half + 4):
                        f = 2 * KC * F + 2 * c * D
                        both = (hidT_hi[:, par, c, :], w_pair[:, z, f:f + 2 * D], y[:, 0:2 * D])
                        one = (hidT_lo[:, par, c, :], w_pair[:, z, f:f + D], y[:, 0:D])
                        for l, r, o in ((both, one) if c < FC - 1 else (one, both)):
                            last = pe.matmul(o, l, r, start=c == 0 and l is both[0], stop=c == FC - 1 and l is both[0])
                last.then_inc(y_done, 1)

            def expert_of(j):
                return pe.value_load(tile_e[0:1, bass.ds(j, 1)], min_val=0, max_val=E - 1)

            def tile(j, par, ahead, e, e_next):
                if ahead >= 1:
                    hidden(j + 1, 1 - par, 0, e_next)
                hidden_transposes(j, par)
                if ahead >= 1:
                    hidden(j + 1, 1 - par, 1, e_next)
                if ahead >= 2:
                    pe.wait_ge(xgT_split, j + 2)
                    slot_transposes(j + 2, par)
                expert_out(j, par, e)

            pe.wait_ge(route_ready, 1)
            slot_transposes(0, 0)
            e0 = expert_of(0)
            for half in range(2):
                hidden(0, 0, half, e0)
            slot_transposes(1, 1)
            with pe.Fori(0, N_TILES // 2 - 1) as t:
                e0, e1, e2 = (expert_of(2 * t + k) for k in range(3))
                tile(2 * t, 0, 2, e0, e1)
                tile(2 * t + 1, 1, 2, e1, e2)
            e0, e1 = expert_of(N_TILES - 2), expert_of(N_TILES - 1)
            tile(N_TILES - 2, 0, 1, e0, e1)
            tile(N_TILES - 1, 1, 0, e1, None)

            for g in range(QUADS):
                for b in range(4):
                    last = pe.transpose(wgt_banks[g][0:E, b * S:(b + 1) * S], wgt[:, 4 * g + b, :], ident[:, :])
                last.then_inc(wgtT_done, 1)
            def input_twice(b):
                pe.matmul(bank[3 + b % 4][:, 0:D], twice, xres[:, b, :], start=True, stop=False)

            def choices(b):
                pe.matmul(bank[3 + b % 4][:, 0:D], wgtT[:, b * S:(b + 1) * S], yz, start=False, stop=True)\
                    .then_inc(part_done, 1)

            pe.wait_ge(two_ready, 1)
            pe.wait_ge(y_copied, N_TILES)
            for b in range(4):
                input_twice(b)
            pe.wait_ge(wgtT_copied, QUADS)
            pe.wait_ge(c_ready, 1)
            pe.matmul(bank[2][0:E, 0:D], ones[0:E, 0:E], dterm, start=True, stop=True).then_inc(csum_done, 1)
            pe.wait_ge(dterm_ready, 1)
            for b in range(4):
                choices(b)
            for b in range(4, B):
                pe.wait_ge(part_read, b - 3)
                input_twice(b)
                choices(b)

        @block.scalar
        def _(act):
            def copy_unit(n, src, kind, *a):
                act.wait_ge(proj_done, n + 1)
                if kind == "x":
                    o, i_ = xT_hi[:, :, a[0] * S:(a[0] + 1) * S], src[:, 0:KC * P].rearrange("p (c t) -> p c t", c=KC)
                elif kind in "qk":
                    o = (qT if kind == "q" else kT)[:, 2 * a[0]:2 * a[0] + 2, :]
                    i_ = src[:, :].rearrange("p (c t) -> p c t", c=2)
                elif kind == "v":
                    o = v_sb[:, a[0], 8 * a[1]:8 * a[1] + 8, 0:HD]
                    i_ = src[:, :].rearrange("p (h e) -> p h e", h=8)
                else:
                    o = oT_hi[:, a[0], 4 * a[1]:4 * a[1] + 4, :]
                    i_ = src[:, :].rearrange("p (c t) -> p c t", c=4)
                nc.scalar.copy(o, i_).then_inc(proj_copied, 1)

            def exponentials(n, s):
                act.wait_ge(shifted, n + 1)
                nc.scalar.activation(probs[:, s % 2, :], probs[:, s % 2, :], ACT.Exp, scale=SCALE).then_inc(exp_done, 1)

            rounds = {("q", 0): [(wq_loaded, wq_hi, wq_raw), (wk_loaded, wkv_hi[:, :, 0:INNER], wk_raw)],
                      ("k", 0): [(wv_loaded, wkv_hi[:, :, INNER:], wv_raw)]}
            for n, u in enumerate(FIRST):
                for loaded, hi, raw in rounds.get(u, []):
                    act.wait_ge(loaded, 16)
                    nc.scalar.copy(hi, raw).then_inc(attn_rounded, 1)
                copy_unit(n, ps_proj[n % 2], *u)
            exponentials(0, 0)

            def pair(i, more):
                k = 0
                for s in range(STEPS):
                    before, after = fillers(s, more)
                    for part in (before, after):
                        for u in part:
                            if u[0] != "w":
                                copy_unit(N_FIRST + i * N_USES + k, ring(k), *u)
                                k += 1
                        if part is before:
                            act.wait_ge(pT_done, i * STEPS + s + 1)
                            nc.scalar.copy(pT, ps_pT[:, :]).then_inc(pT_copied, 1)
                            if s + 1 < STEPS or more:
                                exponentials(i * STEPS + s + 1, (s + 1) % STEPS)
                for u in tail(more):
                    if u[0] not in ("w", "scores"):
                        copy_unit(N_FIRST + i * N_USES + k, ring(k), *u)
                        k += 1

            with act.Fori(0, PAIRS - 1) as i:
                pair(i, True)
            pair(PAIRS - 1, False)

            with act.Fori(0, PAIRS // 2) as t:
                for par in range(2):
                    for to, bk, done, copied in ((x1T[par], pair_banks[par][0], xT_done, xT_copied),
                                                 (ctxT[par], pair_banks[par][1], ctxT_done, ctxT_copied)):
                        act.wait_ge(done, 2 * t + par + 1)
                        nc.scalar.copy(to, bk[:, :].rearrange("p (c t) -> p c t", c=KC)).then_inc(copied, 1)

            act.wait_ge(absf_done, 1)
            nc.scalar.activation(tln, logf, ACT.Exp).then_inc(expf_done, 1)
            act.wait_ge(expf_done, 1)
            nc.scalar.activation(tln, tln, ACT.Ln, bias=1.0).then_inc(lnf_done, 1)
            act.wait_ge(m_ready, 1)
            nc.scalar.activation(tln, logf, ACT.Exp, scale=-1.0).then_inc(em_ready, 1)

            act.wait_ge(tok_ready, 1)
            def decays(n):
                act.wait_ge(mrep_loaded[n % BATCH_TILES], 16 * (n // BATCH_TILES) + 16)
                tile = tiles[n % BATCH_TILES]
                for h in range(XH):
                    last = nc.scalar.activation(tile[:, h, :], tile[:, h, :], ACT.Exp,
                                                bias=g_tok[:, h * B + n:h * B + n + 1], scale=-1.0)
                last.then_inc(decay_done, 1)

            def router_copies(q):
                act.wait_ge(xnT_done, q + 1)
                for c in range(KC):
                    last = nc.scalar.copy(xnT[:, c, :], bank[2 + c][:, :])
                last.then_inc(xnT_copied, 1)
                act.wait_ge(logits_done, q + 1)
                nc.scalar.copy(lg_all[:, 4 * q:4 * q + 4, :], bank[4][:, 0:4 * E].rearrange("p (b e) -> p b e", b=4))\
                    .then_inc(logits_read, 1)

            def keep_u(n):
                act.wait_ge(u_done, n + 1)
                nc.scalar.copy(u_all[:, n, :], bank[n % 2][:, 0:XH * (HD + 1)]).then_inc(u_copied, 1)

            def squares(q):
                act.wait_ge(u_copied, 4 * q + 4)
                if q >= 1:
                    act.wait_ge(sumsq_ready, q)
                u4 = u_all[:, 4 * q:4 * q + 4, :].rearrange("p b (h e) -> p b h e", h=XH)
                nc.scalar.activation(sq.rearrange("p (b h e) -> p b h e", b=4, h=XH), u4[:, :, :, 0:HD], ACT.Square)\
                    .then_inc(sq_done, 1)

            for n in range(BATCH_TILES):
                decays(n)
            for q in range(-1, QUADS):
                n = 4 * (q + 1)
                if n < B:
                    for b in range(n, n + 4):
                        keep_u(b)
                    squares(q + 1)
                if q >= 1:
                    router_copies(q - 1)
                for b in range(n + BATCH_TILES, min(n + BATCH_TILES + 4, B)):
                    decays(b)
            router_copies(QUADS - 1)
            act.wait_ge(route_exp_in, 1)
            nc.scalar.activation(rt[1], rt[0], ACT.Exp).then_inc(route_exp_out, 1)

            def round_xg(j, par):
                act.wait_ge(xgT_done, j + 1)
                nc.scalar.copy(xgT_hi[:, par, :, :], bank[0][:, 0:KC * P].rearrange("p (c t) -> p c t", c=KC))\
                    .then_inc(xgT_rounded, 1)

            def relu(j, par):
                for half in range(2):
                    act.wait_ge(hidT_done, 2 * j + half + 1)
                    nc.scalar.activation(hidT_hi[:, par, 4 * half:4 * half + 4, :],
                                         bank[3 + half][:, :].rearrange("p (c t) -> p c t", c=4), ACT.Relu)\
                        .then_inc(hidT_rounded, 1)

            act.wait_ge(counts_out, 1)
            nc.scalar.activation(twice, ident[:, :], ACT.Copy, scale=2.0).then_inc(two_ready, 1)
            act.wait_ge(scattered, 16 * 2 * B)
            round_xg(0, 0)
            round_xg(1, 1)
            with act.Fori(0, N_TILES // 2 - 1) as t:
                for par in range(2):
                    relu(2 * t + par, par)
                    round_xg(2 * t + par + 2, par)
            relu(N_TILES - 2, 0)
            relu(N_TILES - 1, 1)
            act.wait_ge(y_done, N_TILES)
            act.dma_start(b2_sb, b2).then_inc(b2_loaded, 16)
            for g in range(QUADS):
                act.wait_ge(wgtT_done, g + 1)
                nc.scalar.copy(wgtT[:, 4 * g * S:4 * (g + 1) * S], wgt_banks[g][0:E, :]).then_inc(wgtT_copied, 1)
            for q in range(QUADS):
                act.wait_ge(shift_ready, q + 1)
                for b in (1, 3):
                    last = nc.scalar.activation(xres[:, 4 * q + b, :], zout[:, b, :], ACT.Identity,
                                                bias=shift4[:, b:b + 1], scale=rstd4[:, b:b + 1])
                last.then_inc(out_ready, 1)

        @block.vector
        def _(dve):
            chain = Chain(dve, dve_step)

            def soften(n, s):
                dve.wait_ge(scores_done, n + 1)
                sc = ps_score[s % 2][:, :].rearrange("p (h t) -> p h t", h=4)
                chain.link(nc.vector.tensor_reduce(mx[:, s % 2, :], sc, AX.X, ALU.max))
                m = mx[:, s % 2, :].unsqueeze(2).broadcast_to([P, 4, S])
                nc.vector.tensor_tensor(probs[:, s % 2, :].rearrange("p (h t) -> p h t", h=4), sc, m,
                                        ALU.subtract).then_inc(shifted, 1)

            def norm(n, s):
                half, b, odd = step(s)
                dve.wait_ge(pv_done, n + 1)
                pv = ps_pv[s % 2][:, 0:4 * (HD + 1)].rearrange("p (h e) -> p h e", h=4)
                chain.link(nc.vector.reciprocal(rsum[:, s % 2, :], pv[:, :, HD]))
                r = rsum[:, s % 2, :].unsqueeze(2).broadcast_to([P, 4, HD])
                o = o_sb[:, b, half * 512:(half + 1) * 512].rearrange("p (h z e) -> p h z e", h=4, z=2)[:, :, odd, :]
                nc.vector.tensor_tensor(o, pv[:, :, 0:HD], r, ALU.mult).then_inc(o_normed, 1)

            def rest(n, src, kind, *a):
                dve.wait_ge(proj_copied, n + 1)
                if kind == "x":
                    hi, lo = (t[:, :, a[0] * S:(a[0] + 1) * S] for t in (xT_hi, xT_lo))
                    i_ = src[:, 0:KC * P].rearrange("p (c t) -> p c t", c=KC)
                else:
                    hi, lo = (t[:, a[0], 4 * a[1]:4 * a[1] + 4, :] for t in (oT_hi, oT_lo))
                    i_ = src[:, :].rearrange("p (c t) -> p c t", c=4)
                dve.tensor_tensor(lo, i_, hi.bitcast(F32), ALU.subtract).then_inc(lo_done, 1)

            def read_wo(i, b):
                dve.wait_ge(wo_done, 2 * i + b + 1)
                nc.vector.tensor_tensor(yln[:, b, :], ps_wo[:, 0:D], bo_rep[:, :], ALU.add).then_inc(wo_read, 1)

            def moments(i, b):
                dve.wait_ge(wo_read, 2 * i + b + 2)
                chain.link(nc.vector.tensor_tensor(yln[:, b, :], yln[:, b, :], xres[:, 2 * i + b, :], ALU.add))
                chain.link(nc.vector.bn_stats(stats[:, b, :], yln[:, b, :]))
                dve.sem_inc(stats_seen, 1)
                chain.link(nc.vector.bn_aggr(mv[:, b, :], stats[:, b, :]))

            def normalise(i):
                nc.vector.tensor_scalar(ve[:, :], mv[:, :, 1], LN_EPS, None, ALU.add).then_inc(var_ready, 1)
                dve.wait_ge(rstd_ready, i + 1)
                for b in range(2):
                    last = nc.vector.tensor_scalar(xres[:, 2 * i + b, :], yln[:, b, :], mv[:, b, 0:1],
                                                   rstd[:, b:b + 1], ALU.subtract, ALU.mult)
                last.then_inc(x1_ready, 1)

            PER = 2 * STEPS + 6
            dve.sem_inc(wo_read, 1)
            attn_w = ((wq_hi, wq_lo[:, :, :], wq_raw), (wkv_hi[:, :, 0:INNER], wkv_lo[:, :, 0:INNER], wk_raw),
                      (wkv_hi[:, :, INNER:], wkv_lo[:, :, INNER:], wv_raw))
            for b in range(2):
                rest(b, ps_proj[b], "x", b)
            for k, (hi, lo, raw) in enumerate(attn_w):
                dve.wait_ge(attn_rounded, k + 1)
                dve.tensor_tensor(lo, raw, hi.bitcast(F32), ALU.subtract).then_inc(attn_split, 1)
            soften(0, 0)

            def finish(i):
                for b in range(2):
                    moments(i - 1, b)
                normalise(i - 1)

            def pair(i, first, more):
                chain.start(1 + (i * PER - (0 if first else 6)))
                n = N_FIRST + i * N_USES
                k = 0
                for s in range(STEPS):
                    if s + 1 < STEPS or more:
                        soften(i * STEPS + s + 1, (s + 1) % STEPS)
                    if s == 0 and not first:
                        finish(i)
                    for part in fillers(s, more):
                        for u in part:
                            if u[0] in "xo":
                                rest(n + k, ring(k), *u)
                            k += u[0] != "w"
                    if s + 1 == STEPS:
                        read_wo(i, 0)
                    norm(i * STEPS + s, s)
                rest(n + k, ring(k), "o", 1, 1)
                read_wo(i, 1)
                assert chain.k == 2 * STEPS - (not more) + (0 if first else 6)

            dve.wait_ge(bo_loaded, 16)
            dve.wait_ge(x_loaded, 16)
            pair(0, True, True)
            with dve.Fori(1, PAIRS - 1) as i:
                pair(i, False, True)
            pair(PAIRS - 1, False, False)
            chain.start(PAIRS * PER - 6)
            finish(PAIRS)

            dve.wait_ge(small_loaded, 16 * 7)
            dve.tensor_tensor(gws[:, :, :], gw[:, KC:2 * KC, :], gw[:, 2 * KC:3 * KC, :], ALU.add)\
                .then_inc(gws_ready, 1)
            dve.sem_inc(st_copied, 2)
            with dve.Fori(0, PAIRS) as i:
                dve.wait_ge(gates_done, i + 1)
                dve.wait_ge(gates_stored, 16 * i + 16)
                dve.tensor_scalar(gates, bank[2][0:2 * XH, 0:2 * S], gb[:, 0:1], None, ALU.add).then_inc(gates_ready, 1)
                dve.wait_ge(st_done, i + 1)
                dve.sem_inc(dve_seen, 1)
                for odd in range(2):
                    dst = st_all[:, bass.ds(2 * i, 2), :, :].rearrange("p b (c z) t -> p b c z t", z=2)[:, :, :, odd, :]
                    dve.tensor_copy(dst, bank[3 + odd][:, :].rearrange("p (b c t) -> p b c t", b=2, c=2))\
                        .then_inc(st_copied, 1)

            chain.start(PAIRS * PER)
            dve.wait_ge(gates_loaded, 32)
            chain.link(dve.tensor_scalar(logf, gf, -1.0, None, ALU.mult))
            dve.tensor_tensor(logf, logf, gf, ALU.min).then_inc(absf_done, 1)
            chain.link(dve.tensor_scalar(gf, gf, 0.0, None, ALU.min))
            dve.wait_ge(lnf_done, 1)
            chain.link(dve.tensor_tensor(logf, gf, tln, ALU.subtract))
            dve.wait_ge(aug_ready, 2)
            chain.link(dve.tensor_tensor_scan(cum, ones_bh, logf, 0.0, ALU.mult, ALU.add))
            chain.link(dve.tensor_tensor(gdiff, gi, cum, ALU.subtract))
            dve.tensor_tensor_scan(gmax, ones_bh, gdiff, -3.0e38, ALU.mult, ALU.max).then_inc(gmax_ready, 1)
            dve.wait_ge(gmax_ready, 1)
            dve.tensor_tensor(logf, cum, gmax, ALU.add).then_inc(m_ready, 1)
            dve.wait_ge(gtok_done, 1)
            chain.link(dve.tensor_copy(g_tok[:, :], bank[5][:, 0:BH]))
            dve.wait_ge(gmax_stored, 16)
            dve.tensor_copy(em_tok[:, :], bank[6][:, 0:BH]).then_inc(tok_ready, 1)

            chain.link(dve.tensor_scalar(rms_rep[:, :], rms_rep[:, :], 1.0, None, ALU.add))
            rms1 = rms_rep[:, :].unsqueeze(1).broadcast_to([P, 16, HD])

            def weigh(n):
                dve.wait_ge(masked, n + 1)
                tile = tiles[n % BATCH_TILES]
                dve.scalar_tensor_tensor(tile, st_all[:, n, :, :], float(HD) ** -0.5, tile, ALU.mult, ALU.mult)\
                    .then_inc(ct_done, 1)

            def variance4(of):
                for b in range(4):
                    last = dve.bn_stats(stats4[:, b, :], of(b))
                chain.link(last)
                for b in range(4):
                    last = dve.bn_aggr(mv4[:, b, :], stats4[:, b, :])
                chain.link(last)
                dve.tensor_scalar(ve4[:, :], mv4[:, :, 1], LN_EPS, None, ALU.add).then_inc(var4_ready, 1)

            def normed4(n, of, to):
                dve.wait_ge(rstd4_ready, n + 1)
                for b in range(4):
                    last = dve.tensor_scalar(to(b), of(b), mv4[:, b, 0:1], rstd4[:, b:b + 1], ALU.subtract, ALU.mult)
                return last

            h4 = hq.rearrange("p (n e) -> p n e", e=HD)
            hb = hq.rearrange("p (b d) -> p b d", b=4)
            for q in range(-1, QUADS):
                n = 4 * (q + 1)
                four = slice(4 * q, 4 * q + 4)
                if q >= 0:
                    dve.wait_ge(u_copied, 4 * q + 4)
                    u4 = u_all[:, four, :].rearrange("p b (h e) -> p b h e", h=XH)
                    em4 = em_tok[:, :].rearrange("p (h b) -> p b h", b=B)[:, four, :]
                    d4 = den[:, :].rearrange("p (b h) -> p b h", b=4)
                    chain.link(dve.tensor_tensor(d4, u4[:, :, :, HD], em4, ALU.max))
                    chain.link(dve.tensor_scalar(den[:, :], den[:, :], MLSTM_EPS, None, ALU.add))
                    chain.link(dve.reciprocal(rden[:, :], den[:, :]))
                    dve.wait_ge(sq_done, q + 1)
                    chain.link(dve.tensor_reduce(ssq[:, :], sq.rearrange("p (n e) -> p n e", e=HD), AX.X, ALU.add))
                    chain.link(dve.scalar_tensor_tensor(ssq[:, :], ssq[:, :], 1.0 / HD, rden[:, :], ALU.mult, ALU.mult))
                    chain.link(dve.tensor_tensor(ssq[:, :], ssq[:, :], rden[:, :], ALU.mult))
                    dve.tensor_scalar(ssq[:, :], ssq[:, :], RMS_EPS, None, ALU.add).then_inc(sumsq_ready, 1)
                if n < B:
                    weigh(n)
                    weigh(n + 1)
                    weigh(n + 2)
                if q >= 0:
                    dve.wait_ge(rsq_ready, q + 1)
                    chain.link(dve.tensor_tensor(rden[:, :], rden[:, :], rsq[:, :], ALU.mult))
                    r4 = rden[:, :].rearrange("p (b h) -> p b h", b=4).unsqueeze(3).broadcast_to([P, 4, XH, HD])
                    chain.link(dve.tensor_tensor(hq.rearrange("p (b h e) -> p b h e", b=4, h=XH), u4[:, :, :, 0:HD],
                                                 r4, ALU.mult))
                    chain.link(dve.tensor_tensor(h4, h4, rms1, ALU.mult))
                    chain.link(dve.tensor_tensor(hb, hb, xres[:, four, :], ALU.add))
                    variance4(lambda b: hb[:, b, :])
                if n < B:
                    weigh(n + 3)
                if q >= 0:
                    chain.link(normed4(2 * q, lambda b: hb[:, b, :], lambda b: xres[:, 4 * q + b, :]))
                    variance4(lambda b: xres[:, 4 * q + b, :])
                    last = normed4(2 * q + 1, lambda b: xres[:, 4 * q + b, :], lambda b: xn_all[:, 4 * q + b, :])
                    if n < B:
                        last.then_inc(xn_normed, 1)
                    else:
                        chain.link(last)
                        xn4 = xn_all[:, four, :]
                        chain.link(dve.tensor_tensor(xn4, xn4, gamma_rep.unsqueeze(1).broadcast_to([P, 4, D]),
                                                     ALU.mult))
                        dve.tensor_tensor(xn4, xn4, beta_rep.unsqueeze(1).broadcast_to([P, 4, D]), ALU.add)\
                            .then_inc(xn_ready, 1)

            def over_e(v):
                return v.unsqueeze(2).broadcast_to([P, B, E])

            def over_b(v):
                return v.unsqueeze(1).broadcast_to([P, B, E])

            dve.wait_ge(logits_read, QUADS)
            top, idx, tot, inv = (rsmall[:, k, :] for k in range(4))
            chain.link(dve.tensor_tensor(lg_all[:, :, :], lg_all[:, :, :], over_b(br_rep[:, :]), ALU.add))
            chain.link(dve.tensor_reduce(top, lg_all[:, :, :], AX.X, ALU.max))
            dve.tensor_tensor(rt[0], lg_all[:, :, :], over_e(top), ALU.subtract).then_inc(route_exp_in, 1)
            dve.wait_ge(route_exp_out, 1)
            chain.link(dve.tensor_reduce(tot, rt[1], AX.X, ALU.add))
            chain.link(dve.reciprocal(inv, tot))
            chain.link(dve.tensor_tensor(rt[1], rt[1], over_e(inv), ALU.mult))
            dve.wait_ge(consts_ready, 3)
            for k in range(2):
                sc_k, hot = score[:, k, :], rt[2 + k]
                chain.link(dve.tensor_reduce(sc_k, rt[1], AX.X, ALU.max))
                chain.link(dve.tensor_tensor(rt[4], rt[1], over_e(sc_k), ALU.is_equal))
                chain.link(dve.tensor_tensor(rt[4], rt[4], over_b(em8[:, :]), ALU.mult))
                chain.link(dve.tensor_reduce(idx, rt[4], AX.X, ALU.min))
                chain.link(dve.tensor_tensor(hot, over_b(em8[:, :]), over_e(idx), ALU.is_equal))
                if k == 0:
                    chain.link(dve.scalar_tensor_tensor(rt[1], hot, -2.0, rt[1], ALU.mult, ALU.add))
            dve.tensor_tensor(rt[7], rt[2], rt[3], ALU.add).then_inc(counts_in, 1)
            chain.link(dve.tensor_tensor(wgt[:, :, :], rt[2], over_e(score[:, 0, :]), ALU.mult))
            chain.link(dve.tensor_tensor(rt[4], rt[3], over_e(score[:, 1, :]), ALU.mult))
            chain.link(dve.tensor_tensor(wgt[:, :, :], wgt[:, :, :], rt[4], ALU.add))

            dve.wait_ge(counts_out, 1)
            totals = bank[1][:, 0:ROUT].rearrange("p (b e) -> p b e", e=E)
            chain.link(dve.tensor_copy(rt[0], totals))
            cur, nxt = rt[0], rt[4]
            d = 1
            while d < B:
                chain.link(dve.tensor_copy(nxt[:, 0:d, :], cur[:, 0:d, :]))
                chain.link(dve.tensor_tensor(nxt[:, d:, :], cur[:, d:, :], cur[:, 0:B - d, :], ALU.add))
                cur, nxt = nxt, cur
                d *= 2
            before = rt[5]
            chain.link(dve.tensor_tensor(before, cur, totals, ALU.subtract))
            n1, tiles_e, ends, ends2 = (esmall[:, k, :] for k in range(4))
            chain.link(dve.tensor_scalar(n1, cur[:, B - 1, :], 1.0, None, ALU.add))
            w_cnt = wide[:, 0:E * MAX_E_TILES].rearrange("p (e j) -> p e j", e=E)
            chain.link(dve.tensor_tensor(w_cnt, n1.unsqueeze(2).broadcast_to([P, E, MAX_E_TILES]),
                                         io128[:, :].unsqueeze(1).broadcast_to([P, E, MAX_E_TILES]), ALU.is_gt))
            chain.link(dve.tensor_reduce(tiles_e, w_cnt, AX.X, ALU.add))
            chain.link(dve.tensor_copy(ends, tiles_e))
            cur_e, nxt_e = ends, ends2
            d = 1
            while d < E:
                chain.link(dve.tensor_copy(nxt_e[:, 0:d], cur_e[:, 0:d]))
                chain.link(dve.tensor_tensor(nxt_e[:, d:], cur_e[:, d:], cur_e[:, 0:E - d], ALU.add))
                cur_e, nxt_e = nxt_e, cur_e
                d *= 2
            w_tile = wide.rearrange("p (j e) -> p j e", e=E)
            chain.link(dve.tensor_tensor(w_tile, cur_e.unsqueeze(1).broadcast_to([P, N_TILES, E]),
                                         iotile[:, :].unsqueeze(2).broadcast_to([P, N_TILES, E]), ALU.is_le))
            chain.link(dve.tensor_reduce(tile_f[:, :], w_tile, AX.X, ALU.add))
            chain.link(dve.tensor_scalar(tile_e[:, :], tile_f[:, :], float(E - 1), None, ALU.min))
            chain.link(dve.tensor_copy(tile_end[:, :], cur_e))
            first = n1
            chain.link(dve.tensor_tensor(first, cur_e, tiles_e, ALU.subtract))
            chain.link(dve.tensor_scalar(first, first, float(P), None, ALU.mult))
            chain.link(dve.tensor_tensor(ends[0:E, :] if cur_e is ends2 else ends2[0:E, :], first[0:E, :],
                                         ident[0:E, 0:E], ALU.mult))
            chain.link(dve.tensor_reduce(zslot_f[:, :], (ends if cur_e is ends2 else ends2)[0:E, :], AX.X, ALU.add))
            chain.link(dve.tensor_copy(zslot[:, :], zslot_f[:, :]))
            chain.link(dve.tensor_tensor(before, before, over_b(first), ALU.add))
            chain.link(dve.scalar_tensor_tensor(before, bank[0][:, 0:ROUT].rearrange("p (b e) -> p b e", e=E), 1.0,
                                                before, ALU.add, ALU.add))
            for k in range(2):
                chain.link(dve.tensor_tensor(rt[6], before, rt[2 + k], ALU.mult))
                chain.link(dve.tensor_reduce(slot_f[:, k, :], rt[6], AX.X, ALU.add))
            dve.tensor_copy(slot[:, :, :], slot_f[:, :, :]).then_inc(route_ready, 1)

            def bias(j, par, e, half):
                dve.wait_ge(hid_done, 2 * j + half + 1)
                dve.tensor_tensor(hid[par][:, half * 512:(half + 1) * 512], bank[1 + half][:, :],
                                  b1_rep[:, e, half * 512:(half + 1) * 512], ALU.add).then_inc(hid_biased, 1)

            def rows_out(j, par):
                dve.wait_ge(y_done, j + 1)
                dve.wait_ge(y_stored[par], 8 * (j - par) + 16)
                dve.tensor_reduce(ysb[par], bank[5 + par][:, :].rearrange("p (k n) -> p n k", k=2), AX.X, ALU.add)\
                    .then_inc(y_copied, 1)

            def expert_of(j):
                return dve.value_load(tile_e[0:1, bass.ds(j, 1)], min_val=0, max_val=E - 1)

            dve.wait_ge(route_ready, 1)
            dve.wait_ge(scattered, 16 * 2 * B)
            dve.wait_ge(b1_loaded, 16)
            for par in range(2):
                dve.sem_inc(y_stored[par], 16)

            def rest_xg(j, par):
                dve.wait_ge(xgT_rounded, j + 1)
                dve.tensor_tensor(xgT_lo[:, par, :, :], bank[0][:, 0:KC * P].rearrange("p (c t) -> p c t", c=KC),
                                  xgT_hi[:, par, :, :].bitcast(F32), ALU.subtract).then_inc(xgT_split, 1)

            def rest_hidden(j, par):
                for half in range(2):
                    dve.wait_ge(hidT_rounded, 2 * j + half + 1)
                    hi = hidT_hi[:, par, 4 * half:4 * half + 4, :].rearrange("p c t -> p (c t)")
                    lo = hidT_lo[:, par, 4 * half:4 * half + 4, :].rearrange("p c t -> p (c t)")
                    dve.scalar_tensor_tensor(lo, bank[3 + half][:, :], 0.0, hi.bitcast(F32), ALU.max, ALU.subtract)\
                        .then_inc(hidT_split, 1)

            def tile(j, par, ahead):
                if ahead >= 1:
                    e = expert_of(j + 1)
                    bias(j + 1, 1 - par, e, 0)
                rest_hidden(j, par)
                if ahead >= 1:
                    bias(j + 1, 1 - par, e, 1)
                if ahead >= 2:
                    rest_xg(j + 2, par)
                rows_out(j, par)

            rest_xg(0, 0)
            e0 = expert_of(0)
            for half in range(2):
                bias(0, 0, e0, half)
            rest_xg(1, 1)
            with dve.Fori(0, N_TILES // 2 - 1) as t:
                tile(2 * t, 0, 2)
                tile(2 * t + 1, 1, 2)
            tile(N_TILES - 2, 0, 1)
            tile(N_TILES - 1, 1, 0)

            dve.wait_ge(z_gathered, 16)
            dve.wait_ge(b2_loaded, 16)
            dve.tensor_tensor(dterm, yz, b2_sb, ALU.add).then_inc(c_ready, 1)
            dve.wait_ge(csum_done, 1)
            chain.link(dve.tensor_tensor(b2_sb, b2_sb, dterm, ALU.subtract))
            dve.tensor_tensor(yz, b2_sb, bank[2][0:E, 0:D], ALU.add).then_inc(dterm_ready, 1)
            for q in range(QUADS):
                if q:
                    dve.wait_ge(out_ready, 2 * q)
                for b in range(4 * q, 4 * q + 4):
                    z = zout[:, b % 4, :]
                    dve.wait_ge(gathered[b // 2], 16 * 4)
                    dve.wait_ge(part_done, b + 1)
                    dve.scalar_tensor_tensor(z, y_all[:, 0, b, :], score[:, 0, b:b + 1],
                                             bank[3 + b % 4][:, 0:D], ALU.mult, ALU.add).then_inc(part_read, 1)
                    dve.wait_ge(part_read, b + 1)
                    chain.link(dve.scalar_tensor_tensor(z, y_all[:, 1, b, :], score[:, 1, b:b + 1], z,
                                                        ALU.mult, ALU.add))
                    last = dve.bn_stats(stats4[:, b % 4, :], z)
                chain.link(last)
                for b in range(4):
                    last = dve.bn_aggr(mv4[:, b, :], stats4[:, b, :])
                chain.link(last)
                dve.tensor_scalar(ve4[:, :], mv4[:, :, 1], LN_EPS, None, ALU.add).then_inc(var4_ready, 1)
                dve.wait_ge(rstd4_ready, 2 * QUADS + q + 1)
                dve.scalar_tensor_tensor(shift4[:, :], mv4[:, :, 0], -1.0, rstd4[:, :], ALU.mult, ALU.mult)\
                    .then_inc(shift_ready, 1)
                for b in (0, 2):
                    last = dve.tensor_scalar(xres[:, 4 * q + b, :], zout[:, b, :], mv4[:, b, 0:1], rstd4[:, b:b + 1],
                                             ALU.subtract, ALU.mult)
                last.then_inc(out_ready, 1)


_INS = ['x', 'ctx_1024', 'L0_attn_Wq', 'L0_attn_Wkv', 'L0_attn_Wo', 'L0_attn_bo', 'L0_xattn_igate_kernel',
        'L0_xattn_igate_bias', 'L0_xattn_fgate_kernel', 'L0_xattn_fgate_bias', 'L0_xattn_rms_scale',
        'L0_ffn_gamma', 'L0_ffn_beta', 'L0_ffn_Wr', 'L0_ffn_br', 'L0_ffn_W1', 'L0_ffn_b1', 'L0_ffn_W2', 'L0_ffn_b2']
_OUTS = [((16, 128, 256), 'float32')]


def kernel(**inputs):
    import numpy as _np
    import concourse.bacc as _bacc
    from concourse import mybir as _mybir
    from concourse.bass_utils import run_bass_kernel_spmd as _run

    nc = _bacc.Bacc("TRN2", target_bir_lowering=False, num_devices=1)
    arrays, args = {}, []
    for name in _INS:
        a = _np.ascontiguousarray(inputs[name])
        arrays[f"in_{name}_dram"] = a
        args.append(nc.dram_tensor(f"in_{name}_dram", a.shape, _mybir.dt.from_np(a.dtype), kind="ExternalInput").ap())
    for i, (shape, dtype) in enumerate(_OUTS):
        dt = _mybir.dt.from_np(_np.dtype(dtype))
        args.append(nc.dram_tensor(f"out_{i}_dram", shape, dt, kind="ExternalOutput").ap())
    decoder_layer(nc, *args)
    r = _run(nc, [arrays], core_ids=[0])
    got = tuple(r.results[0][f"out_{i}_dram"] for i in range(len(_OUTS)))
    return got[0]
```
